# Optimizing a Trainium2 kernel written in Bass

```python
import numpy as np
import jax
import jax.numpy as jnp

def _softmax(x, axis=-1):
    return jax.nn.softmax(x, axis=axis)

def _gelu(x):
    return jax.nn.gelu(x, approximate=True)

def _silu(x):
    return jax.nn.silu(x)

def _sigmoid(x):
    return jax.nn.sigmoid(x)

def _layernorm(x, axis=-1, eps=1e-05):
    m = jnp.mean(x, axis=axis, keepdims=True)
    v = jnp.var(x, axis=axis, keepdims=True)
    return (x - m) / jnp.sqrt(v + eps)

def _scatter_add(tgt, idx, src, axis=0):
    return tgt.at[idx].add(src)

def _segment_sum(src, seg, n):
    return jax.ops.segment_sum(src, seg, n)
kernel_name = 'mk_decoder_postln_d2_seqx_r8_04bfac'

def setup_inputs(seed: int=0):
    np.random.seed(seed)
    _w = jnp.asarray

    def _rec_inputs():
        import jax
        import jax.numpy as jnp
        _rk = jax.random.key(seed)
        x = -0.000125 + 0.9999 * jax.random.normal(jax.random.fold_in(_rk, 1), (128, 64, 128), jnp.float32)
        _lenS = 64 - jax.random.randint(jax.random.fold_in(_rk, 7), (128,), 0, max(1, 64 // 4) + 1, jnp.int32)
        _lenS2 = 64 - jax.random.randint(jax.random.fold_in(_rk, 8), (128,), 0, max(1, 64 // 4) + 1, jnp.int32)
        _ctx_1024P = jax.random.normal(jax.random.fold_in(_rk, 11), (128, 16, 128), jnp.float32)
        _ctx_1024c = jax.random.dirichlet(jax.random.fold_in(_rk, 511), 0.3 * jnp.ones((16,), jnp.float32), (128, 64))
        _ctx_1024t = jnp.einsum('bsk,bkd->bsd', _ctx_1024c, _ctx_1024P)
        _ctx_1024t = _ctx_1024t * jax.lax.rsqrt(jnp.mean(jnp.square(_ctx_1024t)) + 1e-12) * 0.953939
        ctx_1024 = -1.52775e-05 + 0.999936 * (_ctx_1024t + 0.3 * jax.random.normal(jax.random.fold_in(_rk, 611), (128, 64, 128), jnp.float32))
        _validS = jnp.arange(64)[None, :] < _lenS[:, None]
        _validS2 = jnp.arange(64)[None, :] < _lenS2[:, None]
        _causal = jnp.tril(jnp.ones((64, 64), dtype=bool))
        mask_BxS2_bk0 = jnp.logical_not(jnp.broadcast_to(_validS2[:, :], (128, 64)))
        return (x, ctx_1024, mask_BxS2_bk0)
    x, ctx_1024, mask_BxS2_bk0 = _rec_inputs()

    def _L0_attn_setup():
        import jax, jax.numpy as jnp
        import numpy as np
        D_MODEL = 128
        N_HEADS = 16
        D_HEAD = D_MODEL // N_HEADS
        BATCH = 2
        SEQ = 256
        key = jax.random.key(seed)
        ks = jax.random.split(key, 5)
        s = 1.0 / np.sqrt(D_MODEL)
        return {'x': jax.random.normal(ks[0], (BATCH, SEQ, D_MODEL), dtype=jnp.float32), 'W_qkv': jax.random.normal(ks[1], (3 * D_MODEL, D_MODEL), dtype=jnp.float32) * s, 'b_qkv': jax.random.normal(ks[2], (3 * D_MODEL,), dtype=jnp.float32) * 0.01, 'W_out': jax.random.normal(ks[3], (D_MODEL, D_MODEL), dtype=jnp.float32) * s, 'b_out': jax.random.normal(ks[4], (D_MODEL,), dtype=jnp.float32) * 0.01}
    _L0_attn_all = _L0_attn_setup()
    _L0_attn_in = {k: v for k, v in _L0_attn_all.items() if k in ('W_qkv', 'b_qkv', 'W_out', 'b_out')}
    del _L0_attn_all

    def _L0_xattn_setup():
        import jax, jax.numpy as jnp
        import numpy as np
        DECAY = 0.9
        key = jax.random.key(seed)
        k1, k2, k3 = jax.random.split(key, 3)
        B, S, D = (8, 512, 128)
        q = jax.random.normal(k1, (B, S, D), dtype=jnp.float32)
        k = jax.random.normal(k2, (B, S, D), dtype=jnp.float32)
        v = jax.random.normal(k3, (B, S, D), dtype=jnp.float32)
        return {'q': q, 'k': k, 'v': v}
    _L0_xattn_all = _L0_xattn_setup()
    _L0_xattn_in = {k: v for k, v in _L0_xattn_all.items() if k in ()}
    del _L0_xattn_all

    def _L0_ffn_setup():
        import jax, jax.numpy as jnp
        import numpy as np
        N_EMBD = 128
        ITER_SIZE = 4 * N_EMBD
        FULL_SIZE = 3 * ITER_SIZE
        R = 0.7

        def _topk_mask(ck, k):
            probs = jax.nn.softmax(ck, axis=-1)
            _, idx = jax.lax.top_k(probs, k)
            b = jnp.arange(probs.shape[0])[:, None]
            return jnp.zeros_like(probs).at[b, idx].set(1.0)

        def _forward(x, Wm, Wp, Wc1, Wc2):
            B = x.shape[0]
            base = jnp.zeros((B, FULL_SIZE), x.dtype).at[:, :ITER_SIZE].set(1.0)

            def step(carry, _):
                xc, active, history, done = carry
                h = jnp.einsum('btc,fc->btf', xc, Wm) * active[:, None, :]
                h = jax.nn.relu(h)
                x_new = jnp.einsum('btf,cf->btc', h, Wp)
                pooled = x_new.mean(axis=1)
                ck = jnp.einsum('bd,fd->bf', jax.nn.relu(jnp.einsum('bc,dc->bd', pooled, Wc1)), Wc2)
                new_mask = _topk_mask(ck, ITER_SIZE)
                combined = jnp.clip(history + new_mask, 0.0, 1.0)
                novelty = (combined - history).sum(axis=1).mean() / ITER_SIZE
                done_next = jnp.logical_or(done, novelty < R)
                x_out = jnp.where(done, xc, x_new)
                active_out = jnp.where(done, active, new_mask)
                history_out = jnp.where(done, history, combined)
                return ((x_out, active_out, history_out, done_next), None)
            init = (x, base, base, jnp.array(False))
            (x_fin, _, _, _), _ = jax.lax.scan(step, init, None, length=3)
            return x_fin
        key = jax.random.key(seed)
        ks = jax.random.split(key, 5)
        B, T = (8, 128)
        s = 0.02
        return {'x': jax.random.normal(ks[0], (B, T, N_EMBD), jnp.float32), 'Wm': jax.random.normal(ks[1], (FULL_SIZE, N_EMBD), jnp.float32) * s, 'Wp': jax.random.normal(ks[2], (N_EMBD, FULL_SIZE), jnp.float32) * s, 'Wc1': jax.random.normal(ks[3], (N_EMBD // 4, N_EMBD), jnp.float32) * s, 'Wc2': jax.random.normal(ks[4], (FULL_SIZE, N_EMBD // 4), jnp.float32) * s}
    _L0_ffn_all = _L0_ffn_setup()
    _L0_ffn_in = {k: v for k, v in _L0_ffn_all.items() if k in ('Wm', 'Wp', 'Wc1', 'Wc2')}
    del _L0_ffn_all

    def _L1_attn_setup():
        import jax, jax.numpy as jnp
        import numpy as np
        N_HIDDEN = 128
        N_HEADS = 16
        HEAD_DIM = N_HIDDEN // N_HEADS
        KERNEL = 4
        GN_EPS = 1e-05

        def _short_conv_1d(x, weight):
            F, K = weight.shape
            xp = jnp.pad(x, ((0, 0), (K - 1, 0), (0, 0)))
            shifts = jnp.stack([xp[:, i:i + x.shape[1], :] for i in range(K)], axis=-1)
            return jnp.sum(shifts * weight[None, None, :, :], axis=-1)
        key = jax.random.key(seed)
        ks = jax.random.split(key, 16)
        B, S = (4, 512)
        H, Hd = (N_HEADS, N_HIDDEN)
        sc = 0.02
        inp = {'x': jax.random.normal(ks[0], (B, S, Hd), dtype=jnp.float32), 'Wq': jax.random.normal(ks[1], (Hd, Hd), dtype=jnp.float32) * sc, 'bq': jnp.zeros((Hd,), jnp.float32), 'Wk': jax.random.normal(ks[2], (Hd, Hd), dtype=jnp.float32) * sc, 'bk': jnp.zeros((Hd,), jnp.float32), 'Wv': jax.random.normal(ks[3], (Hd, Hd), dtype=jnp.float32) * sc, 'bv': jnp.zeros((Hd,), jnp.float32), 'q_conv': jax.random.normal(ks[4], (Hd, KERNEL), dtype=jnp.float32) * sc, 'k_conv': jax.random.normal(ks[5], (Hd, KERNEL), dtype=jnp.float32) * sc, 'v_conv': jax.random.normal(ks[6], (Hd, KERNEL), dtype=jnp.float32) * sc, 'Wa': jax.random.normal(ks[7], (Hd, H), dtype=jnp.float32) * sc, 'ba': jnp.zeros((H,), jnp.float32), 'Wb': jax.random.normal(ks[8], (Hd, H), dtype=jnp.float32) * sc, 'bb': jnp.zeros((H,), jnp.float32), 'Wg': jax.random.normal(ks[9], (Hd, Hd), dtype=jnp.float32) * sc, 'bg': jnp.zeros((Hd,), jnp.float32), 'gn_scale': jnp.ones((Hd,), jnp.float32), 'gn_bias': jnp.zeros((Hd,), jnp.float32), 'Wo': jax.random.normal(ks[10], (Hd, Hd), dtype=jnp.float32) * sc, 'bo': jnp.zeros((Hd,), jnp.float32)}
        return inp
    _L1_attn_all = _L1_attn_setup()
    _L1_attn_in = {k: v for k, v in _L1_attn_all.items() if k in ('Wq', 'bq', 'Wk', 'bk', 'Wv', 'bv', 'q_conv', 'k_conv', 'v_conv', 'Wa', 'ba', 'Wb', 'bb', 'Wg', 'bg', 'gn_scale', 'gn_bias', 'Wo', 'bo')}
    del _L1_attn_all

    def _L1_xattn_setup():
        import jax, jax.numpy as jnp
        import numpy as np
        HEADS = 8
        DIM_HEAD = 64
        SCALE = DIM_HEAD ** (-0.5)
        LN_EPS = 1e-05
        NEG_INF = -1e+30

        def layernorm(x, gamma, beta):
            mu = jnp.mean(x, axis=-1, keepdims=True)
            var = jnp.var(x, axis=-1, keepdims=True)
            return (x - mu) * jax.lax.rsqrt(var + LN_EPS) * gamma + beta
        key = jax.random.key(seed)
        ks = jax.random.split(key, 8)
        b, f, n, d, inner = (8, 1024, 64, 128, HEADS * DIM_HEAD)
        x = jax.random.normal(ks[0], (b, f, d), dtype=jnp.float32)
        latents = jax.random.normal(ks[1], (b, n, d), dtype=jnp.float32)
        key_padding_mask = jax.random.randint(ks[2], (b, f), 0, 2) > 0
        s = 0.02
        return {'x': x, 'latents': latents, 'key_padding_mask': key_padding_mask, 'kv_gate': jnp.float32(-4.0), 'gamma_media': jnp.ones((d,), jnp.float32), 'beta_media': jnp.zeros((d,), jnp.float32), 'gamma_lat': jnp.ones((d,), jnp.float32), 'beta_lat': jnp.zeros((d,), jnp.float32), 'Wq': jax.random.normal(ks[3], (d, inner), jnp.float32) * s, 'Wk': jax.random.normal(ks[4], (d, inner), jnp.float32) * s, 'Wv': jax.random.normal(ks[5], (d, inner), jnp.float32) * s, 'Wout': jax.random.normal(ks[6], (inner, d), jnp.float32) * s}
    _L1_xattn_all = _L1_xattn_setup()
    _L1_xattn_in = {k: v for k, v in _L1_xattn_all.items() if k in ('kv_gate', 'gamma_media', 'beta_media', 'gamma_lat', 'beta_lat', 'Wq', 'Wk', 'Wv', 'Wout')}
    del _L1_xattn_all

    def _L1_ffn_setup():
        import jax, jax.numpy as jnp
        import numpy as np
        LOOPS = 2
        NUM_GROUPS = 4
        EXPERTS_PER_GROUP = 2
        NUM_EXPERTS = NUM_GROUPS * EXPERTS_PER_GROUP
        GROUPS_TOP_K = 2
        TOP_K = 1
        RMS_EPS = 1e-06
        EPS = 1e-09

        def _rmsnorm(x, w):
            return x * jax.lax.rsqrt(jnp.mean(x * x, axis=-1, keepdims=True) + RMS_EPS) * w

        def _combine_weights(x_flat, w_macro, w_micro):
            T = x_flat.shape[0]
            macro = jax.nn.softmax(x_flat @ w_macro.T, axis=-1)
            mvals, midx = jax.lax.top_k(macro, GROUPS_TOP_K)
            mvals = mvals / (jnp.sum(mvals, axis=-1, keepdims=True) + EPS)
            micro = jax.nn.softmax(jnp.einsum('td,ged->tge', x_flat, w_micro), axis=-1)
            uvals, uidx = jax.lax.top_k(micro, TOP_K)
            uvals = uvals / (jnp.sum(uvals, axis=-1, keepdims=True) + EPS)
            tok = jnp.arange(T)
            combine = jnp.zeros((T, NUM_EXPERTS), x_flat.dtype)
            for s in range(GROUPS_TOP_K):
                g = midx[:, s]
                wg = mvals[:, s:s + 1]
                li = uidx[tok, g]
                lv = uvals[tok, g]
                eidx = g[:, None] * EXPERTS_PER_GROUP + li
                combine = combine.at[tok[:, None], eidx].add(lv * wg)
            return combine
        key = jax.random.key(seed)
        ks = jax.random.split(key, 6)
        B, S, D, F = (2, 128, 128, 256)
        return {'z': jax.random.normal(ks[0], (B, S, D), jnp.float32), 'norm_w': jnp.ones((D,), jnp.float32), 'w_macro': jax.random.normal(ks[1], (NUM_GROUPS, D), jnp.float32) * D ** (-0.5), 'w_micro': jax.random.normal(ks[2], (NUM_GROUPS, EXPERTS_PER_GROUP, D), jnp.float32) * D ** (-0.5), 'w1': jax.random.normal(ks[3], (NUM_EXPERTS, F, D), jnp.float32) * D ** (-0.5), 'w2': jax.random.normal(ks[4], (NUM_EXPERTS, D, F), jnp.float32) * F ** (-0.5)}
    _L1_ffn_all = _L1_ffn_setup()
    _L1_ffn_in = {k: v for k, v in _L1_ffn_all.items() if k in ('norm_w', 'w_macro', 'w_micro', 'w1', 'w2')}
    del _L1_ffn_all
    return {'x': x, 'ctx_1024': ctx_1024, 'mask_BxS2_bk0': mask_BxS2_bk0, 'L0_attn_W_qkv': _L0_attn_in['W_qkv'], 'L0_attn_b_qkv': _L0_attn_in['b_qkv'], 'L0_attn_W_out': _L0_attn_in['W_out'], 'L0_attn_b_out': _L0_attn_in['b_out'], 'L0_ffn_Wm': _L0_ffn_in['Wm'], 'L0_ffn_Wp': _L0_ffn_in['Wp'], 'L0_ffn_Wc1': _L0_ffn_in['Wc1'], 'L0_ffn_Wc2': _L0_ffn_in['Wc2'], 'L1_attn_Wq': _L1_attn_in['Wq'], 'L1_attn_bq': _L1_attn_in['bq'], 'L1_attn_Wk': _L1_attn_in['Wk'], 'L1_attn_bk': _L1_attn_in['bk'], 'L1_attn_Wv': _L1_attn_in['Wv'], 'L1_attn_bv': _L1_attn_in['bv'], 'L1_attn_q_conv': _L1_attn_in['q_conv'], 'L1_attn_k_conv': _L1_attn_in['k_conv'], 'L1_attn_v_conv': _L1_attn_in['v_conv'], 'L1_attn_Wa': _L1_attn_in['Wa'], 'L1_attn_ba': _L1_attn_in['ba'], 'L1_attn_Wb': _L1_attn_in['Wb'], 'L1_attn_bb': _L1_attn_in['bb'], 'L1_attn_Wg': _L1_attn_in['Wg'], 'L1_attn_bg': _L1_attn_in['bg'], 'L1_attn_gn_scale': _L1_attn_in['gn_scale'], 'L1_attn_gn_bias': _L1_attn_in['gn_bias'], 'L1_attn_Wo': _L1_attn_in['Wo'], 'L1_attn_bo': _L1_attn_in['bo'], 'L1_xattn_kv_gate': _L1_xattn_in['kv_gate'], 'L1_xattn_gamma_media': _L1_xattn_in['gamma_media'], 'L1_xattn_beta_media': _L1_xattn_in['beta_media'], 'L1_xattn_gamma_lat': _L1_xattn_in['gamma_lat'], 'L1_xattn_beta_lat': _L1_xattn_in['beta_lat'], 'L1_xattn_Wq': _L1_xattn_in['Wq'], 'L1_xattn_Wk': _L1_xattn_in['Wk'], 'L1_xattn_Wv': _L1_xattn_in['Wv'], 'L1_xattn_Wout': _L1_xattn_in['Wout'], 'L1_ffn_norm_w': _L1_ffn_in['norm_w'], 'L1_ffn_w_macro': _L1_ffn_in['w_macro'], 'L1_ffn_w_micro': _L1_ffn_in['w_micro'], 'L1_ffn_w1': _L1_ffn_in['w1'], 'L1_ffn_w2': _L1_ffn_in['w2']}

def reference(x, ctx_1024, mask_BxS2_bk0, L0_attn_W_qkv, L0_attn_b_qkv, L0_attn_W_out, L0_attn_b_out, L0_ffn_Wm, L0_ffn_Wp, L0_ffn_Wc1, L0_ffn_Wc2, L1_attn_Wq, L1_attn_bq, L1_attn_Wk, L1_attn_bk, L1_attn_Wv, L1_attn_bv, L1_attn_q_conv, L1_attn_k_conv, L1_attn_v_conv, L1_attn_Wa, L1_attn_ba, L1_attn_Wb, L1_attn_bb, L1_attn_Wg, L1_attn_bg, L1_attn_gn_scale, L1_attn_gn_bias, L1_attn_Wo, L1_attn_bo, L1_xattn_kv_gate, L1_xattn_gamma_media, L1_xattn_beta_media, L1_xattn_gamma_lat, L1_xattn_beta_lat, L1_xattn_Wq, L1_xattn_Wk, L1_xattn_Wv, L1_xattn_Wout, L1_ffn_norm_w, L1_ffn_w_macro, L1_ffn_w_micro, L1_ffn_w1, L1_ffn_w2):
    import jax
    import jax.numpy as jnp

    def _L0_attn_ref(x, W_qkv, b_qkv, W_out, b_out):
        import jax, jax.numpy as jnp
        import numpy as np
        D_MODEL = 128
        N_HEADS = 16
        D_HEAD = D_MODEL // N_HEADS
        BATCH = 2
        SEQ = 256
        b, s, d = x.shape
        qkv = x @ W_qkv.T + b_qkv
        qkv = qkv.reshape(b, s, N_HEADS, 3 * D_HEAD)
        q = qkv[..., :D_HEAD]
        k = qkv[..., D_HEAD:2 * D_HEAD]
        v = qkv[..., 2 * D_HEAD:]
        scale = np.sqrt(D_HEAD).astype(np.float32)
        scores = jnp.einsum('bqhd,bkhd->bhqk', q, k) / scale
        attn = jax.nn.softmax(scores, axis=-1)
        out = jnp.einsum('bhqk,bkhd->bqhd', attn, v)
        out = out.reshape(b, s, d)
        return out @ W_out.T + b_out

    def _L0_xattn_ref(q, k, v):
        import jax, jax.numpy as jnp
        import numpy as np
        DECAY = 0.9
        kv = jnp.swapaxes(k * v, 0, 1)

        def step(r, kv_t):
            r = DECAY * r + kv_t
            return (r, r)
        r0 = jnp.zeros(q.shape[:1] + q.shape[2:], dtype=q.dtype)
        _, rs = jax.lax.scan(step, r0, kv)
        return q * jnp.swapaxes(rs, 0, 1)

    def _L0_ffn_ref(x, Wm, Wp, Wc1, Wc2):
        import jax, jax.numpy as jnp
        import numpy as np
        N_EMBD = 128
        ITER_SIZE = 4 * N_EMBD
        FULL_SIZE = 3 * ITER_SIZE
        R = 0.7

        def _topk_mask(ck, k):
            probs = jax.nn.softmax(ck, axis=-1)
            _, idx = jax.lax.top_k(probs, k)
            b = jnp.arange(probs.shape[0])[:, None]
            return jnp.zeros_like(probs).at[b, idx].set(1.0)

        def _forward(x, Wm, Wp, Wc1, Wc2):
            B = x.shape[0]
            base = jnp.zeros((B, FULL_SIZE), x.dtype).at[:, :ITER_SIZE].set(1.0)

            def step(carry, _):
                xc, active, history, done = carry
                h = jnp.einsum('btc,fc->btf', xc, Wm) * active[:, None, :]
                h = jax.nn.relu(h)
                x_new = jnp.einsum('btf,cf->btc', h, Wp)
                pooled = x_new.mean(axis=1)
                ck = jnp.einsum('bd,fd->bf', jax.nn.relu(jnp.einsum('bc,dc->bd', pooled, Wc1)), Wc2)
                new_mask = _topk_mask(ck, ITER_SIZE)
                combined = jnp.clip(history + new_mask, 0.0, 1.0)
                novelty = (combined - history).sum(axis=1).mean() / ITER_SIZE
                done_next = jnp.logical_or(done, novelty < R)
                x_out = jnp.where(done, xc, x_new)
                active_out = jnp.where(done, active, new_mask)
                history_out = jnp.where(done, history, combined)
                return ((x_out, active_out, history_out, done_next), None)
            init = (x, base, base, jnp.array(False))
            (x_fin, _, _, _), _ = jax.lax.scan(step, init, None, length=3)
            return x_fin
        return _forward(x, Wm, Wp, Wc1, Wc2)

    def _L1_attn_ref(x, Wq, bq, Wk, bk, Wv, bv, q_conv, k_conv, v_conv, Wa, ba, Wb, bb, Wg, bg, gn_scale, gn_bias, Wo, bo):
        import jax, jax.numpy as jnp
        import numpy as np
        N_HIDDEN = 128
        N_HEADS = 16
        HEAD_DIM = N_HIDDEN // N_HEADS
        KERNEL = 4
        GN_EPS = 1e-05

        def _short_conv_1d(x, weight):
            F, K = weight.shape
            xp = jnp.pad(x, ((0, 0), (K - 1, 0), (0, 0)))
            shifts = jnp.stack([xp[:, i:i + x.shape[1], :] for i in range(K)], axis=-1)
            return jnp.sum(shifts * weight[None, None, :, :], axis=-1)
        B, S, _ = x.shape
        h, d = (N_HEADS, HEAD_DIM)
        q = jax.nn.silu(_short_conv_1d(x @ Wq + bq, q_conv)).reshape(B, S, h, d)
        q = q / (jnp.linalg.norm(q, axis=-1, keepdims=True) + 1e-06)
        k = jax.nn.silu(_short_conv_1d(x @ Wk + bk, k_conv)).reshape(B, S, h, d)
        k = k / (jnp.linalg.norm(k, axis=-1, keepdims=True) + 1e-06)
        v = jax.nn.silu(_short_conv_1d(x @ Wv + bv, v_conv)).reshape(B, S, h, d)
        alpha = jax.nn.sigmoid(x @ Wa + ba)
        beta = jax.nn.sigmoid(x @ Wb + bb)
        out_gate = jax.nn.silu(x @ Wg + bg)
        qT = jnp.transpose(q, (1, 0, 2, 3))
        kT = jnp.transpose(k, (1, 0, 2, 3))
        vT = jnp.transpose(v, (1, 0, 2, 3))
        aT = jnp.transpose(alpha, (1, 0, 2))
        bT = jnp.transpose(beta, (1, 0, 2))

        def _step(Sst, inputs):
            q_t, k_t, v_t, a_t, b_t = inputs
            a = a_t[:, :, None, None]
            b = b_t[:, :, None, None]
            Sk = jnp.einsum('bhde,bhe->bhd', Sst, k_t)
            delta_gated = v_t - a_t[:, :, None] * Sk
            update = b * jnp.einsum('bhd,bhe->bhde', delta_gated, k_t)
            Sst = a * Sst + update
            o_t = jnp.einsum('bhde,bhe->bhd', Sst, q_t)
            return (Sst, o_t)
        S0 = jnp.zeros((B, h, d, d), dtype=x.dtype)
        _, outs = jax.lax.scan(_step, S0, (qT, kT, vT, aT, bT))
        outs = jnp.transpose(outs, (1, 0, 2, 3)).reshape(B, S, N_HIDDEN)
        g = outs.reshape(B, S, h, d)
        mu = jnp.mean(g, axis=(1, 3), keepdims=True)
        var = jnp.mean(jnp.square(g), axis=(1, 3), keepdims=True) - jnp.square(mu)
        g = (g - mu) * jax.lax.rsqrt(var + GN_EPS)
        y = g.reshape(B, S, N_HIDDEN) * gn_scale + gn_bias
        return out_gate * y @ Wo + bo

    def _L1_xattn_ref(x, latents, key_padding_mask, kv_gate, gamma_media, beta_media, gamma_lat, beta_lat, Wq, Wk, Wv, Wout):
        import jax, jax.numpy as jnp
        import numpy as np
        HEADS = 8
        DIM_HEAD = 64
        SCALE = DIM_HEAD ** (-0.5)
        LN_EPS = 1e-05
        NEG_INF = -1e+30

        def layernorm(x, gamma, beta):
            mu = jnp.mean(x, axis=-1, keepdims=True)
            var = jnp.var(x, axis=-1, keepdims=True)
            return (x - mu) * jax.lax.rsqrt(var + LN_EPS) * gamma + beta
        b, f, d = x.shape
        n = latents.shape[1]
        x = layernorm(x, gamma_media, beta_media)
        latents = layernorm(latents, gamma_lat, beta_lat)
        kv = jnp.concatenate((x, latents * kv_gate), axis=1)
        q = (latents @ Wq).reshape(b, n, HEADS, DIM_HEAD)
        k = (kv @ Wk).reshape(b, f + n, HEADS, DIM_HEAD)
        v = (kv @ Wv).reshape(b, f + n, HEADS, DIM_HEAD)
        sim = jnp.einsum('bqhd,bkhd->bhqk', q * SCALE, k)
        sim = sim - jax.lax.stop_gradient(jnp.max(sim, axis=-1, keepdims=True))
        valid_feat = ~key_padding_mask
        valid_full = jnp.concatenate((valid_feat, jnp.ones((b, n), dtype=bool)), axis=1)
        sim = jnp.where(valid_full[:, None, None, :], sim, NEG_INF)
        attn = jax.nn.softmax(sim, axis=-1)
        out = jnp.einsum('bhqk,bkhd->bqhd', attn, v).reshape(b, n, HEADS * DIM_HEAD)
        return out @ Wout

    def _L1_ffn_ref(z, norm_w, w_macro, w_micro, w1, w2):
        import jax, jax.numpy as jnp
        import numpy as np
        LOOPS = 2
        NUM_GROUPS = 4
        EXPERTS_PER_GROUP = 2
        NUM_EXPERTS = NUM_GROUPS * EXPERTS_PER_GROUP
        GROUPS_TOP_K = 2
        TOP_K = 1
        RMS_EPS = 1e-06
        EPS = 1e-09

        def _rmsnorm(x, w):
            return x * jax.lax.rsqrt(jnp.mean(x * x, axis=-1, keepdims=True) + RMS_EPS) * w

        def _combine_weights(x_flat, w_macro, w_micro):
            T = x_flat.shape[0]
            macro = jax.nn.softmax(x_flat @ w_macro.T, axis=-1)
            mvals, midx = jax.lax.top_k(macro, GROUPS_TOP_K)
            mvals = mvals / (jnp.sum(mvals, axis=-1, keepdims=True) + EPS)
            micro = jax.nn.softmax(jnp.einsum('td,ged->tge', x_flat, w_micro), axis=-1)
            uvals, uidx = jax.lax.top_k(micro, TOP_K)
            uvals = uvals / (jnp.sum(uvals, axis=-1, keepdims=True) + EPS)
            tok = jnp.arange(T)
            combine = jnp.zeros((T, NUM_EXPERTS), x_flat.dtype)
            for s in range(GROUPS_TOP_K):
                g = midx[:, s]
                wg = mvals[:, s:s + 1]
                li = uidx[tok, g]
                lv = uvals[tok, g]
                eidx = g[:, None] * EXPERTS_PER_GROUP + li
                combine = combine.at[tok[:, None], eidx].add(lv * wg)
            return combine
        B, S, D = z.shape
        T = B * S
        for _ in range(LOOPS):
            zn = _rmsnorm(z, norm_w)
            x = zn.reshape(T, D)
            combine = _combine_weights(x, w_macro, w_micro)
            h = jax.nn.silu(jnp.einsum('td,efd->tef', x, w1))
            y = jnp.einsum('tef,edf->ted', h, w2)
            mixed = jnp.einsum('ted,te->td', y, combine)
            z = z + mixed.reshape(B, S, D)
        return z
    x = _layernorm(x + _L0_attn_ref(x, L0_attn_W_qkv, L0_attn_b_qkv, L0_attn_W_out, L0_attn_b_out), axis=-1)
    x = _layernorm(x + _L0_xattn_ref(x, ctx_1024, ctx_1024), axis=-1)
    x = _layernorm(x + _L0_ffn_ref(x, L0_ffn_Wm, L0_ffn_Wp, L0_ffn_Wc1, L0_ffn_Wc2), axis=-1)
    x = _layernorm(x + _L1_attn_ref(x, L1_attn_Wq, L1_attn_bq, L1_attn_Wk, L1_attn_bk, L1_attn_Wv, L1_attn_bv, L1_attn_q_conv, L1_attn_k_conv, L1_attn_v_conv, L1_attn_Wa, L1_attn_ba, L1_attn_Wb, L1_attn_bb, L1_attn_Wg, L1_attn_bg, L1_attn_gn_scale, L1_attn_gn_bias, L1_attn_Wo, L1_attn_bo), axis=-1)
    x = _layernorm(x + _L1_xattn_ref(ctx_1024, x, mask_BxS2_bk0, L1_xattn_kv_gate, L1_xattn_gamma_media, L1_xattn_beta_media, L1_xattn_gamma_lat, L1_xattn_beta_lat, L1_xattn_Wq, L1_xattn_Wk, L1_xattn_Wv, L1_xattn_Wout), axis=-1)
    x = _layernorm(x + _L1_ffn_ref(x, L1_ffn_norm_w, L1_ffn_w_macro, L1_ffn_w_micro, L1_ffn_w1, L1_ffn_w2), axis=-1)
    return x

_drawn_inputs = setup_inputs


def setup_inputs(seed=0):
    import zlib

    import numpy as np

    out = dict(_drawn_inputs(seed))
    spreads = {'L1_attn_bq': (0.0, 0.426),
     'L1_attn_bk': (0.0, 0.427),
     'L1_attn_bv': (0.0, 0.437),
     'L1_attn_ba': (0.0, 2.0),
     'L1_attn_bb': (0.0, 0.8),
     'L1_attn_bg': (0.0, 0.45),
     'L1_attn_gn_scale': (1.0, 0.6),
     'L1_attn_gn_bias': (0.0, 0.599),
     'L1_attn_bo': (0.0, 0.1),
     'L1_xattn_gamma_media': (1.0, 0.6),
     'L1_xattn_beta_media': (0.0, 0.354),
     'L1_xattn_gamma_lat': (1.0, 0.2),
     'L1_xattn_beta_lat': (0.0, 0.1),
     'L1_ffn_norm_w': (1.0, 0.2)}
    factors = {'L1_attn_Wa': 8.0, 'L1_attn_Wb': 8.0}
    for name, (base, spread) in spreads.items():
        noise = np.random.default_rng([zlib.crc32(name.encode()), seed]).standard_normal(out[name].shape)
        drawn = base * np.exp(spread * noise) if base else spread * noise
        out[name] = jnp.asarray(drawn.astype(out[name].dtype))
    for name, factor in factors.items():
        out[name] = (out[name] * factor).astype(out[name].dtype)
    return out
```

```python
import numpy as np
import concourse.bass as bass
from concourse import mybir
from contextlib import ExitStack

F32 = mybir.dt.float32
I32 = mybir.dt.int32
ACT = mybir.ActivationFunctionType
ALU = mybir.AluOpType
AX = mybir.AxisListType

P = 128
B, S, D = 128, 64, 128
TOK = B * S
TILES = 4
GTOK = TILES * P
GROUPS = TOK // GTOK
GB = GTOK // S
H, DH = 16, 8
LN_EPS = 1e-5


def stage_semaphores(nc, ctx, prefix):
    taken = []

    def release():
        nc.clear_and_free_semaphores(taken)
        nc.all_engine_barrier()

    ctx.callback(release)

    def sem(name):
        taken.append(nc.alloc_semaphore(prefix + name))
        return taken[-1]

    return sem


def self_attention_and_ffn(nc, d, keep):
    ident = keep["ident"]
    pooledT = keep["pooledT"]
    VW = DH + 1
    F1 = 4 * D
    FC = F1 // P
    SCALE = float(np.float32(1.0) / np.sqrt(np.float32(DH)))
    x_g = d["x"].rearrange("(g t q) s d -> g (q s) t d", t=TILES, q=2)
    c_g = d["ctx"].rearrange("(g t q) s d -> g (q s) t d", t=TILES, q=2)
    with ExitStack() as ctx:
        def sb(name, shape, dt=F32):
            return ctx.enter_context(nc.sbuf_tensor("A_" + name, shape, dt))

        def pb(name, shape, dt=F32):
            return ctx.enter_context(nc.psum_tensor("A_" + name, shape, dt))

        sem = stage_semaphores(nc, ctx, "A_")

        wqT = sb("wqT", [P, D]); wkT = sb("wkT", [P, D]); wvT = sb("wvT", [P, D])
        bq = sb("bq", [P, 1]); bk = sb("bk", [P, 1]); bv = sb("bv", [P, D])
        woT = sb("woT", [P, D]); bo = sb("bo", [P, D])
        headmask = sb("headmask", [P, 8])
        decayT = sb("decayT", [P, P])
        meanw = sb("meanw", [P, 2])
        wmT = sb("wmT", [P, F1]); wpT = sb("wpT", [P, FC, D])
        neghalf = sb("neghalf", [P, TILES])
        xin = sb("xin", [P, TILES, D]); cin = sb("cin", [P, TILES, D])
        xb = sb("xb", [P, TILES, D]); csq = sb("csq", [P, TILES, D])
        xT = sb("xT", [P, GTOK]); qT = sb("qT", [P, GTOK]); kT = sb("kT", [P, GTOK])
        kM = sb("kM", [P, GB, 8, S])
        va = sb("va", [P, GB, H // 2, 2, VW])
        mx = sb("mx", [P, 2, H])
        e = sb("e", [P, 2, H, S])
        pT = sb("pT", [P, 2, 8, P])
        rden = sb("rden", [P, 2, H]); att = sb("att", [P, 2, D]); attT = sb("attT", [P, 2, P])
        r = sb("r", [P, TILES, D]); x1 = sb("x1", [P, TILES, D]); x2 = sb("x2", [P, TILES, D])
        st = sb("st", [P, TILES, 6]); mv = sb("mv", [P, TILES, 2]); ve = sb("ve", [P, TILES]); rs = sb("rs", [P, TILES])
        x2T = sb("x2T", [P, GTOK]); hT = sb("hT", [P, FC, GTOK]); f1 = sb("f1", [P, TILES, D])
        sc = pb("sc", [P, 2, 2, 512])
        tp = pb("tp", [P, 8, P])
        oa = pb("oa", [P, 512])
        yy = pb("yy", [P, TILES, D])
        o_v = oa[:, 0:8 * 2 * 2 * VW].rearrange("p (j b r w) -> p j b r w", j=8, b=2, r=2)
        o_t = oa[:, 320:320 + P]

        s_const = sem("const")
        s_x = sem("x_loaded"); s_c = sem("c_loaded"); s_ones = sem("ones")
        s_xfree = sem("x_free"); s_cfree = sem("c_free")
        s_xTp = sem("xT_psum"); s_xT = sem("xT"); s_xb = sem("xb"); s_csq = sem("csq")
        s_qkp = sem("qk_psum"); s_vp = sem("v_psum"); s_q = sem("q"); s_k = sem("k"); s_km = sem("k_masked"); s_va = sem("va")
        s_sc = sem("scores"); s_mx = sem("rowmax"); s_sub = sem("sub"); s_exp = sem("exp")
        s_tpa = sem("pT_psum"); s_pt = sem("pT"); s_o = sem("o_psum"); s_rd = sem("rden"); s_at = sem("att")
        s_aTp = sem("attT_psum"); s_aT = sem("attT"); s_y = sem("y_psum")
        s_dv = sem("dve_step")
        s_var = sem("var"); s_rstd = sem("rstd"); s_x1 = sem("x1"); s_r = sem("decay_psum"); s_x2 = sem("x2")
        s_x2Tp = sem("x2T_psum"); s_x2T = sem("x2T"); s_h = sem("h_psum"); s_hT = sem("hT")
        s_f = sem("f_psum"); s_f1 = sem("f1"); s_pl = sem("pool_psum"); s_plc = sem("pooled")
        s_sx2 = sem("x2_stored"); s_sf1 = sem("f1_stored"); s_turn = sem("pe_turn"); s_vturn = sem("dve_turn")
        block = ctx.enter_context(nc.Block())

        @block.sync
        def _(sp):
            n = 0
            for dst, src in ((wqT, d["a0_wqT"]), (wkT, d["a0_wkT"]), (wvT, d["a0_wvT"]), (bq, d["a0_bq"]),
                             (bk, d["a0_bk"]), (woT, d["a0_woT"]), (headmask, d["headmask"]),
                             (decayT, d["decayT"]), (meanw, d["meanw"]), (wmT, d["f0_wmT"][:, 0:F1]),
                             (wpT, d["f0_wpT"][0:F1, :].rearrange("(c p) n -> p c n", p=P)),
                             (bv, d["a0_bv"].broadcast_to((P, D))), (bo, d["a0_bo"].broadcast_to((P, D)))):
                full = dst[tuple(slice(None) for _ in dst.shape)]
                sp.dma_start(full, src).then_inc(s_const, 16)
                n += 16
            keep["A_const"] = n
            with sp.Fori(0, GROUPS) as i:
                sp.wait_ge(s_xfree, i + 1)
                sp.dma_start(xin[:, :, :], x_g[i]).then_inc(s_x, 16)
                sp.wait_ge(s_cfree, i + 1)
                sp.dma_start(cin[:, :, :], c_g[i]).then_inc(s_c, 16)
                sp.wait_ge(s_x2, i + 1)
                sp.dma_start(d["s_x2"][i], x2[:, :, :]).then_inc(s_sx2, 16)
                sp.wait_ge(s_f1, i + 1)
                sp.dma_start(d["s_f1"][i], f1[:, :, :]).then_inc(s_sf1, 16)
            sp.wait_ge(s_sx2, GROUPS * 16 + 1)
            sp.wait_ge(s_sf1, GROUPS * 16 + 1)

        NCONST = 13 * 16

        @block.tensor
        def _(pe):
            pe.wait_ge(s_const, NCONST)
            with pe.Fori(0, GROUPS) as i:
                xps = sc[:, 0, 0, :]
                pe.wait_ge(s_x, i * 16 + 16)
                pe.wait_ge(s_sub, i * TILES + 1)
                for t in range(TILES):
                    m = pe.transpose(xps[:, t * P:(t + 1) * P], xin[:, t, :], ident[:, :])
                m.then_inc(s_xTp, 1)
                pe.wait_ge(s_xT, i + 1)
                pe.matmul(sc[:, 0, 1, :], wqT[:, :], xT[:, :], start=True, stop=True)
                pe.matmul(sc[:, 1, 0, :], wkT[:, :], xT[:, :], start=True, stop=True).then_inc(s_qkp, 1)
                pe.wait_ge(s_pt, i * TILES + 1)
                for b in range(GB):
                    for par in range(2):
                        m = pe.matmul(tp[64 * par:64 * par + 64, b, :], xT[:, b * S:(b + 1) * S], wvT[:, :],
                                      start=True, stop=True)
                m.then_inc(s_vp, 1)

                def scores(t):
                    if t < 2:
                        if t == 0:
                            pe.wait_ge(s_q, i + 1)
                            pe.wait_ge(s_k, i + 1)
                            pe.wait_ge(s_km, i + 1)
                    else:
                        pe.wait_ge(s_sub, i * TILES + t)
                    pe.sem_inc(s_turn, 1)
                    for row in range(2):
                        for b in range(2):
                            m = pe.matmul(sc[64 * b:64 * b + 64, t % 2, row, :],
                                          qT[64 * row:64 * row + 64, (2 * t + b) * S:(2 * t + b + 1) * S],
                                          kM[64 * row:64 * row + 64, 2 * t + b, :, :], start=True, stop=True)
                    m.then_inc(s_sc, 1)

                def transposes(t):
                    pe.wait_ge(s_exp, i * TILES + t + 1)
                    if t == 0:
                        pe.wait_ge(s_va, i + 1)
                    else:
                        pe.wait_ge(s_pt, i * TILES + t + 1)
                    for j in range(8):
                        m = pe.transpose(tp[:, j, :], e[:, t % 2, 2 * j:2 * j + 2, :], ident[:, :])
                    m.then_inc(s_tpa, 1)

                def values(t):
                    pe.wait_ge(s_pt, i * TILES + t + 2)
                    pe.wait_ge(s_aT, i * TILES + t + 1)
                    for j in range(8):
                        m = pe.matmul(o_v[:, j, :, :, :], pT[:, t % 2, j, :], va[:, 2 * t:2 * t + 2, j, :, :],
                                      start=True, stop=True)
                    m.then_inc(s_o, 1)
                    pe.wait_ge(s_at, i * TILES + t + 1)
                    pe.transpose(o_t, att[:, t % 2, :], ident[:, :]).then_inc(s_aTp, 1)

                def project(t):
                    pe.wait_ge(s_aT, i * TILES + t + 2)
                    pe.matmul(yy[:, t, :], attT[:, t % 2, :], woT[:, :], start=True, stop=True).then_inc(s_y, 1)

                scores(0)
                scores(1)
                pe.wait_ge(s_plc, i + 1)
                for t in range(TILES):
                    transposes(t)
                    if t + 2 < TILES:
                        scores(t + 2)
                    values(t)
                    if t:
                        project(t - 1)
                project(TILES - 1)
                pe.wait_ge(s_csq, i + 1)
                pe.matmul(sc[:, 0, 0, :], decayT[:, :], csq[:, :, :], start=True, stop=True).then_inc(s_r, 1)
                pe.wait_ge(s_x2, i + 1)
                for t in range(TILES):
                    m = pe.transpose(sc[:, 0, 1, t * P:(t + 1) * P], x2[:, t, :], ident[:, :])
                m.then_inc(s_x2Tp, 1)
                pe.wait_ge(s_x2T, i + 1)
                for c in range(FC):
                    hp = tp.rearrange("p (a b) n -> p a (b n)", a=2)[:, c, :] if c < 2 else sc[:, 1, c - 2, :]
                    pe.matmul(hp, wmT[:, c * P:(c + 1) * P], x2T[:, :], start=True, stop=True).then_inc(s_h, 1)
                pe.wait_ge(s_hT, i * FC + FC)
                for t in range(TILES):
                    for c in range(FC):
                        m = pe.matmul(yy[:, t, :], hT[:, c, t * P:(t + 1) * P], wpT[:, c, :],
                                      start=(c == 0), stop=(c == FC - 1))
                m.then_inc(s_f, 1)
                pe.wait_ge(s_f1, i + 1)
                for t in range(TILES):
                    m = pe.matmul(oa[:, 460 + 2 * t:462 + 2 * t], f1[:, t, :], meanw[:, :], start=True, stop=True)
                m.then_inc(s_pl, 1)

        @block.scalar
        def _(act):
            act.wait_ge(s_const, NCONST)
            act.sem_inc(s_xfree, 1)
            act.sem_inc(s_pt, 1)
            act.sem_inc(s_aT, 1)
            with act.Fori(0, GROUPS) as i:
                act.wait_ge(s_xTp, i + 1)
                act.activation(xT[:, :], sc[:, 0, 0, :], ACT.Copy).then_inc(s_xT, 1)
                act.wait_ge(s_qkp, i + 1)
                act.activation(qT[:, :], sc[:, 0, 1, :], ACT.Identity, bias=bq[:, :]).then_inc(s_q, 1)
                act.activation(kT[:, :], sc[:, 1, 0, :], ACT.Identity, bias=bk[:, :]).then_inc(s_k, 1)
                act.wait_ge(s_xb, i + 1)
                act.sem_inc(s_xfree, 1)
                for t in range(TILES):
                    act.wait_ge(s_sub, i * TILES + t + 2)
                    act.activation(e[:, t % 2, :, :], e[:, t % 2, :, :], ACT.Exp, scale=SCALE).then_inc(s_exp, 1)
                    act.wait_ge(s_tpa, i * TILES + t + 1)
                    if t >= 2:
                        act.wait_ge(s_o, i * TILES + t - 1)
                    act.activation(pT[:, t % 2, :, :], tp[:, :, :], ACT.Copy).then_inc(s_pt, 1)
                    act.wait_ge(s_aTp, i * TILES + t + 1)
                    act.activation(attT[:, t % 2, :], o_t, ACT.Copy).then_inc(s_aT, 1)
                act.wait_ge(s_x2Tp, i + 1)
                act.activation(x2T[:, :], sc[:, 0, 1, :], ACT.Copy).then_inc(s_x2T, 1)
                for c in range(FC):
                    hp = tp.rearrange("p (a b) n -> p a (b n)", a=2)[:, c, :] if c < 2 else sc[:, 1, c - 2, :]
                    act.wait_ge(s_h, i * FC + c + 1)
                    act.activation(hT[:, c, :], hp, ACT.Relu).then_inc(s_hT, 1)

        @block.gpsimd
        def _(pool):
            pool.memset(neghalf[:, :], -0.5).then_inc(s_ones, 1)
            pool.memset(va[:, :, :, :, :], 0.0).then_inc(s_ones, 1)
            pool.wait_ge(s_ones, 2)
            pool.memset(va[0:64, :, :, 0, DH:VW], 1.0).then_inc(s_ones, 1)
            pool.memset(va[64:128, :, :, 1, DH:VW], 1.0).then_inc(s_ones, 1)
            pool.wait_ge(s_const, NCONST)
            pool.sem_inc(s_cfree, 1)
            with pool.Fori(0, GROUPS) as i:
                pool.wait_ge(s_k, i + 1)
                pool.tensor_tensor(kM[:, :, :, :],
                                   kT.rearrange("p (b o s) -> p b o s", b=GB, o=1).broadcast_to((P, GB, 8, S)),
                                   headmask.rearrange("p (b h s) -> p b h s", b=1, s=1).broadcast_to((P, GB, 8, S)),
                                   ALU.mult).then_inc(s_km, 1)
                pool.wait_ge(s_x, i * 16 + 16)
                pool.tensor_tensor(xb[:, :, :], xin[:, :, :],
                                   bo.rearrange("p (o n) -> p o n", o=1).broadcast_to((P, TILES, D)), ALU.add).then_inc(s_xb, 1)
                pool.wait_ge(s_c, i * 16 + 16)
                pool.tensor_tensor(csq[:, :, :], cin[:, :, :], cin[:, :, :], ALU.mult).then_inc(s_csq, 1)
                pool.wait_ge(s_csq, i + 1)
                pool.sem_inc(s_cfree, 1)
                for n in range(2):
                    pool.wait_ge(s_var, i * 2 + n + 1)
                    pool.tensor_tensor(rs[:, :], ve[:, :], neghalf[:, :], ALU.pow).then_inc(s_rstd, 1)

        @block.vector
        def _(v):
            v.wait_ge(s_const, NCONST)
            v.wait_ge(s_ones, 4)
            v.sem_inc(s_sub, 1)
            v.sem_inc(s_plc, 1)
            v.sem_inc(s_sx2, 1)
            v.sem_inc(s_sf1, 1)
            with v.Fori(0, GROUPS) as i:
                step = [0]
                STEPS = 10

                def link(ins):
                    step[0] += 1
                    ins.then_inc(s_dv, 1)
                    v.wait_ge(s_dv, i * STEPS + step[0])

                v.wait_ge(s_vp, i + 1)
                v5 = tp.rearrange("p b (j r d) -> p b j r d", j=8, r=2)
                b4 = bv.rearrange("p (o j r d) -> p o j r d", o=1, j=8, r=2)
                for par in range(2):
                    q = slice(64 * par, 64 * par + 64)
                    m = v.tensor_tensor(va[q, :, :, par, 0:DH], v5[q, :, :, par, :],
                                        b4[q, :, :, par, :].broadcast_to((64, GB, 8, DH)), ALU.add)
                m.then_inc(s_va, 1)

                def softmax(t):
                    v.wait_ge(s_sc, i * TILES + t + 1)
                    s4 = sc[:, t % 2, :, :].rearrange("p r (h k) -> p (r h) k", k=S)
                    v.tensor_reduce(mx[:, t % 2, :], s4, AX.X, ALU.max).then_inc(s_mx, 1)
                    v.wait_ge(s_mx, i * TILES + t + 1)
                    if t >= 2:
                        v.wait_ge(s_tpa, i * TILES + t - 1)
                    v.tensor_tensor(e[:, t % 2, :, :], s4,
                                    mx[:, t % 2, :].rearrange("p (h o) -> p h o", o=1).broadcast_to((P, H, S)),
                                    ALU.subtract).then_inc(s_sub, 1)

                def normalise(t):
                    v.wait_ge(s_o, i * TILES + t + 1)
                    for b in range(2):
                        q = slice(64 * b, 64 * b + 64)
                        m = v.reciprocal(rden[q, t % 2, :].rearrange("p (j r) -> p j r", j=8), o_v[q, :, b, :, DH])
                    m.then_inc(s_rd, 1)
                    v.wait_ge(s_rd, i * TILES + t + 1)
                    for b in range(2):
                        q = slice(64 * b, 64 * b + 64)
                        m = v.tensor_tensor(att[q, t % 2, :].rearrange("p (j r d) -> p j r d", j=8, r=2),
                                            o_v[q, :, b, :, 0:DH],
                                            rden[q, t % 2, :].rearrange("p (j r o) -> p j r o", j=8, r=2)
                                            .broadcast_to((64, 8, 2, DH)), ALU.mult)
                    m.then_inc(s_at, 1)

                def layernorm(dst, n, done):
                    for t in range(TILES):
                        m = v.bn_stats(st[:, t, :], r[:, t, :])
                    link(m)
                    v.sem_inc(s_vturn, 1)
                    for t in range(TILES):
                        m = v.bn_aggr(mv[:, t, :], st[:, t, :])
                    link(m)
                    v.tensor_scalar(ve[:, :], mv[:, :, 1], LN_EPS, None, ALU.add).then_inc(s_var, 1)
                    v.wait_ge(s_rstd, i * 2 + n + 1)
                    for t in range(TILES):
                        m = v.tensor_scalar(dst[:, t, :], r[:, t, :], mv[:, t, 0:1], rs[:, t:t + 1],
                                            ALU.subtract, ALU.mult)
                    m.then_inc(done, 1)

                softmax(0)
                for t in range(TILES):
                    if t + 1 < TILES:
                        softmax(t + 1)
                    normalise(t)
                v.wait_ge(s_y, i * TILES + TILES)
                v.wait_ge(s_xb, i + 1)
                link(v.tensor_tensor(r[:, :, :], yy[:, :, :], xb[:, :, :], ALU.add))
                layernorm(x1, 0, s_x1)
                v.wait_ge(s_x1, i + 1)
                v.wait_ge(s_r, i + 1)
                link(v.scalar_tensor_tensor(r[:, :, :].rearrange("p t d -> p (t d)"), sc[:, 0, 0, :], 1.0,
                                            x1[:, :, :].rearrange("p t d -> p (t d)"), ALU.add, ALU.mult))
                v.wait_ge(s_sx2, i * 16 + 1)
                layernorm(x2, 1, s_x2)
                v.wait_ge(s_f, i + 1)
                v.wait_ge(s_sf1, i * 16 + 1)
                v.tensor_copy(f1[:, :, :], yy[:, :, :]).then_inc(s_f1, 1)
                v.wait_ge(s_pl, i + 1)
                v.tensor_copy(pooledT[:, bass.ds(i * GB, GB)], oa[:, 460:468]).then_inc(s_plc, 1)
                STEPS_USED = step[0]
                assert STEPS_USED <= STEPS
                for _ in range(STEPS - STEPS_USED):
                    v.sem_inc(s_dv, 1)


FULL = 12 * D
KEEP = 4 * D
FCH = FULL // P
BISECT = 48
NOVELTY = float(np.float32(0.7)) * B * KEEP


def route(nc, d, keep, first, run):
    ident, pooledT, go, mask, maskT = (keep[k] for k in ("ident", "pooledT", "go", "mask", "maskT"))
    name = ("R" if not run else "S" if first else "T") + "_"
    choose = first or not run
    with ExitStack() as ctx:
        def sb(n, shape, dt=F32):
            return ctx.enter_context(nc.sbuf_tensor(name + n, shape, dt))

        def pb(n, shape, dt=F32):
            return ctx.enter_context(nc.psum_tensor(name + n, shape, dt))

        sem = stage_semaphores(nc, ctx, name)

        s_const = sem("const")
        if run:
            wmT = sb("wmT", [P, FULL]); wpT = sb("wpT", [P, FCH, D]); meanw = sb("meanw", [P, 2])
            xc = sb("xc", [P, TILES, D]); xT = sb("xT", [P, GTOK])
            hr = sb("hr", [P, FCH, GTOK]); hm = sb("hm", [P, FCH, GTOK]); fo = sb("fo", [P, TILES, D])
            ph = pb("ph", [P, 3, GTOK]); pt = pb("pt", [P, GTOK]); pf = pb("pf", [P, TILES, D])
            s_x = sem("x"); s_xfree = sem("xfree"); s_xTp = sem("xTp"); s_xT = sem("xT")
            s_h = sem("h"); s_hr = sem("hr"); s_hm = sem("hm"); s_f = sem("f"); s_fo = sem("fo"); s_fst = sem("fst")
            s_pl = sem("pl"); s_plc = sem("plc")
        if choose:
            wc1T = sb("wc1T", [P, D // 4]); wc2T = sb("wc2T", [D // 4, FULL])
            hid = sb("hid", [D // 4, B]); ck = sb("ck", [P, FULL]); junk = sb("junk", [P, FULL])
            gt = sb("gt", [P, FULL]); eq = sb("eq", [P, FULL]); cum = sb("cum", [P, FULL]); old = sb("old", [P, FULL])
            one = sb("one", [P, FULL]); ones = sb("ones", [P, 1])
            sm = sb("sm", [P, 16])
            pc = pb("pc", [P, 3, 512]) if not run else None
            s_hid = sem("hid"); s_hidr = sem("hidr"); s_ck = sem("ck"); s_d = sem("d"); s_msk = sem("msk"); s_pm = sem("pm")
            s_mt = sem("mt"); s_tot = sem("tot"); s_go = sem("go"); s_loop = sem("loop")
            if run:
                pc = ph
        pm = pb("pm", [P, 512])
        block = ctx.enter_context(nc.Block())
        loads = []
        if run:
            loads += [(wmT[:, :], d["f0_wmT"]), (wpT[:, :, :], d["f0_wpT"].rearrange("(c p) n -> p c n", p=P)),
                      (meanw[:, :], d["meanw"])]
        if choose:
            loads += [(wc1T[:, :], d["f0_wc1T"]), (wc2T[:, :], d["f0_wc2T"])]
        NCONST = 16 * len(loads)

        def conditional(eng, body):
            if not run:
                body()
                return
            due = eng.value_load(go[0:1, 0:1], min_val=0, max_val=1)
            with eng.If(due > 0):
                body()
                eng.nop()
            with eng.Else():
                eng.nop()

        @block.sync
        def _(sp):
            def body():
                for dst, src in loads:
                    sp.dma_start(dst, src).then_inc(s_const, 16)
                if run:
                    with sp.Fori(0, GROUPS) as i:
                        sp.wait_ge(s_xfree, i + 1)
                        sp.dma_start(xc[:, :, :], d["s_f1"][i]).then_inc(s_x, 16)
                        sp.wait_ge(s_fo, i + 1)
                        sp.dma_start(d["s_f1"][i], fo[:, :, :]).then_inc(s_fst, 16)
                    sp.wait_ge(s_fst, GROUPS * 16)
                else:
                    sp.wait_ge(s_const, NCONST)
            conditional(sp, body)

        @block.tensor
        def _(pe):
            def body():
                pe.wait_ge(s_const, NCONST)
                if run:
                    with pe.Fori(0, GROUPS) as i:
                        pe.wait_ge(s_x, i * 16 + 16)
                        for t in range(TILES):
                            m = pe.transpose(pt[:, t * P:(t + 1) * P], xc[:, t, :], ident[:, :])
                        m.then_inc(s_xTp, 1)
                        pe.wait_ge(s_xT, i + 1)
                        for c in range(FCH):
                            if c >= 3:
                                pe.wait_ge(s_hr, i * FCH + c - 2)
                            pe.matmul(ph[:, c % 3, :], wmT[:, c * P:(c + 1) * P], xT[:, :],
                                      start=True, stop=True).then_inc(s_h, 1)
                        pe.wait_ge(s_hm, i * FCH + FCH + 1)
                        for t in range(TILES):
                            for c in range(FCH):
                                m = pe.matmul(pf[:, t, :], hm[:, c, t * P:(t + 1) * P], wpT[:, c, :],
                                              start=(c == 0), stop=(c == FCH - 1))
                        m.then_inc(s_f, 1)
                        pe.wait_ge(s_fo, i + 1)
                        if choose:
                            pe.wait_ge(s_plc, i + 1)
                            for t in range(TILES):
                                m = pe.matmul(pm[:, 2 * t:2 * t + 2], fo[:, t, :], meanw[:, :], start=True, stop=True)
                            m.then_inc(s_pl, 1)
                if choose:
                    if run:
                        pe.wait_ge(s_plc, GROUPS + 1)
                    pe.matmul(pm[0:D // 4, 128:128 + B], wc1T[:, :], pooledT[:, :], start=True, stop=True).then_inc(s_hid, 1)
                    pe.wait_ge(s_hidr, 1)
                    for c in range(3):
                        m = pe.matmul(pc[:, c, :], hid[:, :], wc2T[:, c * 512:(c + 1) * 512], start=True, stop=True)
                    m.then_inc(s_ck, 1)
                    pe.wait_ge(s_msk, 1)
                    for c in range(3):
                        for j in range(4):
                            m = pe.transpose(pc[:, c, j * P:(j + 1) * P], mask[:, (4 * c + j) * P:(4 * c + j + 1) * P], ident[:, :])
                    m.then_inc(s_pm, 1)
                    pe.matmul(pm[0:1, 0:1], sm[:, 8:9], ones[:, :], start=True, stop=True).then_inc(s_tot, 1)
            conditional(pe, body)

        @block.scalar
        def _(act):
            def body():
                act.wait_ge(s_const, NCONST)
                if run:
                    act.sem_inc(s_xfree, 1)
                    with act.Fori(0, GROUPS) as i:
                        act.wait_ge(s_xTp, i + 1)
                        act.activation(xT[:, :], pt[:, :], ACT.Copy).then_inc(s_xT, 1)
                        act.wait_ge(s_xT, i + 1)
                        act.sem_inc(s_xfree, 1)
                        for c in range(FCH):
                            act.wait_ge(s_h, i * FCH + c + 1)
                            if c == 0:
                                act.wait_ge(s_hm, i * FCH + 1)
                            act.activation(hr[:, c, :], ph[:, c % 3, :], ACT.Relu).then_inc(s_hr, 1)
                if choose:
                    act.wait_ge(s_hid, 1)
                    act.activation(hid[:, :], pm[0:D // 4, 128:128 + B], ACT.Relu).then_inc(s_hidr, 1)
                    act.wait_ge(s_pm, 1)
                    for c in range(3):
                        m = act.activation(maskT[:, 4 * c:4 * c + 4, :], pc[:, c, :], ACT.Copy)
                    m.then_inc(s_mt, 1)
                    act.wait_ge(s_mt, 1)
            conditional(act, body)

        @block.gpsimd
        def _(pool):
            pool.nop()

        @block.vector
        def _(v):
            n = [0]

            def link(ins):
                n[0] += 1
                ins.then_inc(s_d, 1)
                v.wait_ge(s_d, n[0])

            def body():
                v.wait_ge(s_const, NCONST)
                if run:
                    v.sem_inc(s_hm, 1)
                    if choose:
                        v.sem_inc(s_plc, 1)
                    with v.Fori(0, GROUPS) as i:
                        for c in range(FCH):
                            v.wait_ge(s_hr, i * FCH + c + 1)
                            m4 = maskT[:, c, bass.ds(i * GB, GB)].rearrange("p (b o) -> p b o", o=1).broadcast_to((P, GB, S))
                            v.tensor_tensor(hm[:, c, :].rearrange("p (b s) -> p b s", s=S),
                                            hr[:, c, :].rearrange("p (b s) -> p b s", s=S), m4, ALU.mult).then_inc(s_hm, 1)
                        v.wait_ge(s_f, i + 1)
                        v.wait_ge(s_x, i * 16 + 16)
                        v.tensor_copy(fo[:, :, :], pf[:, :, :]).then_inc(s_fo, 1)
                        if choose:
                            v.wait_ge(s_pl, i + 1)
                            v.tensor_copy(pooledT[:, bass.ds(i * GB, GB)], pm[:, 0:8]).then_inc(s_plc, 1)
                if not choose:
                    return
                lo, w, mid, cnt, t0, hi, need, cg = (sm[:, k:k + 1] for k in range(8))
                new = sm[:, 8:9]
                v.wait_ge(s_ck, 1)
                v.memset(one[:, :], 1.0)
                v.memset(ones[:, :], 1.0)
                if run:
                    link(v.tensor_copy(old[:, :], mask[:, :]))
                    link(v.memset(old[:, 0:KEEP], 1.0))
                else:
                    v.memset(old[:, KEEP:FULL], 0.0)
                    link(v.memset(old[:, 0:KEEP], 1.0))
                link(v.tensor_copy(ck[:, :], pc[:, :, :].rearrange("p c n -> p (c n)")))
                v.tensor_reduce(lo, ck[:, :], AX.X, ALU.min)
                link(v.tensor_reduce(hi, ck[:, :], AX.X, ALU.max))
                link(v.tensor_tensor(w, hi, lo, ALU.subtract))
                link(v.tensor_scalar(w, w, 2.0, None, ALU.mult))
                with v.Fori(0, BISECT) as j:
                    k = [0]

                    def chain(ins):
                        k[0] += 1
                        ins.then_inc(s_loop, 1)
                        v.wait_ge(s_loop, j * 5 + k[0])

                    chain(v.tensor_scalar(w, w, 0.5, None, ALU.mult))
                    chain(v.tensor_tensor(mid, lo, w, ALU.add))
                    chain(v.tensor_scalar(junk[:, :], ck[:, :], mid, 0.0, ALU.is_ge, ALU.add, accum_out=cnt))
                    chain(v.scalar_tensor_tensor(t0, cnt, float(KEEP), w, ALU.is_ge, ALU.mult))
                    chain(v.tensor_tensor(lo, lo, t0, ALU.add))
                link(v.tensor_scalar(junk[:, :], ck[:, :], lo, 3.0e38, ALU.is_lt, ALU.mult))
                link(v.tensor_tensor(junk[:, :], junk[:, :], ck[:, :], ALU.add))
                link(v.tensor_reduce(hi, junk[:, :], AX.X, ALU.min))
                v.tensor_scalar(gt[:, :], ck[:, :], hi, 0.0, ALU.is_gt, ALU.add, accum_out=cg)
                link(v.tensor_scalar(eq[:, :], ck[:, :], hi, None, ALU.is_equal))
                link(v.tensor_tensor_scan(cum[:, :], one[:, :], gt[:, :], 0.0, ALU.mult, ALU.add))
                link(v.scalar_tensor_tensor(gt[:, :], cum[:, :], float(KEEP), gt[:, :], ALU.is_le, ALU.mult))
                link(v.tensor_scalar(need, cg, -1.0, float(KEEP), ALU.mult, ALU.add))
                link(v.tensor_tensor_scan(cum[:, :], one[:, :], eq[:, :], 0.0, ALU.mult, ALU.add))
                link(v.scalar_tensor_tensor(eq[:, :], cum[:, :], need, eq[:, :], ALU.is_le, ALU.mult))
                link(v.tensor_tensor(mask[:, :], gt[:, :], eq[:, :], ALU.add))
                link(v.tensor_tensor(junk[:, :], mask[:, :], old[:, :], ALU.mult))
                link(v.tensor_tensor(junk[:, :], mask[:, :], junk[:, :], ALU.subtract))
                v.tensor_reduce(new, junk[:, :], AX.X, ALU.add).then_inc(s_msk, 1)
                v.wait_ge(s_tot, 1)
                v.tensor_scalar(go[0:1, :], pm[0:1, 0:1], keep["novelty"], None, ALU.is_ge).then_inc(s_go, 1)
                v.wait_ge(s_go, 1)
            conditional(v, body)


CONV = 4
PAD = CONV - 1
TW = 4 * D + H


def delta_inputs(nc, d, keep):
    ident = keep["ident"]
    rows_g = d["s_rows"].rearrange("(g t q) s n -> g (q s) t n", t=TILES, q=2)
    with ExitStack() as ctx:
        def sb(name, shape, dt=F32):
            return ctx.enter_context(nc.sbuf_tensor("C_" + name, shape, dt))

        def pb(name, shape, dt=F32):
            return ctx.enter_context(nc.psum_tensor("C_" + name, shape, dt))

        sem = stage_semaphores(nc, ctx, "C_")

        w = sb("w", [P, 3, D]); bias = sb("bias", [P, 3]); cw = sb("cw", [P, 3, CONV])
        wab = sb("wab", [P, 2 * H]); bab = sb("bab", [P, 2 * H]); wg = sb("wg", [P, D]); bg = sb("bg", [P, D])
        neghalf = sb("neghalf", [P, TILES]); half = sb("half", [P, 2 * TILES * H])
        xa = sb("xa", [P, TILES, D]); xf = sb("xf", [P, TILES, D]); r = sb("r", [P, TILES, D]); x3 = sb("x3", [P, TILES, D])
        st = sb("st", [P, TILES, 6]); mv = sb("mv", [P, TILES, 2]); ve = sb("ve", [P, TILES]); rs = sb("rs", [P, TILES])
        xT = sb("xT", [P, GTOK])
        z = sb("z", [P, 3, GB, PAD + S]); cv = sb("cv", [P, 3, GTOK]); cs = sb("cs", [P, 3, GTOK])
        sq = sb("sq", [P, 2, TILES, D]); ss = sb("ss", [P, 2 * TILES * H]); nr = sb("nr", [P, 2 * TILES * H])
        ne = sb("ne", [P, 2 * TILES * H]); rn = sb("rn", [P, 2 * TILES * H])
        abr = sb("abr", [P, TILES, 2 * H]); abt = sb("abt", [P, TILES, 2 * H]); ab = sb("ab", [P, TILES, 2 * H])
        apb = sb("apb", [P, TILES, H])
        gr = sb("gr", [P, TILES, D]); g = sb("g", [P, TILES, D])
        out = sb("out", [P, TILES, TW])
        vs = sb("vs", [P, TILES, D])
        px = pb("px", [P, GTOK]); pq = pb("pq", [P, 3, GTOK]); pg = pb("pg", [P, TILES, D]); pt = pb("pt", [P, 3, TILES, D])
        pab = px[:, 0:TILES * 2 * H].rearrange("p (t n) -> p t n", t=TILES)

        s_const = sem("const"); s_set = sem("set"); s_x = sem("x"); s_xfree = sem("xfree"); s_dv = sem("dv")
        s_var = sem("var"); s_rstd = sem("rstd"); s_x3 = sem("x3"); s_xTp = sem("xTp"); s_xT = sem("xT")
        s_p = sem("proj"); s_z = sem("z"); s_cv = sem("cv"); s_cs = sem("cs"); s_pt = sem("pt"); s_sq = sem("sq")
        s_ss = sem("ss"); s_nr = sem("nr"); s_ne = sem("ne"); s_qk = sem("qk"); s_vs = sem("vs"); s_abp = sem("abp")
        s_abr = sem("abr"); s_abt = sem("abt"); s_ab = sem("ab"); s_apb = sem("apb"); s_gp = sem("gp"); s_gr = sem("gr"); s_g = sem("g")
        s_out = sem("out"); s_sx = sem("sx3"); s_sg = sem("sg"); s_rows = sem("rows"); s_turn = sem("turn")
        block = ctx.enter_context(nc.Block())
        loads = [(w[:, :, :], d["l1_w"]), (bias[:, :], d["l1_b"]), (cw[:, :, :], d["l1_conv"]), (wab[:, :], d["l1_wab"]),
                 (bab[:, :], d["l1_bab"].broadcast_to((P, 2 * H))), (wg[:, :], d["l1_wg"]), (bg[:, :], d["l1_bg"].broadcast_to((P, D)))]
        NCONST = 16 * len(loads)

        @block.sync
        def _(sp):
            for dst, src in loads:
                sp.dma_start(dst, src).then_inc(s_const, 16)
            with sp.Fori(0, GROUPS) as i:
                sp.wait_ge(s_xfree, i + 1)
                sp.dma_start(xa[:, :, :], d["s_x2"][i]).then_inc(s_x, 16)
                sp.dma_start(xf[:, :, :], d["s_f1"][i]).then_inc(s_x, 16)
                sp.wait_ge(s_x3, i + 1)
                sp.dma_start(d["s_x3"][i], x3[:, :, :]).then_inc(s_sx, 16)
                sp.wait_ge(s_g, i + 1)
                sp.dma_start(d["s_gate"][i], g[:, :, :]).then_inc(s_sg, 16)
                sp.wait_ge(s_out, i + 2)
                for t in range(TILES):
                    sp.dma_start(rows_g[i][:, t, :], out[:, t, :]).then_inc(s_rows, 16)
            sp.wait_ge(s_sx, GROUPS * 16 + 1)
            sp.wait_ge(s_sg, GROUPS * 16 + 1)
            sp.wait_ge(s_rows, GROUPS * 16 * TILES + 1)

        @block.tensor
        def _(pe):
            pe.wait_ge(s_const, NCONST)
            with pe.Fori(0, GROUPS) as i:
                pe.wait_ge(s_x3, i + 1)
                pe.wait_ge(s_abr, i + 1)
                for t in range(TILES):
                    m = pe.transpose(px[:, t * P:(t + 1) * P], x3[:, t, :], ident[:, :])
                m.then_inc(s_xTp, 1)
                pe.wait_ge(s_xT, i + 1)
                pe.wait_ge(s_z, i * 3 + 1)
                for c in range(3):
                    pe.matmul(pq[:, c, :], w[:, c, :], xT[:, :], start=True, stop=True).then_inc(s_p, 1)
                for t in range(TILES):
                    m = pe.matmul(pab[:, t, :], xT[:, t * P:(t + 1) * P], wab[:, :], start=True, stop=True)
                m.then_inc(s_abp, 1)
                pe.wait_ge(s_gr, i + 1)
                for t in range(TILES):
                    m = pe.matmul(pg[:, t, :], xT[:, t * P:(t + 1) * P], wg[:, :], start=True, stop=True)
                m.then_inc(s_gp, 1)
                pe.wait_ge(s_qk, i + 1)
                pe.wait_ge(s_vs, i + 1)
                for c in range(3):
                    pe.wait_ge(s_cs, i * 3 + c + 1)
                    for t in range(TILES):
                        m = pe.transpose(pt[:, c, t, :], cs[:, c, t * P:(t + 1) * P], ident[:, :])
                    m.then_inc(s_pt, 1)

        @block.scalar
        def _(act):
            act.wait_ge(s_const, NCONST)
            act.wait_ge(s_set, 3)
            act.sem_inc(s_z, 1)
            act.sem_inc(s_vs, 1)
            act.sem_inc(s_sg, 1)
            with act.Fori(0, GROUPS) as i:
                act.wait_ge(s_xTp, i + 1)
                act.activation(xT[:, :], px[:, :], ACT.Copy).then_inc(s_xT, 1)
                for c in range(3):
                    act.wait_ge(s_p, i * 3 + c + 1)
                    if c == 0:
                        act.wait_ge(s_cv, i * 3 + 1)
                    act.activation(z[:, c, :, PAD:PAD + S], pq[:, c, :].rearrange("p (b s) -> p b s", s=S),
                                   ACT.Identity, bias=bias[:, c:c + 1]).then_inc(s_z, 1)
                act.wait_ge(s_abr, i + 2)
                act.activation(abt[:, :, :], abr[:, :, :], ACT.Tanh, scale=0.5).then_inc(s_abt, 1)
                act.wait_ge(s_gr, i + 2)
                act.wait_ge(s_sg, i * 16 + 1)
                act.activation(g[:, :, :], gr[:, :, :], ACT.Silu).then_inc(s_g, 1)
                for c in range(3):
                    act.wait_ge(s_cv, i * 3 + c + 2)
                    act.activation(cs[:, c, :], cv[:, c, :], ACT.Silu).then_inc(s_cs, 1)
                for c in range(2):
                    act.wait_ge(s_pt, i * 3 + c + 1)
                    act.activation(sq[:, c, :, :], pt[:, c, :, :], ACT.Square).then_inc(s_sq, 1)
                act.wait_ge(s_pt, i * 3 + 3)
                act.wait_ge(s_out, i + 1)
                act.activation(vs[:, :, :], pt[:, 2, :, :], ACT.Copy).then_inc(s_vs, 1)

        @block.gpsimd
        def _(pool):
            pool.memset(neghalf[:, :], -0.5).then_inc(s_set, 1)
            pool.memset(half[:, :], 0.5).then_inc(s_set, 1)
            pool.memset(z[:, :, :, 0:PAD], 0.0).then_inc(s_set, 1)
            pool.wait_ge(s_set, 3)
            pool.sem_inc(s_out, 1)
            with pool.Fori(0, GROUPS) as i:
                pool.wait_ge(s_var, i + 1)
                pool.tensor_tensor(rs[:, :], ve[:, :], neghalf[:, :], ALU.pow).then_inc(s_rstd, 1)
                pool.wait_ge(s_ss, i + 1)
                pool.tensor_tensor(nr[:, :], ss[:, :], half[:, :], ALU.pow).then_inc(s_nr, 1)
                pool.wait_ge(s_qk, i + 2)
                pool.wait_ge(s_ab, i + 1)
                pool.tensor_tensor(out[:, :, 2 * D:3 * D].rearrange("p t (h e) -> p t h e", e=DH),
                                   out[:, :, D:2 * D].rearrange("p t (h e) -> p t h e", e=DH),
                                   apb.rearrange("p t (h o) -> p t h o", o=1).broadcast_to((P, TILES, H, DH)), ALU.mult)
                pool.wait_ge(s_vs, i + 2)
                pool.tensor_tensor(out[:, :, 3 * D:4 * D].rearrange("p t (h e) -> p t h e", e=DH),
                                   vs.rearrange("p t (h e) -> p t h e", e=DH),
                                   ab[:, :, H:2 * H].rearrange("p t (h o) -> p t h o", o=1).broadcast_to((P, TILES, H, DH)),
                                   ALU.mult).then_inc(s_out, 1)

        @block.vector
        def _(v):
            v.wait_ge(s_const, NCONST)
            v.wait_ge(s_set, 3)
            v.sem_inc(s_xfree, 1)
            v.sem_inc(s_cv, 1)
            v.sem_inc(s_abr, 1)
            v.sem_inc(s_gr, 1)
            v.sem_inc(s_qk, 1)
            v.sem_inc(s_sx, 1)
            v.sem_inc(s_rows, 1)
            with v.Fori(0, GROUPS) as i:
                n = [0]
                STEPS = 20

                def link(ins):
                    n[0] += 1
                    ins.then_inc(s_dv, 1)
                    v.wait_ge(s_dv, i * STEPS + n[0])

                v.wait_ge(s_x, i * 32 + 32)
                link(v.tensor_tensor(r[:, :, :], xa[:, :, :], xf[:, :, :], ALU.add))
                v.sem_inc(s_xfree, 1)
                for t in range(TILES):
                    m = v.bn_stats(st[:, t, :], r[:, t, :])
                link(m)
                v.sem_inc(s_turn, 1)
                for t in range(TILES):
                    m = v.bn_aggr(mv[:, t, :], st[:, t, :])
                link(m)
                v.tensor_scalar(ve[:, :], mv[:, :, 1], LN_EPS, None, ALU.add).then_inc(s_var, 1)
                v.wait_ge(s_rstd, i + 1)
                v.wait_ge(s_sx, i * 16 + 1)
                for t in range(TILES):
                    m = v.tensor_scalar(x3[:, t, :], r[:, t, :], mv[:, t, 0:1], rs[:, t:t + 1], ALU.subtract, ALU.mult)
                m.then_inc(s_x3, 1)
                v.wait_ge(s_abp, i + 1)
                v.tensor_tensor(abr[:, :, :], pab, bab.rearrange("p (o n) -> p o n", o=1).broadcast_to((P, TILES, 2 * H)),
                                ALU.add).then_inc(s_abr, 1)
                v.wait_ge(s_gp, i + 1)
                v.tensor_tensor(gr[:, :, :], pg[:, :, :], bg.rearrange("p (o n) -> p o n", o=1).broadcast_to((P, TILES, D)),
                                ALU.add).then_inc(s_gr, 1)
                for c in range(3):
                    v.wait_ge(s_z, i * 3 + c + 2)
                    acc = cv[:, c, :].rearrange("p (b s) -> p b s", s=S)
                    for k in range(CONV):
                        src = z[:, c, :, k:k + S]
                        if k == 0:
                            link(v.tensor_scalar(acc, src, cw[:, c, k:k + 1], None, ALU.mult))
                        elif k < CONV - 1:
                            link(v.scalar_tensor_tensor(acc, src, cw[:, c, k:k + 1], acc, ALU.mult, ALU.add))
                        else:
                            v.scalar_tensor_tensor(acc, src, cw[:, c, k:k + 1], acc, ALU.mult, ALU.add).then_inc(s_cv, 1)
                v.wait_ge(s_abt, i + 1)
                link(v.tensor_scalar(ab[:, :, :], abt[:, :, :], 0.5, 0.5, ALU.mult, ALU.add))
                v.wait_ge(s_out, i + 1)
                v.wait_ge(s_rows, i * 16 * TILES + 1)
                v.tensor_tensor(apb[:, :, :], ab[:, :, 0:H], ab[:, :, H:2 * H], ALU.mult)
                v.tensor_copy(out[:, :, 4 * D:TW], ab[:, :, 0:H]).then_inc(s_ab, 1)
                v.wait_ge(s_sq, i * 2 + 2)
                v.tensor_reduce(ss[:, :], sq.rearrange("p c t (h e) -> p (c t h) e", e=DH), AX.X, ALU.add).then_inc(s_ss, 1)
                v.wait_ge(s_nr, i + 1)
                link(v.tensor_scalar(ne[:, :], nr[:, :], 1e-6, None, ALU.add))
                link(v.reciprocal(rn[:, :], ne[:, :]))
                for c in range(2):
                    m = v.tensor_tensor(out[:, :, c * D:(c + 1) * D].rearrange("p t (h e) -> p t h e", e=DH),
                                        pt[:, c, :, :].rearrange("p t (h e) -> p t h e", e=DH),
                                        rn.rearrange("p (c t h o) -> p c t h o", c=2, t=TILES, o=1)[:, c].broadcast_to((P, TILES, H, DH)),
                                        ALU.mult)
                m.then_inc(s_qk, 1)
                assert n[0] <= STEPS, n
                for _ in range(STEPS - n[0]):
                    v.sem_inc(s_dv, 1)


def delta_scan(nc, d, keep):
    ident = keep["ident"]
    HH = H // 2
    CH = 8
    with ExitStack() as ctx:
        def sb(name, shape, dt=F32):
            return ctx.enter_context(nc.sbuf_tensor("D_" + name, shape, dt))

        def pb(name, shape, dt=F32):
            return ctx.enter_context(nc.psum_tensor("D_" + name, shape, dt))

        sem = stage_semaphores(nc, ctx, "D_")

        rows = sb("rows", [P, S + 1, TW])
        Sx = [sb(f"S{f}", [P, HH, DH, DH]) for f in range(2)]
        aS = [sb(f"aS{f}", [P, HH, DH, DH]) for f in range(2)]
        T1 = [sb(f"T1{f}", [P, HH, DH, DH]) for f in range(2)]
        T2 = [sb(f"T2{f}", [P, HH, DH, DH]) for f in range(2)]
        U = [sb(f"U{f}", [P, HH, DH, DH]) for f in range(2)]
        de = [sb(f"de{f}", [P, HH * DH]) for f in range(2)]
        gs = sb("gs", [P, D]); gb = sb("gb", [P, D]); sums = sb("sums", [P, 2, H]); small = sb("small", [P, 6, H])
        A = sb("A", [P, D]); Bc = sb("Bc", [P, D]); nh = sb("nh", [P, H])
        psk = [pb(f"psk{f}", [P, 512]) for f in range(2)]
        po = [pb(f"po{f}", [P, 512]) for f in range(2)]
        s_const = sem("const"); s_set = sem("set"); s_rows = sem("rows"); s_pad = sem("pad")
        s_t1 = [sem(f"t1{f}") for f in range(2)]; s_sk = [sem(f"sk{f}") for f in range(2)]
        s_as = [sem(f"as{f}") for f in range(2)]; s_de = [sem(f"de{f}") for f in range(2)]
        s_u = [sem(f"u{f}") for f in range(2)]; s_S = [sem(f"S{f}") for f in range(2)]
        s_t2 = [sem(f"t2{f}") for f in range(2)]; s_o = [sem(f"o{f}") for f in range(2)]; s_oc = [sem(f"oc{f}") for f in range(2)]
        s_sqr = sem("sqr"); s_n = sem("n"); s_var = sem("var"); s_rstd = sem("rstd"); s_y = sem("y"); s_sy = sem("sy")
        block = ctx.enter_context(nc.Block())
        NCONST = 32
        YC = 4

        def vec(t, c, f, how):
            x = rows[:, bass.ds(t, 1), c * D + f * HH * DH:c * D + (f + 1) * HH * DH].rearrange("p o (h e) -> p (o h) e", h=HH)
            if how == "k":
                return x.rearrange("p h (o e) -> p h o e", o=1).broadcast_to((P, HH, DH, DH))
            return x.rearrange("p h (e o) -> p h e o", o=1).broadcast_to((P, HH, DH, DH))

        @block.sync
        def _(sp):
            sp.dma_start(gs[:, :], d["l1_gs"].broadcast_to((P, D))).then_inc(s_const, 16)
            sp.dma_start(gb[:, :], d["l1_gb"].broadcast_to((P, D))).then_inc(s_const, 16)
            for c in range(S // CH):
                q = slice(c * CH, (c + 1) * CH)
                sp.dma_start(rows[:, q, :], d["s_rows"][:, q, :]).then_inc(s_rows, 16)
                sp.wait_ge(s_rows, 16 * (c + 1))
            sp.sem_inc(s_rows, 16)
            for c in range(YC):
                sp.wait_ge(s_y, c + 1)
                q = slice(c * S // YC, (c + 1) * S // YC)
                sp.dma_start(d["s_y"][:, q, :], rows[:, q, 2 * D:3 * D]).then_inc(s_sy, 16)
            sp.wait_ge(s_sy, 16 * YC)

        @block.tensor
        def _(pe):
            with pe.Fori(0, S) as t:
                for f in range(2):
                    pe.wait_ge(s_t1[f], t + 1)
                    pe.wait_ge(s_de[f], t + 1)
                    for e in range(DH):
                        m = pe.matmul(psk[f][:, 0:HH * DH], ident[:, :], T1[f].rearrange("p h d e -> p (h d) e")[:, :, e],
                                      start=(e == 0), stop=(e == DH - 1))
                    m.then_inc(s_sk[f], 1)
                for f in range(2):
                    pe.wait_ge(s_t2[f], t + 1)
                    pe.wait_ge(s_oc[f], t + 1)
                    for e in range(DH):
                        m = pe.matmul(po[f][:, 0:HH * DH], ident[:, :], T2[f].rearrange("p h d e -> p (h d) e")[:, :, e],
                                      start=(e == 0), stop=(e == DH - 1))
                    m.then_inc(s_o[f], 1)

        @block.scalar
        def _(act):
            act.sem_inc(s_oc[0], 1)
            act.sem_inc(s_oc[1], 1)
            with act.Fori(0, S) as t:
                for f in range(2):
                    act.wait_ge(s_t1[f], t + 1)
                    for h in range(HH):
                        at = 4 * D + f * HH + h
                        m = act.activation(aS[f][:, h, :, :].rearrange("p d e -> p (d e)"), Sx[f][:, h, :, :].rearrange("p d e -> p (d e)"),
                                           ACT.Copy, scale=rows[:, bass.ds(t, 1), at:at + 1].rearrange("p o n -> p (o n)"))
                    m.then_inc(s_as[f], 1)
                for f in range(2):
                    act.wait_ge(s_o[f], t + 1)
                    act.activation(rows[:, bass.ds(t, 1), f * HH * DH:(f + 1) * HH * DH].rearrange("p o n -> p (o n)"),
                                   po[f][:, 0:HH * DH], ACT.Copy).then_inc(s_oc[f], 1)
            act.wait_ge(s_oc[0], S + 1)
            act.wait_ge(s_oc[1], S + 1)
            act.activation(rows[:, :, D:2 * D], rows[:, :, 0:D], ACT.Square).then_inc(s_sqr, 1)

        @block.gpsimd
        def _(pool):
            pool.memset(nh[:, :], -0.5).then_inc(s_set, 1)
            pool.wait_ge(s_set, 1)
            pool.wait_ge(s_var, 1)
            pool.tensor_tensor(small[:, 3, :], small[:, 2, :], nh[:, :], ALU.pow).then_inc(s_rstd, 1)

        @block.vector
        def _(v):
            v.memset(rows[:, S:S + 1, :], 0.0).then_inc(s_pad, 1)
            v.wait_ge(s_pad, 1)
            v.wait_ge(s_rows, 32)
            for f in range(2):
                v.memset(Sx[f][:, :, :, :], 0.0).then_inc(s_S[f], 1)
                v.memset(T1[f][:, :, :, :], 0.0).then_inc(s_t1[f], 1)
                v.sem_inc(s_de[f], 1)
            with v.Fori(0, S // CH) as c:
                v.wait_ge(s_rows, c * 16 + 32)
                v.sem_inc(s_pad, 1)
                with v.Fori(0, CH) as j:
                    t = c * CH + j
                    for f in range(2):
                        v.wait_ge(s_sk[f], t + 1)
                        vb = rows[:, bass.ds(t, 1), 3 * D + f * HH * DH:3 * D + (f + 1) * HH * DH].rearrange("p o n -> p (o n)")
                        v.tensor_tensor(de[f][:, :], vb, psk[f][:, 0:HH * DH], ALU.subtract).then_inc(s_de[f], 1)
                        v.wait_ge(s_de[f], t + 2)
                        v.tensor_tensor(U[f][:, :, :, :], de[f].rearrange("p (h d o) -> p h d o", h=HH, o=1).broadcast_to((P, HH, DH, DH)),
                                        vec(t, 1, f, "k"), ALU.mult).then_inc(s_u[f], 1)
                        v.wait_ge(s_u[f], t + 1)
                        v.wait_ge(s_as[f], t + 1)
                        v.tensor_tensor(Sx[f][:, :, :, :], aS[f][:, :, :, :], U[f][:, :, :, :], ALU.add).then_inc(s_S[f], 1)
                        v.wait_ge(s_S[f], t + 2)
                        nxt = t + 1
                        v.tensor_tensor(T1[f][:, :, :, :], Sx[f][:, :, :, :], vec(nxt, 2, f, "k"), ALU.mult).then_inc(s_t1[f], 1)
                        v.wait_ge(s_oc[f], t + 1)
                        v.tensor_tensor(T2[f][:, :, :, :], Sx[f][:, :, :, :], vec(t, 0, f, "k"), ALU.mult).then_inc(s_t2[f], 1)
            n = [0]

            def link(ins):
                n[0] += 1
                ins.then_inc(s_n, 1)
                v.wait_ge(s_n, n[0])

            cnt = 1.0 / (S * DH)
            o4 = rows[:, :, 0:D].rearrange("p s (h e) -> p h s e", h=H)
            q4 = rows[:, :, D:2 * D].rearrange("p s (h e) -> p h s e", h=H)
            v.wait_ge(s_oc[0], S + 1)
            v.wait_ge(s_oc[1], S + 1)
            v.tensor_reduce(sums[:, 0, :], o4, AX.XY, ALU.add)
            v.wait_ge(s_sqr, 1)
            link(v.tensor_reduce(sums[:, 1, :], q4, AX.XY, ALU.add))
            mu, m2, ve, rstd, t0 = (small[:, k, :] for k in range(5))
            link(v.tensor_scalar(mu, sums[:, 0, :], cnt, None, ALU.mult))
            link(v.tensor_tensor(t0, mu, mu, ALU.mult))
            link(v.scalar_tensor_tensor(m2, sums[:, 1, :], cnt, t0, ALU.mult, ALU.subtract))
            v.tensor_scalar(ve, m2, 1e-5, None, ALU.add).then_inc(s_var, 1)
            v.wait_ge(s_rstd, 1)
            v.wait_ge(s_const, NCONST)
            hd = lambda x: x.rearrange("p (h e) -> p h e", h=H)
            bc = lambda x: x.rearrange("p (h o) -> p h o", o=1).broadcast_to((P, H, DH))
            link(v.tensor_tensor(hd(A), hd(gs), bc(rstd), ALU.mult))
            link(v.tensor_tensor(hd(Bc), hd(A), bc(mu), ALU.mult))
            link(v.tensor_tensor(Bc[:, :], gb[:, :], Bc[:, :], ALU.subtract))
            for c in range(YC):
                q = slice(c * S // YC, (c + 1) * S // YC)
                n4 = S // YC
                b3 = lambda x: x.rearrange("p (o n) -> p o n", o=1).broadcast_to((P, n4, D))
                link(v.tensor_tensor(rows[:, q, D:2 * D], rows[:, q, 0:D], b3(A), ALU.mult))
                v.tensor_tensor(rows[:, q, 2 * D:3 * D], rows[:, q, D:2 * D], b3(Bc), ALU.add).then_inc(s_y, 1)


XH, XD = 8, 64
XSCALE = XD ** -0.5
KEYS = 2 * S
XP = XH // 2
MASKED = -1e30


def latent_attention(nc, d, keep):
    ident = keep["ident"]
    with ExitStack() as ctx:
        def sb(name, shape, dt=F32):
            return ctx.enter_context(nc.sbuf_tensor("F_" + name, shape, dt))

        def pb(name, shape, dt=F32):
            return ctx.enter_context(nc.psum_tensor("F_" + name, shape, dt))

        sem = stage_semaphores(nc, ctx, "F_")

        wo = sb("wo", [P, D]); bo = sb("bo", [P, D])
        wqT = sb("wqT", [XD, XH, D]); wkT = sb("wkT", [XD, XH, D]); wvT = sb("wvT", [XD, XH, D]); wout = sb("wout", [XD, XH, D])
        qk = sb("qk", [P, XH, D]); vo = sb("vo", [P, XH, D])
        par = sb("par", [P, 5])
        gg = sb("gg", [P, 2])
        neghalf = sb("neghalf", [P, TILES])
        yi = sb("yi", [P, TILES, D]); gi = sb("gi", [P, TILES, D]); xi = sb("xi", [P, TILES, D]); ci = sb("ci", [P, TILES, D])
        mi = sb("mi", [P, GB, S], mybir.dt.uint8); pen = sb("pen", [P, GB, S])
        zz = sb("zz", [P, TILES, D]); zT = sb("zT", [P, GTOK]); xb = sb("xb", [P, TILES, D])
        r = sb("r", [P, TILES, D]); x4 = sb("x4", [P, TILES, D]); ln = sb("ln", [P, TILES, D]); cn = sb("cn", [P, TILES, D])
        x5 = sb("x5", [P, TILES, D])
        st = sb("st", [P, TILES, 6]); mv = sb("mv", [P, TILES, 2]); ve = sb("ve", [P, TILES]); rs = sb("rs", [P, TILES])
        latT = sb("latT", [P, GTOK]); kvT = sb("kvT", [P, GB, 2, S]); kvN = sb("kvN", [P, GB, D])
        qh = sb("qh", [P, XP, GB, 2, S])
        e = sb("e", [P, 2, XP, KEYS]); nm = sb("nm", [P, 2, XP]); den = sb("den", [P, 2, XP]); rd = sb("rd", [P, 2, XP])
        en = sb("en", [P, 2, XP, KEYS]); pT = sb("pT", [P, 2, XP, P]); gh = sb("gh", [P, XH, GB, S])
        pw = pb("pw", [P, 2, 512]); sc = pb("sc", [P, 2, 512]); tp = pb("tp", [P, XP, P]); pg = pb("pg", [P, 2, 512])
        yy = pb("yy", [P, TILES, D])

        s_const = sem("const"); s_set = sem("set"); s_w = sem("w"); s_wc = sem("wc"); s_gg = sem("gg")
        s_in = sem("in"); s_infree = sem("infree"); s_c = sem("c"); s_m = sem("m"); s_pen = sem("pen")
        s_zz = sem("zz"); s_zTp = sem("zTp"); s_zT = sem("zT"); s_y = sem("y"); s_dv = sem("dv"); s_turn = sem("turn")
        s_var = sem("var"); s_rstd = sem("rstd"); s_x4 = sem("x4"); s_ln = sem("ln"); s_cn = sem("cn")
        s_lp = sem("lp"); s_lT = sem("lT"); s_cp = sem("cp"); s_kvT = sem("kvT"); s_kp = sem("kp"); s_kvN = sem("kvN")
        s_qp = sem("qp"); s_qa = sem("qa"); s_qd = sem("qd")
        s_sc = sem("sc"); s_nm = sem("nm"); s_exp = sem("exp"); s_rd = sem("rd"); s_en = sem("en")
        s_tp = sem("tp"); s_pT = sem("pT"); s_g = sem("g"); s_gh = sem("gh"); s_o = sem("o"); s_x5 = sem("x5"); s_st = sem("st")
        s_mxp = sem("mxp")
        block = ctx.enter_context(nc.Block())
        y_g = d["s_y"].rearrange("(g t q) s d -> g (q s) t d", t=TILES, q=2)
        c_g = d["ctx"].rearrange("(g t q) s d -> g (q s) t d", t=TILES, q=2)
        m_g = d["mask"].rearrange("(o g b) s -> g o b s", o=1, b=GB)
        loads = [(wo[:, :], d["l1_wo"]), (bo[:, :], d["l1_bo"].broadcast_to((P, D))), (wqT[:, :, :], d["x_wqT"]),
                 (wkT[:, :, :], d["x_wkT"]), (wvT[:, :, :], d["x_wvT"]), (wout[:, :, :], d["x_wout"]),
                 (par[:, 0:4], d["x_par"]), (par[:, 4:5], d["x_gate"].broadcast_to((P, 1)))]
        NCONST = 16 * len(loads)
        NLN = 4

        @block.sync
        def _(sp):
            for dst, src in loads:
                sp.dma_start(dst, src).then_inc(s_const, 16)
            with sp.Fori(0, GROUPS) as i:
                sp.wait_ge(s_infree, i + 1)
                sp.dma_start(yi[:, :, :], y_g[i]).then_inc(s_in, 16)
                sp.dma_start(gi[:, :, :], d["s_gate"][i]).then_inc(s_in, 16)
                sp.dma_start(xi[:, :, :], d["s_x3"][i]).then_inc(s_in, 16)
                sp.dma_start(ci[:, :, :], c_g[i]).then_inc(s_in, 16)
                sp.dma_start(mi[:, :, :], m_g[i].broadcast_to((P, GB, S))).then_inc(s_in, 16)
                sp.wait_ge(s_x5, i + 1)
                sp.dma_start(d["s_x5"][i], x5[:, :, :]).then_inc(s_st, 16)
            sp.wait_ge(s_st, GROUPS * 16 + 1)

        @block.tensor
        def _(pe):
            pe.wait_ge(s_const, NCONST)
            for c in range(4):
                a, b = ((wqT, wkT), (wvT, wout))[c // 2]
                if c >= 2:
                    pe.wait_ge(s_wc, c - 1)
                for h in range(4):
                    hh = 4 * (c % 2) + h
                    m = pe.matmul(pw[:, c % 2, h * D:(h + 1) * D], a[:, hh, :], b[:, hh, :], start=True, stop=True)
                m.then_inc(s_w, 1)
            pe.wait_ge(s_wc, 4)
            with pe.Fori(0, GROUPS) as i:
                pe.wait_ge(s_zz, i + 1)
                for t in range(TILES):
                    m = pe.transpose(pw[:, 0, t * P:(t + 1) * P], zz[:, t, :], ident[:, :])
                m.then_inc(s_zTp, 1)
                pe.wait_ge(s_cn, i + 1)
                for t in range(TILES):
                    m = pe.transpose(pw[:, 1, t * P:(t + 1) * P], cn[:, t, :], ident[:, :])
                m.then_inc(s_cp, 1)
                pe.wait_ge(s_zT, i + 1)
                for t in range(TILES):
                    m = pe.matmul(yy[:, t, :], zT[:, t * P:(t + 1) * P], wo[:, :], start=True, stop=True)
                m.then_inc(s_y, 1)
                pe.wait_ge(s_ln, i + 1)
                for t in range(TILES):
                    m = pe.transpose(pw[:, 0, t * P:(t + 1) * P], ln[:, t, :], ident[:, :])
                m.then_inc(s_lp, 1)
                pe.wait_ge(s_lT, i + 1)
                pe.wait_ge(s_kvT, i * 2 + 2)
                pe.wait_ge(s_gh, i * GB + 1)
                for b in range(GB):
                    m = pe.transpose(pg[:, b // 4, (b % 4) * P:(b % 4 + 1) * P], kvT[:, b, :, :].rearrange("p a s -> p (a s)"), ident[:, :])
                m.then_inc(s_kp, 1)
                for h in range(XH):
                    if h >= 2:
                        pe.wait_ge(s_qa if h % 2 == 0 else s_qd, i * XP + h // 2)
                    pe.matmul(pw[:, h % 2, :], qk[:, h, :], latT[:, :], start=True, stop=True).then_inc(s_qp, 1)
                pe.wait_ge(s_qa, i * XP + XP)
                pe.wait_ge(s_qd, i * XP + XP)

                def scores(b):
                    if b >= 2:
                        pe.wait_ge(s_exp, i * GB + b - 1)
                    for j in range(XP):
                        m = pe.matmul(sc[:, b % 2, j * KEYS:(j + 1) * KEYS], qh[:, j, b, :, :].rearrange("p a s -> p (a s)"),
                                      kvT[:, b, :, :].rearrange("p a s -> p (a s)"), start=True, stop=True)
                    m.then_inc(s_sc, 1)

                def transposes(b):
                    pe.wait_ge(s_en, i * GB + b + 1)
                    pe.wait_ge(s_pT, i * GB + b + 1)
                    for j in range(XP):
                        m = pe.transpose(tp[:, j, :], en[:, b % 2, j, :], ident[:, :])
                    m.then_inc(s_tp, 1)

                def weighted(b):
                    pe.wait_ge(s_pT, i * GB + b + 2)
                    if b == 0:
                        pe.wait_ge(s_kvN, i + 1)
                    if b >= 2:
                        pe.wait_ge(s_gh, i * GB + b)
                    pe.matmul(pg[:, b % 2, :], kvN[:, b, :], pT[:, b % 2, :, :], start=True, stop=True).then_inc(s_g, 1)

                scores(0)
                scores(1)
                for b in range(GB):
                    transposes(b)
                    if b + 2 < GB:
                        scores(b + 2)
                    weighted(b)
                pe.wait_ge(s_gh, i * GB + GB + 1)
                for t in range(TILES):
                    for h in range(XH):
                        m = pe.matmul(yy[:, t, :], gh[:, h, 2 * t:2 * t + 2, :].rearrange("p a s -> p (a s)"), vo[:, h, :],
                                      start=(h == 0), stop=(h == XH - 1))
                m.then_inc(s_o, 1)

        @block.scalar
        def _(act):
            act.wait_ge(s_const, NCONST)
            act.wait_ge(s_set, 1)
            for c in range(4):
                dst = (qk, vo)[c // 2]
                act.wait_ge(s_w, c + 1)
                act.activation(dst[:, 4 * (c % 2):4 * (c % 2) + 4, :], pw[:, c % 2, :], ACT.Copy,
                               scale=XSCALE if c < 2 else 1.0).then_inc(s_wc, 1)
            act.sem_inc(s_pT, 1)
            act.sem_inc(s_gh, 1)
            with act.Fori(0, GROUPS) as i:
                act.wait_ge(s_zTp, i + 1)
                act.activation(zT[:, :], pw[:, 0, :], ACT.Copy).then_inc(s_zT, 1)
                act.wait_ge(s_cp, i + 1)
                act.activation(kvT[:, :, 0, :], pw[:, 1, :].rearrange("p (b s) -> p b s", s=S), ACT.Identity,
                               bias=par[:, 1:2], scale=par[:, 0:1]).then_inc(s_kvT, 1)
                act.wait_ge(s_lp, i + 1)
                act.activation(latT[:, :], pw[:, 0, :], ACT.Identity, bias=par[:, 3:4], scale=par[:, 2:3])
                act.wait_ge(s_gg, 1)
                act.activation(kvT[:, :, 1, :], pw[:, 0, :].rearrange("p (b s) -> p b s", s=S), ACT.Identity,
                               bias=gg[:, 1:2], scale=gg[:, 0:1]).then_inc(s_kvT, 1)
                act.sem_inc(s_turn, 1)
                act.wait_ge(s_kvT, i * 2 + 2)
                act.sem_inc(s_lT, 1)
                act.wait_ge(s_kp, i + 1)
                act.activation(kvN[:, :, :].rearrange("p b n -> p (b n)"), pg[:, :, :].rearrange("p a n -> p (a n)"), ACT.Copy).then_inc(s_kvN, 1)
                for j in range(XP):
                    act.wait_ge(s_qp, i * XH + 2 * j + 1)
                    act.activation(qh[:, j, :, 0, :], pw[:, 0, :].rearrange("p (b s) -> p b s", s=S), ACT.Copy).then_inc(s_qa, 1)

                def exps(b):
                    act.wait_ge(s_nm, i * GB + b + 1)
                    if b >= 2:
                        act.wait_ge(s_en, i * GB + b - 1)
                    for j in range(XP):
                        m = act.activation(e[:, b % 2, j, :], sc[:, b % 2, j * KEYS:(j + 1) * KEYS], ACT.Exp,
                                           bias=nm[:, b % 2, j:j + 1], accum_out=den[:, b % 2, j:j + 1])
                    m.then_inc(s_exp, 1)

                exps(0)
                for b in range(GB):
                    if b + 1 < GB:
                        exps(b + 1)
                    act.wait_ge(s_tp, i * GB + b + 1)
                    if b >= 2:
                        act.wait_ge(s_g, i * GB + b - 1)
                    act.activation(pT[:, b % 2, :, :], tp[:, :, :], ACT.Copy).then_inc(s_pT, 1)
                    act.wait_ge(s_g, i * GB + b + 1)
                    act.activation(gh[:, :, b, :], pg[:, b % 2, :].rearrange("p (h s) -> p h s", s=S), ACT.Copy).then_inc(s_gh, 1)

        @block.gpsimd
        def _(pool):
            pool.memset(neghalf[:, :], -0.5).then_inc(s_set, 1)
            pool.wait_ge(s_set, 1)
            with pool.Fori(0, GROUPS) as i:
                for n in range(NLN):
                    pool.wait_ge(s_var, i * NLN + n + 1)
                    pool.tensor_tensor(rs[:, :], ve[:, :], neghalf[:, :], ALU.pow).then_inc(s_rstd, 1)

        @block.vector
        def _(v):
            v.wait_ge(s_const, NCONST)
            v.tensor_scalar(gg[:, :], par[:, 2:4], par[:, 4:5], None, ALU.mult).then_inc(s_gg, 1)
            v.sem_inc(s_infree, 1)
            v.sem_inc(s_st, 1)
            with v.Fori(0, GROUPS) as i:
                n = [0]
                STEPS = 16

                def link(ins):
                    n[0] += 1
                    ins.then_inc(s_dv, 1)
                    v.wait_ge(s_dv, i * STEPS + n[0])

                def layernorm(dst, src, k):
                    for t in range(TILES):
                        m = v.bn_stats(st[:, t, :], src[:, t, :])
                    link(m)
                    v.sem_inc(s_turn, 1)
                    for t in range(TILES):
                        m = v.bn_aggr(mv[:, t, :], st[:, t, :])
                    link(m)
                    v.tensor_scalar(ve[:, :], mv[:, :, 1], LN_EPS, None, ALU.add).then_inc(s_var, 1)
                    v.wait_ge(s_rstd, i * NLN + k + 1)
                    for t in range(TILES):
                        m = v.tensor_scalar(dst[:, t, :], src[:, t, :], mv[:, t, 0:1], rs[:, t:t + 1], ALU.subtract, ALU.mult)
                    return m

                v.wait_ge(s_in, i * 80 + 80)
                v.tensor_tensor(zz[:, :, :], yi[:, :, :], gi[:, :, :], ALU.mult).then_inc(s_zz, 1)
                v.tensor_scalar(pen[:, :, :], mi[:, :, :], MASKED, None, ALU.mult).then_inc(s_pen, 1)
                v.tensor_tensor(xb[:, :, :], xi[:, :, :], bo.rearrange("p (o n) -> p o n", o=1).broadcast_to((P, TILES, D)), ALU.add)
                layernorm(cn, ci, 0).then_inc(s_cn, 1)
                v.wait_ge(s_cn, i + 1)
                v.sem_inc(s_infree, 1)
                v.wait_ge(s_y, i + 1)
                link(v.tensor_tensor(r[:, :, :], yy[:, :, :], xb[:, :, :], ALU.add))
                link(layernorm(x4, r, 1))
                layernorm(ln, x4, 2).then_inc(s_ln, 1)
                for j in range(XP):
                    v.wait_ge(s_qp, i * XH + 2 * j + 2)
                    v.tensor_copy(qh[:, j, :, 1, :], pw[:, 1, :].rearrange("p (b s) -> p b s", s=S)).then_inc(s_qd, 1)

                def rowmax(b):
                    v.wait_ge(s_sc, i * GB + b + 1)
                    s3 = sc[:, b % 2, :].rearrange("p (j k) -> p j k", j=XP)
                    v.tensor_tensor(s3[:, :, 0:S], s3[:, :, 0:S],
                                    pen[:, b:b + 1, :].broadcast_to((P, XP, S)), ALU.add).then_inc(s_mxp, 1)
                    v.wait_ge(s_mxp, i * GB + b + 1)
                    if b >= 2:
                        v.wait_ge(s_exp, i * GB + b - 1)
                    v.tensor_reduce(nm[:, b % 2, :], s3, AX.X, ALU.max, negate=True).then_inc(s_nm, 1)

                def normalise(b):
                    v.wait_ge(s_exp, i * GB + b + 1)
                    v.reciprocal(rd[:, b % 2, :], den[:, b % 2, :]).then_inc(s_rd, 1)
                    v.wait_ge(s_rd, i * GB + b + 1)
                    if b >= 2:
                        v.wait_ge(s_tp, i * GB + b - 1)
                    v.tensor_tensor(en[:, b % 2, :, :], e[:, b % 2, :, :],
                                    rd[:, b % 2, :].rearrange("p (j o) -> p j o", o=1).broadcast_to((P, XP, KEYS)),
                                    ALU.mult).then_inc(s_en, 1)

                rowmax(0)
                for b in range(GB):
                    if b + 1 < GB:
                        rowmax(b + 1)
                    normalise(b)
                v.wait_ge(s_o, i + 1)
                link(v.tensor_tensor(r[:, :, :], yy[:, :, :], x4[:, :, :], ALU.add))
                v.wait_ge(s_st, i * 16 + 1)
                layernorm(x5, r, 3).then_inc(s_x5, 1)
                assert n[0] <= STEPS, n
                for _ in range(STEPS - n[0]):
                    v.sem_inc(s_dv, 1)


E8, FF = 8, 256
EC = FF // P
NG4, NL = 4, 2
LOOPS = 2
RMS_EPS, TOP_EPS = 1e-6, 1e-9


def experts(nc, d, keep):
    ident = keep["ident"]
    with ExitStack() as ctx:
        def sb(name, shape, dt=F32):
            return ctx.enter_context(nc.sbuf_tensor("G_" + name, shape, dt))

        def pb(name, shape, dt=F32):
            return ctx.enter_context(nc.psum_tensor("G_" + name, shape, dt))

        sem = stage_semaphores(nc, ctx, "G_")

        w1 = sb("w1", [P, E8 * EC, P]); w2 = sb("w2", [P, E8 * EC, D]); wr = sb("wr", [P, NG4 + E8]); nw = sb("nw", [P, 1])
        neghalf = sb("neghalf", [P, TILES]); euler = sb("euler", [P, TILES * 12]); tri = sb("tri", [P, NG4, NG4])
        xin = sb("xin", [P, TILES, D]); z = sb("z", [P, TILES, D]); zn = sb("zn", [P, TILES, D])
        acc = sb("acc", [P, TILES, D]); junk = sb("junk", [P, TILES, D])
        ss = sb("ss", [P, TILES]); ve = sb("ve", [P, TILES]); rs = sb("rs", [P, TILES])
        st = sb("st", [P, TILES, 6]); mv = sb("mv", [P, TILES, 2]); out = sb("out", [P, TILES, D])
        znT = sb("znT", [P, GTOK]); hT = sb("hT", [P, E8 * EC, GTOK])
        lg = sb("lg", [P, TILES, 12]); ex = sb("ex", [P, TILES, 12]); pr = sb("pr", [P, TILES, 12])
        t4 = sb("t4", [P, 8, TILES, NG4]); t1 = sb("t1", [P, 4, TILES]); cmp = sb("cmp", [P, TILES, NG4, NG4])
        ceq = sb("ceq", [P, TILES, NG4, NG4]); s1 = sb("s1", [P, TILES, NG4, NL]); comb = sb("comb", [P, TILES, E8])
        px = pb("px", [P, 2, 512]); ph = pb("ph", [P, 3, 512]); py = pb("py", [P, 2, TILES, D])

        s_const = sem("const"); s_set = sem("set"); s_x = sem("x"); s_xfree = sem("xfree"); s_z = sem("z"); s_sq = sem("sq")
        s_var = sem("var"); s_rstd = sem("rstd"); s_zn = sem("zn"); s_znp = sem("znp"); s_znT = sem("znT")
        s_lg = sem("lg"); s_sub = sem("sub"); s_ex = sem("ex"); s_h = sem("h"); s_hT = sem("hT"); s_y = sem("y"); s_acc = sem("acc")
        s_dv = sem("dv"); s_turn = sem("turn"); s_out = sem("out"); s_st = sem("st")
        block = ctx.enter_context(nc.Block())
        o_g = d["out"].rearrange("(g t q) s d -> g (q s) t d", t=TILES, q=2)
        loads = [(w1[:, :, :], d["m_w1"]), (w2[:, :, :], d["m_w2"]), (wr[:, :], d["m_wr"]), (nw[:, :], d["m_nw"])]
        NCONST = 16 * len(loads)
        NP = LOOPS + 1

        @block.sync
        def _(sp):
            for dst, src in loads:
                sp.dma_start(dst, src).then_inc(s_const, 16)
            with sp.Fori(0, GROUPS) as i:
                sp.wait_ge(s_xfree, i + 1)
                sp.dma_start(xin[:, :, :], d["s_x5"][i]).then_inc(s_x, 16)
                sp.wait_ge(s_out, i + 1)
                sp.dma_start(o_g[i], out[:, :, :]).then_inc(s_st, 16)
            sp.wait_ge(s_st, GROUPS * 16 + 1)

        @block.tensor
        def _(pe):
            pe.wait_ge(s_const, NCONST)
            with pe.Fori(0, GROUPS) as i:
                for l in range(LOOPS):
                    k = i * LOOPS + l
                    pe.wait_ge(s_zn, k + 1)
                    for t in range(TILES):
                        m = pe.transpose(px[:, 0, t * P:(t + 1) * P], zn[:, t, :], ident[:, :])
                    m.then_inc(s_znp, 1)
                    pe.wait_ge(s_znT, k + 1)
                    for t in range(TILES):
                        m = pe.matmul(px[:, 1, 12 * t:12 * t + 12], znT[:, t * P:(t + 1) * P], wr[:, :], start=True, stop=True)
                    m.then_inc(s_lg, 1)
                    NC = E8 * EC
                    for c in range(NC + 4):
                        if c < NC:
                            if c >= 3:
                                pe.wait_ge(s_hT, k * NC + c - 2)
                            pe.matmul(ph[:, c % 3, :], w1[:, c, :], znT[:, :], start=True, stop=True).then_inc(s_h, 1)
                        if c >= 5 and c % 2 == 1:
                            ee = (c - 5) // 2
                            pe.wait_ge(s_hT, k * NC + 2 * ee + 2)
                            pe.wait_ge(s_acc, k * E8 + ee + 1)
                            for t in range(TILES):
                                for q in range(EC):
                                    m = pe.matmul(py[:, ee % 2, t, :], hT[:, 2 * ee + q, t * P:(t + 1) * P], w2[:, 2 * ee + q, :],
                                                  start=(q == 0), stop=(q == EC - 1))
                            m.then_inc(s_y, 1)

        @block.scalar
        def _(act):
            act.wait_ge(s_const, NCONST)
            with act.Fori(0, GROUPS) as i:
                for l in range(LOOPS):
                    k = i * LOOPS + l
                    act.wait_ge(s_z, k + 1)
                    for t in range(TILES):
                        m = act.activation(junk[:, t, :], z[:, t, :], ACT.Square, accum_out=ss[:, t:t + 1])
                    m.then_inc(s_sq, 1)
                    act.wait_ge(s_znp, k + 1)
                    act.activation(znT[:, :], px[:, 0, :], ACT.Copy, scale=nw[:, :]).then_inc(s_znT, 1)
                    for c in range(E8 * EC):
                        act.wait_ge(s_h, k * E8 * EC + c + 1)
                        if c % 2 == 0 and c // 2 == 0:
                            act.wait_ge(s_acc, k * E8 + 2)
                        act.activation(hT[:, c, :], ph[:, c % 3, :], ACT.Silu).then_inc(s_hT, 1)

        @block.gpsimd
        def _(pool):
            pool.memset(neghalf[:, :], -0.5).then_inc(s_set, 1)
            pool.memset(euler[:, :], float(np.e)).then_inc(s_set, 1)
            pool.memset(tri[:, :, :], 0.0).then_inc(s_set, 1)
            pool.wait_ge(s_set, 3)
            for g in range(1, NG4):
                pool.memset(tri[:, g, 0:g], 1.0).then_inc(s_set, 1)
            with pool.Fori(0, GROUPS) as i:
                for n in range(NP):
                    pool.wait_ge(s_var, i * NP + n + 1)
                    pool.tensor_tensor(rs[:, :], ve[:, :], neghalf[:, :], ALU.pow).then_inc(s_rstd, 1)
                    if n < LOOPS:
                        pool.wait_ge(s_sub, i * LOOPS + n + 1)
                        pool.tensor_tensor(ex.rearrange("p t n -> p (t n)"), euler[:, :], lg.rearrange("p t n -> p (t n)"),
                                           ALU.pow).then_inc(s_ex, 1)

        @block.vector
        def _(v):
            v.wait_ge(s_const, NCONST)
            v.wait_ge(s_set, 3 + NG4 - 1)
            v.sem_inc(s_xfree, 1)
            v.sem_inc(s_acc, 2)
            v.sem_inc(s_st, 1)
            with v.Fori(0, GROUPS) as i:
                n = [0]
                STEPS = 96

                def link(ins):
                    n[0] += 1
                    ins.then_inc(s_dv, 1)
                    v.wait_ge(s_dv, i * STEPS + n[0])

                def b4(x):
                    return x.rearrange("p (t o) -> p t o", o=1).broadcast_to((P, TILES, NG4))

                v.wait_ge(s_x, i * 16 + 16)
                v.tensor_copy(z[:, :, :], xin[:, :, :]).then_inc(s_z, 1)
                v.wait_ge(s_z, i * LOOPS + 1)
                for l in range(LOOPS):
                    k = i * LOOPS + l
                    v.wait_ge(s_sq, k + 1)
                    v.tensor_scalar(ve[:, :], ss[:, :], 1.0 / D, RMS_EPS, ALU.mult, ALU.add).then_inc(s_var, 1)
                    v.wait_ge(s_rstd, i * NP + l + 1)
                    for t in range(TILES):
                        m = v.tensor_scalar(zn[:, t, :], z[:, t, :], rs[:, t:t + 1], None, ALU.mult)
                    m.then_inc(s_zn, 1)
                    v.wait_ge(s_lg, k + 1)
                    raw = px[:, 1, 0:TILES * 12].rearrange("p (t n) -> p t n", t=TILES)
                    v.tensor_reduce(t1[:, 0, :], raw[:, :, 0:NG4], AX.X, ALU.max)
                    link(v.tensor_reduce(t4[:, 0, :, :], raw[:, :, NG4:12].rearrange("p t (g l) -> p t g l", l=NL), AX.X, ALU.max))
                    v.tensor_tensor(lg[:, :, 0:NG4], raw[:, :, 0:NG4], b4(t1[:, 0, :]), ALU.subtract)
                    v.tensor_tensor(lg[:, :, NG4:12].rearrange("p t (g l) -> p t g l", l=NL),
                                    raw[:, :, NG4:12].rearrange("p t (g l) -> p t g l", l=NL),
                                    t4[:, 0, :, :].rearrange("p t (g o) -> p t g o", o=1).broadcast_to((P, TILES, NG4, NL)),
                                    ALU.subtract).then_inc(s_sub, 1)
                    v.wait_ge(s_ex, k + 1)
                    exl = ex[:, :, NG4:12].rearrange("p t (g l) -> p t g l", l=NL)
                    prl = pr[:, :, NG4:12].rearrange("p t (g l) -> p t g l", l=NL)
                    v.tensor_reduce(t1[:, 1, :], ex[:, :, 0:NG4], AX.X, ALU.add)
                    link(v.tensor_reduce(t4[:, 1, :, :], exl, AX.X, ALU.add))
                    v.reciprocal(t1[:, 2, :], t1[:, 1, :])
                    link(v.reciprocal(t4[:, 2, :, :], t4[:, 1, :, :]))
                    v.tensor_tensor(pr[:, :, 0:NG4], ex[:, :, 0:NG4], b4(t1[:, 2, :]), ALU.mult)
                    link(v.tensor_tensor(prl, exl, t4[:, 2, :, :].rearrange("p t (g o) -> p t g o", o=1).broadcast_to((P, TILES, NG4, NL)), ALU.mult))
                    mine = pr[:, :, 0:NG4].rearrange("p t (g o) -> p t g o", o=1).broadcast_to((P, TILES, NG4, NG4))
                    other = pr[:, :, 0:NG4].rearrange("p t (o g) -> p t o g", o=1).broadcast_to((P, TILES, NG4, NG4))
                    v.tensor_tensor(cmp[:, :, :, :], other, mine, ALU.is_gt)
                    v.tensor_tensor(s1[:, :, :, 1], prl[:, :, :, 1], prl[:, :, :, 0], ALU.is_gt)
                    v.tensor_tensor(t4[:, 3, :, :], prl[:, :, :, 0], prl[:, :, :, 1], ALU.max)
                    link(v.tensor_tensor(ceq[:, :, :, :], other, mine, ALU.is_equal))
                    v.tensor_scalar(s1[:, :, :, 0], s1[:, :, :, 1], -1.0, 1.0, ALU.mult, ALU.add)
                    v.tensor_scalar(t4[:, 4, :, :], t4[:, 3, :, :], TOP_EPS, None, ALU.add)
                    link(v.tensor_tensor(ceq[:, :, :, :], ceq[:, :, :, :],
                                         tri.rearrange("p (o a) b -> p o a b", o=1).broadcast_to((P, TILES, NG4, NG4)), ALU.mult))
                    v.reciprocal(t4[:, 5, :, :], t4[:, 4, :, :])
                    link(v.tensor_tensor(cmp[:, :, :, :], cmp[:, :, :, :], ceq[:, :, :, :], ALU.add))
                    v.tensor_tensor(t4[:, 6, :, :], t4[:, 3, :, :], t4[:, 5, :, :], ALU.mult)
                    link(v.tensor_reduce(t4[:, 7, :, :], cmp[:, :, :, :], AX.X, ALU.add))
                    link(v.tensor_scalar(t4[:, 7, :, :], t4[:, 7, :, :], 2.0, None, ALU.is_lt))
                    link(v.tensor_tensor(t4[:, 7, :, :], t4[:, 7, :, :], pr[:, :, 0:NG4], ALU.mult))
                    link(v.tensor_reduce(t1[:, 3, :], t4[:, 7, :, :], AX.X, ALU.add))
                    link(v.tensor_scalar(t1[:, 3, :], t1[:, 3, :], TOP_EPS, None, ALU.add))
                    link(v.reciprocal(t1[:, 0, :], t1[:, 3, :]))
                    link(v.tensor_tensor(t4[:, 0, :, :], t4[:, 7, :, :], b4(t1[:, 0, :]), ALU.mult))
                    link(v.tensor_tensor(t4[:, 0, :, :], t4[:, 0, :, :], t4[:, 6, :, :], ALU.mult))
                    link(v.tensor_tensor(comb.rearrange("p t (g l) -> p t g l", l=NL), s1[:, :, :, :],
                                         t4[:, 0, :, :].rearrange("p t (g o) -> p t g o", o=1).broadcast_to((P, TILES, NG4, NL)), ALU.mult))
                    for ee in range(E8):
                        v.wait_ge(s_y, k * E8 + ee + 1)
                        if ee:
                            v.wait_ge(s_acc, k * E8 + ee + 2)
                        for t in range(TILES):
                            base = z if ee == 0 else acc
                            dst = z if ee == E8 - 1 else acc
                            m = v.scalar_tensor_tensor(dst[:, t, :], py[:, ee % 2, t, :], comb[:, t, ee:ee + 1], base[:, t, :],
                                                       ALU.mult, ALU.add)
                        m.then_inc(s_acc, 1)
                    v.wait_ge(s_acc, k * E8 + E8 + 2)
                    if l + 1 < LOOPS:
                        v.sem_inc(s_z, 1)
                link(v.tensor_tensor(acc[:, :, :], z[:, :, :], xin[:, :, :], ALU.add))
                v.sem_inc(s_xfree, 1)
                for t in range(TILES):
                    m = v.bn_stats(st[:, t, :], acc[:, t, :])
                link(m)
                v.sem_inc(s_turn, 1)
                for t in range(TILES):
                    m = v.bn_aggr(mv[:, t, :], st[:, t, :])
                link(m)
                v.tensor_scalar(ve[:, :], mv[:, :, 1], LN_EPS, None, ALU.add).then_inc(s_var, 1)
                v.wait_ge(s_rstd, i * NP + NP)
                v.wait_ge(s_st, i * 16 + 1)
                for t in range(TILES):
                    m = v.tensor_scalar(out[:, t, :], acc[:, t, :], mv[:, t, 0:1], rs[:, t:t + 1], ALU.subtract, ALU.mult)
                m.then_inc(s_out, 1)
                assert n[0] <= STEPS, n
                for _ in range(STEPS - n[0]):
                    v.sem_inc(s_dv, 1)


SCRATCH = [P, TILES, D]


def decoder(nc, d):
    for name in ("s_x2", "s_f1", "s_x3", "s_gate", "s_x5"):
        d[name] = nc.dram_tensor(name, [GROUPS] + SCRATCH, F32, kind="Internal").ap()
    d["s_rows"] = nc.dram_tensor("s_rows", [B, S, TW], F32, kind="Internal").ap()
    d["s_y"] = nc.dram_tensor("s_y", [B, S, D], F32, kind="Internal").ap()
    with ExitStack() as ctx:
        ident = ctx.enter_context(nc.sbuf_tensor("ident", [P, P], F32))
        keep = {"ident": ident, "novelty": NOVELTY}
        ident_loaded = ctx.enter_context(nc.semaphore("ident_loaded"))
        with nc.Block() as block:
            @block.sync
            def _(sp):
                sp.dma_start(ident[:, :], d["ident"]).then_inc(ident_loaded, 16)
                sp.wait_ge(ident_loaded, 16)
        with ExitStack() as ffn:
            for name, shape, dt in (("pooledT", [P, B], F32), ("go", [1, 1], I32), ("mask", [P, FULL], F32),
                                    ("maskT", [P, FCH, P], F32)):
                keep[name] = ffn.enter_context(nc.sbuf_tensor(name, shape, dt))
            self_attention_and_ffn(nc, d, keep)
            route(nc, d, keep, True, False)
            route(nc, d, keep, True, True)
            route(nc, d, keep, False, True)
        delta_inputs(nc, d, keep)
        delta_scan(nc, d, keep)
        latent_attention(nc, d, keep)
        experts(nc, d, keep)


def layouts(x, ctx_1024, mask_BxS2_bk0, **w):
    p = np.arange(P)
    lag = p[None, :] - p[:, None]
    same = p[None, :] // S == p[:, None] // S
    qkv = w["L0_attn_W_qkv"].reshape(H, 3, DH, D)
    bqkv = w["L0_attn_b_qkv"].reshape(H, 3, DH)
    a = {
        "x": x, "ctx": ctx_1024, "mask": mask_BxS2_bk0,
        "ident": np.eye(P, dtype=np.float32),
        "headmask": ((p[:, None] % 64) // DH == np.arange(8)[None]).astype(np.float32),
        "decayT": np.where((lag >= 0) & same, 0.9 ** np.maximum(lag, 0), 0.0).astype(np.float32),
        "meanw": np.where(p[:, None] // S == np.arange(2)[None], 1.0 / S, 0.0).astype(np.float32),
        "a0_wqT": qkv[:, 0].reshape(D, D).T, "a0_wkT": qkv[:, 1].reshape(D, D).T, "a0_wvT": qkv[:, 2].reshape(D, D).T,
        "a0_bq": bqkv[:, 0].reshape(D, 1), "a0_bk": bqkv[:, 1].reshape(D, 1), "a0_bv": bqkv[:, 2].reshape(1, D),
        "a0_woT": w["L0_attn_W_out"].T, "a0_bo": w["L0_attn_b_out"][None],
        "f0_wmT": w["L0_ffn_Wm"].T, "f0_wpT": w["L0_ffn_Wp"].T, "f0_wc1T": w["L0_ffn_Wc1"].T, "f0_wc2T": w["L0_ffn_Wc2"].T,
        "l1_w": np.stack([w["L1_attn_W" + c] for c in "qkv"], 1), "l1_b": np.stack([w["L1_attn_b" + c] for c in "qkv"], 1),
        "l1_conv": np.stack([w[f"L1_attn_{c}_conv"] for c in "qkv"], 1),
        "l1_wab": np.concatenate([w["L1_attn_Wa"], w["L1_attn_Wb"]], 1),
        "l1_bab": np.concatenate([w["L1_attn_ba"], w["L1_attn_bb"]])[None],
        "l1_wg": w["L1_attn_Wg"], "l1_bg": w["L1_attn_bg"][None],
        "l1_gs": w["L1_attn_gn_scale"][None], "l1_gb": w["L1_attn_gn_bias"][None],
        "l1_wo": w["L1_attn_Wo"], "l1_bo": w["L1_attn_bo"][None],
        "x_wqT": w["L1_xattn_Wq"].reshape(D, XH, XD).transpose(2, 1, 0),
        "x_wkT": w["L1_xattn_Wk"].reshape(D, XH, XD).transpose(2, 1, 0),
        "x_wvT": w["L1_xattn_Wv"].reshape(D, XH, XD).transpose(2, 1, 0),
        "x_wout": w["L1_xattn_Wout"].reshape(XH, XD, D).transpose(1, 0, 2),
        "x_par": np.stack([w["L1_xattn_" + c] for c in ("gamma_media", "beta_media", "gamma_lat", "beta_lat")], 1),
        "x_gate": w["L1_xattn_kv_gate"].reshape(1, 1),
        "m_w1": w["L1_ffn_w1"].reshape(E8, EC, P, D).transpose(3, 0, 1, 2).reshape(D, E8 * EC, P),
        "m_w2": w["L1_ffn_w2"].reshape(E8, D, EC, P).transpose(3, 0, 2, 1).reshape(P, E8 * EC, D),
        "m_wr": np.concatenate([w["L1_ffn_w_macro"], w["L1_ffn_w_micro"].reshape(E8, D)]).T,
        "m_nw": w["L1_ffn_norm_w"][:, None],
    }
    return {k: np.ascontiguousarray(v) for k, v in a.items()}


def kernel(**inputs):
    import concourse.bacc as bacc
    from concourse.bass_utils import run_bass_kernel_spmd

    arrays = layouts(**{k: np.asarray(v) for k, v in inputs.items()})
    nc = bacc.Bacc("TRN2", target_bir_lowering=False, num_devices=1)
    d = {k: nc.dram_tensor("in_" + k, a.shape, mybir.dt.from_np(a.dtype), kind="ExternalInput").ap()
         for k, a in arrays.items()}
    d["out"] = nc.dram_tensor("out", [B, S, D], F32, kind="ExternalOutput").ap()
    decoder(nc, d)
    r = run_bass_kernel_spmd(nc, [{"in_" + k: a for k, a in arrays.items()}], core_ids=[0])
    return r.results[0]["out"]
```

```python
import numpy as np
import concourse.bass as bass
from concourse import mybir
from contextlib import ExitStack

F32 = mybir.dt.float32
I32 = mybir.dt.int32
ACT = mybir.ActivationFunctionType
ALU = mybir.AluOpType
AX = mybir.AxisListType

P = 128
B, S, D = 128, 64, 128
TOK = B * S
TILES = 4
GTOK = TILES * P
GROUPS = TOK // GTOK
GB = GTOK // S
H, DH = 16, 8
LN_EPS = 1e-5


def stage_semaphores(nc, ctx, prefix):
    taken = []

    def release():
        nc.clear_and_free_semaphores(taken)
        nc.all_engine_barrier()

    ctx.callback(release)

    def sem(name):
        taken.append(nc.alloc_semaphore(prefix + name))
        return taken[-1]

    return sem


def self_attention_and_ffn(nc, d, keep):
    ident = keep["ident"]
    pooledT = keep["pooledT"]
    VW = DH + 1
    F1 = 4 * D
    FC = F1 // P
    SCALE = float(np.float32(1.0) / np.sqrt(np.float32(DH)))
    x_g = d["x"].rearrange("(g t q) s d -> g (q s) t d", t=TILES, q=2)
    c_g = d["ctx"].rearrange("(g t q) s d -> g (q s) t d", t=TILES, q=2)
    with ExitStack() as ctx:
        def sb(name, shape, dt=F32):
            return ctx.enter_context(nc.sbuf_tensor("A_" + name, shape, dt))

        def pb(name, shape, dt=F32):
            return ctx.enter_context(nc.psum_tensor("A_" + name, shape, dt))

        sem = stage_semaphores(nc, ctx, "A_")

        wqT = sb("wqT", [P, D]); wkT = sb("wkT", [P, D]); wvT = sb("wvT", [P, D])
        bq = sb("bq", [P, 1]); bk = sb("bk", [P, 1]); bv = sb("bv", [P, D])
        woT = sb("woT", [P, D]); bo = sb("bo", [P, D])
        headmask = sb("headmask", [P, 8])
        decayT = sb("decayT", [P, P])
        meanw = sb("meanw", [P, 2])
        wmT = sb("wmT", [P, F1]); wpT = sb("wpT", [P, FC, D])
        neghalf = sb("neghalf", [P, TILES])
        xin = sb("xin", [P, TILES, D]); cin = sb("cin", [P, TILES, D])
        xb = sb("xb", [P, TILES, D]); csq = sb("csq", [P, TILES, D])
        xT = sb("xT", [P, GTOK]); qT = sb("qT", [P, GTOK]); kT = sb("kT", [P, GTOK])
        kM = sb("kM", [P, GB, 8, S])
        va = sb("va", [P, GB, H // 2, 2, VW])
        mx = sb("mx", [P, 2, H])
        e = sb("e", [P, 2, H, S])
        pT = sb("pT", [P, 2, 8, P])
        rden = sb("rden", [P, 2, H]); att = sb("att", [P, 2, D]); attT = sb("attT", [P, 2, P])
        r = sb("r", [P, TILES, D]); x1 = sb("x1", [P, TILES, D]); x2 = sb("x2", [P, TILES, D])
        st = sb("st", [P, TILES, 6]); mv = sb("mv", [P, TILES, 2]); ve = sb("ve", [P, TILES]); rs = sb("rs", [P, TILES])
        x2T = sb("x2T", [P, GTOK]); hT = sb("hT", [P, FC, GTOK]); f1 = sb("f1", [P, TILES, D])
        sc = pb("sc", [P, 2, 2, 512])
        tp = pb("tp", [P, 8, P])
        oa = pb("oa", [P, 512])
        yy = pb("yy", [P, TILES, D])
        o_v = oa[:, 0:8 * 2 * 2 * VW].rearrange("p (j b r w) -> p j b r w", j=8, b=2, r=2)
        o_t = oa[:, 320:320 + P]

        s_const = sem("const")
        s_x = sem("x_loaded"); s_c = sem("c_loaded"); s_ones = sem("ones")
        s_xfree = sem("x_free"); s_cfree = sem("c_free")
        s_xTp = sem("xT_psum"); s_xT = sem("xT"); s_xb = sem("xb"); s_csq = sem("csq")
        s_qkp = sem("qk_psum"); s_vp = sem("v_psum"); s_q = sem("q"); s_k = sem("k"); s_km = sem("k_masked"); s_va = sem("va")
        s_sc = sem("scores"); s_mx = sem("rowmax"); s_sub = sem("sub"); s_exp = sem("exp")
        s_tpa = sem("pT_psum"); s_pt = sem("pT"); s_o = sem("o_psum"); s_rd = sem("rden"); s_at = sem("att")
        s_aTp = sem("attT_psum"); s_aT = sem("attT"); s_y = sem("y_psum")
        s_dv = sem("dve_step")
        s_var = sem("var"); s_rstd = sem("rstd"); s_x1 = sem("x1"); s_r = sem("decay_psum"); s_x2 = sem("x2")
        s_x2Tp = sem("x2T_psum"); s_x2T = sem("x2T"); s_h = sem("h_psum"); s_hT = sem("hT")
        s_f = sem("f_psum"); s_f1 = sem("f1"); s_pl = sem("pool_psum"); s_plc = sem("pooled")
        s_sx2 = sem("x2_stored"); s_sf1 = sem("f1_stored"); s_turn = sem("pe_turn"); s_vturn = sem("dve_turn")
        block = ctx.enter_context(nc.Block())

        @block.sync
        def _(sp):
            n = 0
            for dst, src in ((wqT, d["a0_wqT"]), (wkT, d["a0_wkT"]), (wvT, d["a0_wvT"]), (bq, d["a0_bq"]),
                             (bk, d["a0_bk"]), (woT, d["a0_woT"]), (headmask, d["headmask"]),
                             (decayT, d["decayT"]), (meanw, d["meanw"]), (wmT, d["f0_wmT"][:, 0:F1]),
                             (wpT, d["f0_wpT"][0:F1, :].rearrange("(c p) n -> p c n", p=P)),
                             (bv, d["a0_bv"].broadcast_to((P, D))), (bo, d["a0_bo"].broadcast_to((P, D)))):
                full = dst[tuple(slice(None) for _ in dst.shape)]
                sp.dma_start(full, src).then_inc(s_const, 16)
                n += 16
            keep["A_const"] = n
            with sp.Fori(0, GROUPS) as i:
                sp.wait_ge(s_xfree, i + 1)
                sp.dma_start(xin[:, :, :], x_g[i]).then_inc(s_x, 16)
                sp.wait_ge(s_cfree, i + 1)
                sp.dma_start(cin[:, :, :], c_g[i]).then_inc(s_c, 16)
                sp.wait_ge(s_x2, i + 1)
                sp.dma_start(d["s_x2"][i], x2[:, :, :]).then_inc(s_sx2, 16)
                sp.wait_ge(s_f1, i + 1)
                sp.dma_start(d["s_f1"][i], f1[:, :, :]).then_inc(s_sf1, 16)
            sp.wait_ge(s_sx2, GROUPS * 16 + 1)
            sp.wait_ge(s_sf1, GROUPS * 16 + 1)

        NCONST = 13 * 16

        @block.tensor
        def _(pe):
            pe.wait_ge(s_const, NCONST)
            with pe.Fori(0, GROUPS) as i:
                xps = sc[:, 0, 0, :]
                pe.wait_ge(s_x, i * 16 + 16)
                pe.wait_ge(s_sub, i * TILES + 1)
                for t in range(TILES):
                    m = pe.transpose(xps[:, t * P:(t + 1) * P], xin[:, t, :], ident[:, :])
                m.then_inc(s_xTp, 1)
                pe.wait_ge(s_xT, i + 1)
                pe.matmul(sc[:, 0, 1, :], wqT[:, :], xT[:, :], start=True, stop=True)
                pe.matmul(sc[:, 1, 0, :], wkT[:, :], xT[:, :], start=True, stop=True).then_inc(s_qkp, 1)
                pe.wait_ge(s_pt, i * TILES + 1)
                for b in range(GB):
                    for par in range(2):
                        m = pe.matmul(tp[64 * par:64 * par + 64, b, :], xT[:, b * S:(b + 1) * S], wvT[:, :],
                                      start=True, stop=True)
                m.then_inc(s_vp, 1)

                def scores(t):
                    if t < 2:
                        if t == 0:
                            pe.wait_ge(s_q, i + 1)
                            pe.wait_ge(s_k, i + 1)
                            pe.wait_ge(s_km, i + 1)
                    else:
                        pe.wait_ge(s_sub, i * TILES + t)
                    pe.sem_inc(s_turn, 1)
                    for row in range(2):
                        for b in range(2):
                            m = pe.matmul(sc[64 * b:64 * b + 64, t % 2, row, :],
                                          qT[64 * row:64 * row + 64, (2 * t + b) * S:(2 * t + b + 1) * S],
                                          kM[64 * row:64 * row + 64, 2 * t + b, :, :], start=True, stop=True)
                    m.then_inc(s_sc, 1)

                def transposes(t):
                    pe.wait_ge(s_exp, i * TILES + t + 1)
                    if t == 0:
                        pe.wait_ge(s_va, i + 1)
                    else:
                        pe.wait_ge(s_pt, i * TILES + t + 1)
                    for j in range(8):
                        m = pe.transpose(tp[:, j, :], e[:, t % 2, 2 * j:2 * j + 2, :], ident[:, :])
                    m.then_inc(s_tpa, 1)

                def values(t):
                    pe.wait_ge(s_pt, i * TILES + t + 2)
                    pe.wait_ge(s_aT, i * TILES + t + 1)
                    for j in range(8):
                        m = pe.matmul(o_v[:, j, :, :, :], pT[:, t % 2, j, :], va[:, 2 * t:2 * t + 2, j, :, :],
                                      start=True, stop=True)
                    m.then_inc(s_o, 1)
                    pe.wait_ge(s_at, i * TILES + t + 1)
                    pe.transpose(o_t, att[:, t % 2, :], ident[:, :]).then_inc(s_aTp, 1)

                def project(t):
                    pe.wait_ge(s_aT, i * TILES + t + 2)
                    pe.matmul(yy[:, t, :], attT[:, t % 2, :], woT[:, :], start=True, stop=True).then_inc(s_y, 1)

                scores(0)
                scores(1)
                pe.wait_ge(s_plc, i + 1)
                for t in range(TILES):
                    transposes(t)
                    if t + 2 < TILES:
                        scores(t + 2)
                    values(t)
                    if t:
                        project(t - 1)
                project(TILES - 1)
                pe.wait_ge(s_csq, i + 1)
                pe.matmul(sc[:, 0, 0, :], decayT[:, :], csq[:, :, :], start=True, stop=True).then_inc(s_r, 1)
                pe.wait_ge(s_x2, i + 1)
                for t in range(TILES):
                    m = pe.transpose(sc[:, 0, 1, t * P:(t + 1) * P], x2[:, t, :], ident[:, :])
                m.then_inc(s_x2Tp, 1)
                pe.wait_ge(s_x2T, i + 1)
                for c in range(FC):
                    hp = tp.rearrange("p (a b) n -> p a (b n)", a=2)[:, c, :] if c < 2 else sc[:, 1, c - 2, :]
                    pe.matmul(hp, wmT[:, c * P:(c + 1) * P], x2T[:, :], start=True, stop=True).then_inc(s_h, 1)
                pe.wait_ge(s_hT, i * FC + FC)
                for t in range(TILES):
                    for c in range(FC):
                        m = pe.matmul(yy[:, t, :], hT[:, c, t * P:(t + 1) * P], wpT[:, c, :],
                                      start=(c == 0), stop=(c == FC - 1))
                m.then_inc(s_f, 1)
                pe.wait_ge(s_f1, i + 1)
                for t in range(TILES):
                    m = pe.matmul(oa[:, 460 + 2 * t:462 + 2 * t], f1[:, t, :], meanw[:, :], start=True, stop=True)
                m.then_inc(s_pl, 1)

        @block.scalar
        def _(act):
            act.wait_ge(s_const, NCONST)
            act.sem_inc(s_xfree, 1)
            act.sem_inc(s_pt, 1)
            act.sem_inc(s_aT, 1)
            with act.Fori(0, GROUPS) as i:
                act.wait_ge(s_xTp, i + 1)
                act.activation(xT[:, :], sc[:, 0, 0, :], ACT.Copy).then_inc(s_xT, 1)
                act.wait_ge(s_qkp, i + 1)
                act.activation(qT[:, :], sc[:, 0, 1, :], ACT.Identity, bias=bq[:, :]).then_inc(s_q, 1)
                act.activation(kT[:, :], sc[:, 1, 0, :], ACT.Identity, bias=bk[:, :]).then_inc(s_k, 1)
                act.wait_ge(s_xb, i + 1)
                act.sem_inc(s_xfree, 1)
                for t in range(TILES):
                    act.wait_ge(s_sub, i * TILES + t + 2)
                    act.activation(e[:, t % 2, :, :], e[:, t % 2, :, :], ACT.Exp, scale=SCALE).then_inc(s_exp, 1)
                    act.wait_ge(s_tpa, i * TILES + t + 1)
                    if t >= 2:
                        act.wait_ge(s_o, i * TILES + t - 1)
                    act.activation(pT[:, t % 2, :, :], tp[:, :, :], ACT.Copy).then_inc(s_pt, 1)
                    act.wait_ge(s_aTp, i * TILES + t + 1)
                    act.activation(attT[:, t % 2, :], o_t, ACT.Copy).then_inc(s_aT, 1)
                act.wait_ge(s_x2Tp, i + 1)
                act.activation(x2T[:, :], sc[:, 0, 1, :], ACT.Copy).then_inc(s_x2T, 1)
                for c in range(FC):
                    hp = tp.rearrange("p (a b) n -> p a (b n)", a=2)[:, c, :] if c < 2 else sc[:, 1, c - 2, :]
                    act.wait_ge(s_h, i * FC + c + 1)
                    act.activation(hT[:, c, :], hp, ACT.Relu).then_inc(s_hT, 1)

        @block.gpsimd
        def _(pool):
            pool.memset(neghalf[:, :], -0.5).then_inc(s_ones, 1)
            pool.memset(va[:, :, :, :, :], 0.0).then_inc(s_ones, 1)
            pool.wait_ge(s_ones, 2)
            pool.memset(va[0:64, :, :, 0, DH:VW], 1.0).then_inc(s_ones, 1)
            pool.memset(va[64:128, :, :, 1, DH:VW], 1.0).then_inc(s_ones, 1)
            pool.wait_ge(s_const, NCONST)
            pool.sem_inc(s_cfree, 1)
            with pool.Fori(0, GROUPS) as i:
                pool.wait_ge(s_k, i + 1)
                pool.tensor_tensor(kM[:, :, :, :],
                                   kT.rearrange("p (b o s) -> p b o s", b=GB, o=1).broadcast_to((P, GB, 8, S)),
                                   headmask.rearrange("p (b h s) -> p b h s", b=1, s=1).broadcast_to((P, GB, 8, S)),
                                   ALU.mult).then_inc(s_km, 1)
                pool.wait_ge(s_x, i * 16 + 16)
                pool.tensor_tensor(xb[:, :, :], xin[:, :, :],
                                   bo.rearrange("p (o n) -> p o n", o=1).broadcast_to((P, TILES, D)), ALU.add).then_inc(s_xb, 1)
                pool.wait_ge(s_c, i * 16 + 16)
                pool.tensor_tensor(csq[:, :, :], cin[:, :, :], cin[:, :, :], ALU.mult).then_inc(s_csq, 1)
                pool.wait_ge(s_csq, i + 1)
                pool.sem_inc(s_cfree, 1)
                for n in range(2):
                    pool.wait_ge(s_var, i * 2 + n + 1)
                    pool.tensor_tensor(rs[:, :], ve[:, :], neghalf[:, :], ALU.pow).then_inc(s_rstd, 1)

        @block.vector
        def _(v):
            v.wait_ge(s_const, NCONST)
            v.wait_ge(s_ones, 4)
            v.sem_inc(s_sub, 1)
            v.sem_inc(s_plc, 1)
            v.sem_inc(s_sx2, 1)
            v.sem_inc(s_sf1, 1)
            with v.Fori(0, GROUPS) as i:
                step = [0]
                STEPS = 10

                def link(ins):
                    step[0] += 1
                    ins.then_inc(s_dv, 1)
                    v.wait_ge(s_dv, i * STEPS + step[0])

                v.wait_ge(s_vp, i + 1)
                v5 = tp.rearrange("p b (j r d) -> p b j r d", j=8, r=2)
                b4 = bv.rearrange("p (o j r d) -> p o j r d", o=1, j=8, r=2)
                for par in range(2):
                    q = slice(64 * par, 64 * par + 64)
                    m = v.tensor_tensor(va[q, :, :, par, 0:DH], v5[q, :, :, par, :],
                                        b4[q, :, :, par, :].broadcast_to((64, GB, 8, DH)), ALU.add)
                m.then_inc(s_va, 1)

                def softmax(t):
                    v.wait_ge(s_sc, i * TILES + t + 1)
                    s4 = sc[:, t % 2, :, :].rearrange("p r (h k) -> p (r h) k", k=S)
                    v.tensor_reduce(mx[:, t % 2, :], s4, AX.X, ALU.max).then_inc(s_mx, 1)
                    v.wait_ge(s_mx, i * TILES + t + 1)
                    if t >= 2:
                        v.wait_ge(s_tpa, i * TILES + t - 1)
                    v.tensor_tensor(e[:, t % 2, :, :], s4,
                                    mx[:, t % 2, :].rearrange("p (h o) -> p h o", o=1).broadcast_to((P, H, S)),
                                    ALU.subtract).then_inc(s_sub, 1)

                def normalise(t):
                    v.wait_ge(s_o, i * TILES + t + 1)
                    for b in range(2):
                        q = slice(64 * b, 64 * b + 64)
                        m = v.reciprocal(rden[q, t % 2, :].rearrange("p (j r) -> p j r", j=8), o_v[q, :, b, :, DH])
                    m.then_inc(s_rd, 1)
                    v.wait_ge(s_rd, i * TILES + t + 1)
                    for b in range(2):
                        q = slice(64 * b, 64 * b + 64)
                        m = v.tensor_tensor(att[q, t % 2, :].rearrange("p (j r d) -> p j r d", j=8, r=2),
                                            o_v[q, :, b, :, 0:DH],
                                            rden[q, t % 2, :].rearrange("p (j r o) -> p j r o", j=8, r=2)
                                            .broadcast_to((64, 8, 2, DH)), ALU.mult)
                    m.then_inc(s_at, 1)

                def layernorm(dst, n, done):
                    for t in range(TILES):
                        m = v.bn_stats(st[:, t, :], r[:, t, :])
                    link(m)
                    v.sem_inc(s_vturn, 1)
                    for t in range(TILES):
                        m = v.bn_aggr(mv[:, t, :], st[:, t, :])
                    link(m)
                    v.tensor_scalar(ve[:, :], mv[:, :, 1], LN_EPS, None, ALU.add).then_inc(s_var, 1)
                    v.wait_ge(s_rstd, i * 2 + n + 1)
                    for t in range(TILES):
                        m = v.tensor_scalar(dst[:, t, :], r[:, t, :], mv[:, t, 0:1], rs[:, t:t + 1],
                                            ALU.subtract, ALU.mult)
                    m.then_inc(done, 1)

                softmax(0)
                for t in range(TILES):
                    if t + 1 < TILES:
                        softmax(t + 1)
                    normalise(t)
                v.wait_ge(s_y, i * TILES + TILES)
                v.wait_ge(s_xb, i + 1)
                link(v.tensor_tensor(r[:, :, :], yy[:, :, :], xb[:, :, :], ALU.add))
                layernorm(x1, 0, s_x1)
                v.wait_ge(s_x1, i + 1)
                v.wait_ge(s_r, i + 1)
                link(v.scalar_tensor_tensor(r[:, :, :].rearrange("p t d -> p (t d)"), sc[:, 0, 0, :], 1.0,
                                            x1[:, :, :].rearrange("p t d -> p (t d)"), ALU.add, ALU.mult))
                v.wait_ge(s_sx2, i * 16 + 1)
                layernorm(x2, 1, s_x2)
                v.wait_ge(s_f, i + 1)
                v.wait_ge(s_sf1, i * 16 + 1)
                v.tensor_copy(f1[:, :, :], yy[:, :, :]).then_inc(s_f1, 1)
                v.wait_ge(s_pl, i + 1)
                v.tensor_copy(pooledT[:, bass.ds(i * GB, GB)], oa[:, 460:468]).then_inc(s_plc, 1)
                STEPS_USED = step[0]
                assert STEPS_USED <= STEPS
                for _ in range(STEPS - STEPS_USED):
                    v.sem_inc(s_dv, 1)


FULL = 12 * D
KEEP = 4 * D
FCH = FULL // P
BISECT = 48
NOVELTY = float(np.float32(0.7)) * B * KEEP


def route(nc, d, keep, first, run):
    ident, pooledT, go, mask, maskT = (keep[k] for k in ("ident", "pooledT", "go", "mask", "maskT"))
    name = ("R" if not run else "S" if first else "T") + "_"
    choose = first or not run
    with ExitStack() as ctx:
        def sb(n, shape, dt=F32):
            return ctx.enter_context(nc.sbuf_tensor(name + n, shape, dt))

        def pb(n, shape, dt=F32):
            return ctx.enter_context(nc.psum_tensor(name + n, shape, dt))

        sem = stage_semaphores(nc, ctx, name)

        s_const = sem("const")
        if run:
            wmT = sb("wmT", [P, FULL]); wpT = sb("wpT", [P, FCH, D]); meanw = sb("meanw", [P, 2])
            xc = sb("xc", [P, TILES, D]); xT = sb("xT", [P, GTOK])
            hr = sb("hr", [P, FCH, GTOK]); hm = sb("hm", [P, FCH, GTOK]); fo = sb("fo", [P, TILES, D])
            ph = pb("ph", [P, 3, GTOK]); pt = pb("pt", [P, GTOK]); pf = pb("pf", [P, TILES, D])
            s_x = sem("x"); s_xfree = sem("xfree"); s_xTp = sem("xTp"); s_xT = sem("xT")
            s_h = sem("h"); s_hr = sem("hr"); s_hm = sem("hm"); s_f = sem("f"); s_fo = sem("fo"); s_fst = sem("fst")
            s_pl = sem("pl"); s_plc = sem("plc")
        if choose:
            wc1T = sb("wc1T", [P, D // 4]); wc2T = sb("wc2T", [D // 4, FULL])
            hid = sb("hid", [D // 4, B]); ck = sb("ck", [P, FULL]); junk = sb("junk", [P, FULL])
            gt = sb("gt", [P, FULL]); eq = sb("eq", [P, FULL]); cum = sb("cum", [P, FULL]); old = sb("old", [P, FULL])
            one = sb("one", [P, FULL]); ones = sb("ones", [P, 1])
            sm = sb("sm", [P, 16])
            pc = pb("pc", [P, 3, 512]) if not run else None
            s_hid = sem("hid"); s_hidr = sem("hidr"); s_ck = sem("ck"); s_d = sem("d"); s_msk = sem("msk"); s_pm = sem("pm")
            s_mt = sem("mt"); s_tot = sem("tot"); s_go = sem("go"); s_loop = sem("loop")
            if run:
                pc = ph
        pm = pb("pm", [P, 512])
        block = ctx.enter_context(nc.Block())
        loads = []
        if run:
            loads += [(wmT[:, :], d["f0_wmT"]), (wpT[:, :, :], d["f0_wpT"].rearrange("(c p) n -> p c n", p=P)),
                      (meanw[:, :], d["meanw"])]
        if choose:
            loads += [(wc1T[:, :], d["f0_wc1T"]), (wc2T[:, :], d["f0_wc2T"])]
        NCONST = 16 * len(loads)

        def conditional(eng, body):
            if not run:
                body()
                return
            due = eng.value_load(go[0:1, 0:1], min_val=0, max_val=1)
            with eng.If(due > 0):
                body()
                eng.nop()
            with eng.Else():
                eng.nop()

        @block.sync
        def _(sp):
            def body():
                for dst, src in loads:
                    sp.dma_start(dst, src).then_inc(s_const, 16)
                if run:
                    with sp.Fori(0, GROUPS) as i:
                        sp.wait_ge(s_xfree, i + 1)
                        sp.dma_start(xc[:, :, :], d["s_f1"][i]).then_inc(s_x, 16)
                        sp.wait_ge(s_fo, i + 1)
                        sp.dma_start(d["s_f1"][i], fo[:, :, :]).then_inc(s_fst, 16)
                    sp.wait_ge(s_fst, GROUPS * 16)
                else:
                    sp.wait_ge(s_const, NCONST)
            conditional(sp, body)

        @block.tensor
        def _(pe):
            def body():
                pe.wait_ge(s_const, NCONST)
                if run:
                    with pe.Fori(0, GROUPS) as i:
                        pe.wait_ge(s_x, i * 16 + 16)
                        for t in range(TILES):
                            m = pe.transpose(pt[:, t * P:(t + 1) * P], xc[:, t, :], ident[:, :])
                        m.then_inc(s_xTp, 1)
                        pe.wait_ge(s_xT, i + 1)
                        for c in range(FCH):
                            if c >= 3:
                                pe.wait_ge(s_hr, i * FCH + c - 2)
                            pe.matmul(ph[:, c % 3, :], wmT[:, c * P:(c + 1) * P], xT[:, :],
                                      start=True, stop=True).then_inc(s_h, 1)
                        pe.wait_ge(s_hm, i * FCH + FCH + 1)
                        for t in range(TILES):
                            for c in range(FCH):
                                m = pe.matmul(pf[:, t, :], hm[:, c, t * P:(t + 1) * P], wpT[:, c, :],
                                              start=(c == 0), stop=(c == FCH - 1))
                        m.then_inc(s_f, 1)
                        pe.wait_ge(s_fo, i + 1)
                        if choose:
                            pe.wait_ge(s_plc, i + 1)
                            for t in range(TILES):
                                m = pe.matmul(pm[:, 2 * t:2 * t + 2], fo[:, t, :], meanw[:, :], start=True, stop=True)
                            m.then_inc(s_pl, 1)
                if choose:
                    if run:
                        pe.wait_ge(s_plc, GROUPS + 1)
                    pe.matmul(pm[0:D // 4, 128:128 + B], wc1T[:, :], pooledT[:, :], start=True, stop=True).then_inc(s_hid, 1)
                    pe.wait_ge(s_hidr, 1)
                    for c in range(3):
                        m = pe.matmul(pc[:, c, :], hid[:, :], wc2T[:, c * 512:(c + 1) * 512], start=True, stop=True)
                    m.then_inc(s_ck, 1)
                    pe.wait_ge(s_msk, 1)
                    for c in range(3):
                        for j in range(4):
                            m = pe.transpose(pc[:, c, j * P:(j + 1) * P], mask[:, (4 * c + j) * P:(4 * c + j + 1) * P], ident[:, :])
                    m.then_inc(s_pm, 1)
                    pe.matmul(pm[0:1, 0:1], sm[:, 8:9], ones[:, :], start=True, stop=True).then_inc(s_tot, 1)
            conditional(pe, body)

        @block.scalar
        def _(act):
            def body():
                act.wait_ge(s_const, NCONST)
                if run:
                    act.sem_inc(s_xfree, 1)
                    with act.Fori(0, GROUPS) as i:
                        act.wait_ge(s_xTp, i + 1)
                        act.activation(xT[:, :], pt[:, :], ACT.Copy).then_inc(s_xT, 1)
                        act.wait_ge(s_xT, i + 1)
                        act.sem_inc(s_xfree, 1)
                        for c in range(FCH):
                            act.wait_ge(s_h, i * FCH + c + 1)
                            if c == 0:
                                act.wait_ge(s_hm, i * FCH + 1)
                            act.activation(hr[:, c, :], ph[:, c % 3, :], ACT.Relu).then_inc(s_hr, 1)
                if choose:
                    act.wait_ge(s_hid, 1)
                    act.activation(hid[:, :], pm[0:D // 4, 128:128 + B], ACT.Relu).then_inc(s_hidr, 1)
                    act.wait_ge(s_pm, 1)
                    for c in range(3):
                        m = act.activation(maskT[:, 4 * c:4 * c + 4, :], pc[:, c, :], ACT.Copy)
                    m.then_inc(s_mt, 1)
                    act.wait_ge(s_mt, 1)
            conditional(act, body)

        @block.gpsimd
        def _(pool):
            pool.nop()

        @block.vector
        def _(v):
            n = [0]

            def link(ins):
                n[0] += 1
                ins.then_inc(s_d, 1)
                v.wait_ge(s_d, n[0])

            def body():
                v.wait_ge(s_const, NCONST)
                if run:
                    v.sem_inc(s_hm, 1)
                    if choose:
                        v.sem_inc(s_plc, 1)
                    with v.Fori(0, GROUPS) as i:
                        for c in range(FCH):
                            v.wait_ge(s_hr, i * FCH + c + 1)
                            m4 = maskT[:, c, bass.ds(i * GB, GB)].rearrange("p (b o) -> p b o", o=1).broadcast_to((P, GB, S))
                            v.tensor_tensor(hm[:, c, :].rearrange("p (b s) -> p b s", s=S),
                                            hr[:, c, :].rearrange("p (b s) -> p b s", s=S), m4, ALU.mult).then_inc(s_hm, 1)
                        v.wait_ge(s_f, i + 1)
                        v.wait_ge(s_x, i * 16 + 16)
                        v.tensor_copy(fo[:, :, :], pf[:, :, :]).then_inc(s_fo, 1)
                        if choose:
                            v.wait_ge(s_pl, i + 1)
                            v.tensor_copy(pooledT[:, bass.ds(i * GB, GB)], pm[:, 0:8]).then_inc(s_plc, 1)
                if not choose:
                    return
                lo, w, mid, cnt, t0, hi, need, cg = (sm[:, k:k + 1] for k in range(8))
                new = sm[:, 8:9]
                v.wait_ge(s_ck, 1)
                v.memset(one[:, :], 1.0)
                v.memset(ones[:, :], 1.0)
                if run:
                    link(v.tensor_copy(old[:, :], mask[:, :]))
                    link(v.memset(old[:, 0:KEEP], 1.0))
                else:
                    v.memset(old[:, KEEP:FULL], 0.0)
                    link(v.memset(old[:, 0:KEEP], 1.0))
                link(v.tensor_copy(ck[:, :], pc[:, :, :].rearrange("p c n -> p (c n)")))
                v.tensor_reduce(lo, ck[:, :], AX.X, ALU.min)
                link(v.tensor_reduce(hi, ck[:, :], AX.X, ALU.max))
                link(v.tensor_tensor(w, hi, lo, ALU.subtract))
                link(v.tensor_scalar(w, w, 2.0, None, ALU.mult))
                with v.Fori(0, BISECT) as j:
                    k = [0]

                    def chain(ins):
                        k[0] += 1
                        ins.then_inc(s_loop, 1)
                        v.wait_ge(s_loop, j * 5 + k[0])

                    chain(v.tensor_scalar(w, w, 0.5, None, ALU.mult))
                    chain(v.tensor_tensor(mid, lo, w, ALU.add))
                    chain(v.tensor_scalar(junk[:, :], ck[:, :], mid, 0.0, ALU.is_ge, ALU.add, accum_out=cnt))
                    chain(v.scalar_tensor_tensor(t0, cnt, float(KEEP), w, ALU.is_ge, ALU.mult))
                    chain(v.tensor_tensor(lo, lo, t0, ALU.add))
                link(v.tensor_scalar(junk[:, :], ck[:, :], lo, 3.0e38, ALU.is_lt, ALU.mult))
                link(v.tensor_tensor(junk[:, :], junk[:, :], ck[:, :], ALU.add))
                link(v.tensor_reduce(hi, junk[:, :], AX.X, ALU.min))
                v.tensor_scalar(gt[:, :], ck[:, :], hi, 0.0, ALU.is_gt, ALU.add, accum_out=cg)
                link(v.tensor_scalar(eq[:, :], ck[:, :], hi, None, ALU.is_equal))
                link(v.tensor_tensor_scan(cum[:, :], one[:, :], gt[:, :], 0.0, ALU.mult, ALU.add))
                link(v.scalar_tensor_tensor(gt[:, :], cum[:, :], float(KEEP), gt[:, :], ALU.is_le, ALU.mult))
                link(v.tensor_scalar(need, cg, -1.0, float(KEEP), ALU.mult, ALU.add))
                link(v.tensor_tensor_scan(cum[:, :], one[:, :], eq[:, :], 0.0, ALU.mult, ALU.add))
                link(v.scalar_tensor_tensor(eq[:, :], cum[:, :], need, eq[:, :], ALU.is_le, ALU.mult))
                link(v.tensor_tensor(mask[:, :], gt[:, :], eq[:, :], ALU.add))
                link(v.tensor_tensor(junk[:, :], mask[:, :], old[:, :], ALU.mult))
                link(v.tensor_tensor(junk[:, :], mask[:, :], junk[:, :], ALU.subtract))
                v.tensor_reduce(new, junk[:, :], AX.X, ALU.add).then_inc(s_msk, 1)
                v.wait_ge(s_tot, 1)
                v.tensor_scalar(go[0:1, :], pm[0:1, 0:1], keep["novelty"], None, ALU.is_ge).then_inc(s_go, 1)
                v.wait_ge(s_go, 1)
            conditional(v, body)


CONV = 4
PAD = CONV - 1
TW = 4 * D + H


def delta_inputs(nc, d, keep):
    ident = keep["ident"]
    rows_g = d["s_rows"].rearrange("(g t q) s n -> g (q s) t n", t=TILES, q=2)
    with ExitStack() as ctx:
        def sb(name, shape, dt=F32):
            return ctx.enter_context(nc.sbuf_tensor("C_" + name, shape, dt))

        def pb(name, shape, dt=F32):
            return ctx.enter_context(nc.psum_tensor("C_" + name, shape, dt))

        sem = stage_semaphores(nc, ctx, "C_")

        w = sb("w", [P, 3, D]); bias = sb("bias", [P, 3]); cw = sb("cw", [P, 3, CONV])
        wab = sb("wab", [P, 2 * H]); bab = sb("bab", [P, 2 * H]); wg = sb("wg", [P, D]); bg = sb("bg", [P, D])
        neghalf = sb("neghalf", [P, TILES]); half = sb("half", [P, 2 * TILES * H])
        xa = sb("xa", [P, TILES, D]); xf = sb("xf", [P, TILES, D]); r = sb("r", [P, TILES, D]); x3 = sb("x3", [P, TILES, D])
        st = sb("st", [P, TILES, 6]); mv = sb("mv", [P, TILES, 2]); ve = sb("ve", [P, TILES]); rs = sb("rs", [P, TILES])
        xT = sb("xT", [P, GTOK])
        z = sb("z", [P, 3, GB, PAD + S]); cv = sb("cv", [P, 3, GTOK]); cs = sb("cs", [P, 3, GTOK])
        sq = sb("sq", [P, 2, TILES, D]); ss = sb("ss", [P, 2 * TILES * H]); nr = sb("nr", [P, 2 * TILES * H])
        ne = sb("ne", [P, 2 * TILES * H]); rn = sb("rn", [P, 2 * TILES * H])
        abr = sb("abr", [P, TILES, 2 * H]); abt = sb("abt", [P, TILES, 2 * H]); ab = sb("ab", [P, TILES, 2 * H])
        apb = sb("apb", [P, TILES, H])
        gr = sb("gr", [P, TILES, D]); g = sb("g", [P, TILES, D])
        out = sb("out", [P, TILES, TW])
        vs = sb("vs", [P, TILES, D])
        px = pb("px", [P, GTOK]); pq = pb("pq", [P, 3, GTOK]); pg = pb("pg", [P, TILES, D]); pt = pb("pt", [P, 3, TILES, D])
        pab = px[:, 0:TILES * 2 * H].rearrange("p (t n) -> p t n", t=TILES)

        s_const = sem("const"); s_set = sem("set"); s_x = sem("x"); s_xfree = sem("xfree"); s_dv = sem("dv")
        s_var = sem("var"); s_rstd = sem("rstd"); s_x3 = sem("x3"); s_xTp = sem("xTp"); s_xT = sem("xT")
        s_p = sem("proj"); s_z = sem("z"); s_cv = sem("cv"); s_cs = sem("cs"); s_pt = sem("pt"); s_sq = sem("sq")
        s_ss = sem("ss"); s_nr = sem("nr"); s_ne = sem("ne"); s_qk = sem("qk"); s_vs = sem("vs"); s_abp = sem("abp")
        s_abr = sem("abr"); s_abt = sem("abt"); s_ab = sem("ab"); s_apb = sem("apb"); s_gp = sem("gp"); s_gr = sem("gr"); s_g = sem("g")
        s_out = sem("out"); s_sx = sem("sx3"); s_sg = sem("sg"); s_rows = sem("rows"); s_turn = sem("turn")
        block = ctx.enter_context(nc.Block())
        loads = [(w[:, :, :], d["l1_w"]), (bias[:, :], d["l1_b"]), (cw[:, :, :], d["l1_conv"]), (wab[:, :], d["l1_wab"]),
                 (bab[:, :], d["l1_bab"].broadcast_to((P, 2 * H))), (wg[:, :], d["l1_wg"]), (bg[:, :], d["l1_bg"].broadcast_to((P, D)))]
        NCONST = 16 * len(loads)

        @block.sync
        def _(sp):
            for dst, src in loads:
                sp.dma_start(dst, src).then_inc(s_const, 16)
            with sp.Fori(0, GROUPS) as i:
                sp.wait_ge(s_xfree, i + 1)
                sp.dma_start(xa[:, :, :], d["s_x2"][i]).then_inc(s_x, 16)
                sp.dma_start(xf[:, :, :], d["s_f1"][i]).then_inc(s_x, 16)
                sp.wait_ge(s_x3, i + 1)
                sp.dma_start(d["s_x3"][i], x3[:, :, :]).then_inc(s_sx, 16)
                sp.wait_ge(s_g, i + 1)
                sp.dma_start(d["s_gate"][i], g[:, :, :]).then_inc(s_sg, 16)
                sp.wait_ge(s_out, i + 2)
                for t in range(TILES):
                    sp.dma_start(rows_g[i][:, t, :], out[:, t, :]).then_inc(s_rows, 16)
            sp.wait_ge(s_sx, GROUPS * 16 + 1)
            sp.wait_ge(s_sg, GROUPS * 16 + 1)
            sp.wait_ge(s_rows, GROUPS * 16 * TILES + 1)

        @block.tensor
        def _(pe):
            pe.wait_ge(s_const, NCONST)
            with pe.Fori(0, GROUPS) as i:
                pe.wait_ge(s_x3, i + 1)
                pe.wait_ge(s_abr, i + 1)
                for t in range(TILES):
                    m = pe.transpose(px[:, t * P:(t + 1) * P], x3[:, t, :], ident[:, :])
                m.then_inc(s_xTp, 1)
                pe.wait_ge(s_xT, i + 1)
                pe.wait_ge(s_z, i * 3 + 1)
                for c in range(3):
                    pe.matmul(pq[:, c, :], w[:, c, :], xT[:, :], start=True, stop=True).then_inc(s_p, 1)
                for t in range(TILES):
                    m = pe.matmul(pab[:, t, :], xT[:, t * P:(t + 1) * P], wab[:, :], start=True, stop=True)
                m.then_inc(s_abp, 1)
                pe.wait_ge(s_gr, i + 1)
                for t in range(TILES):
                    m = pe.matmul(pg[:, t, :], xT[:, t * P:(t + 1) * P], wg[:, :], start=True, stop=True)
                m.then_inc(s_gp, 1)
                pe.wait_ge(s_qk, i + 1)
                pe.wait_ge(s_vs, i + 1)
                for c in range(3):
                    pe.wait_ge(s_cs, i * 3 + c + 1)
                    for t in range(TILES):
                        m = pe.transpose(pt[:, c, t, :], cs[:, c, t * P:(t + 1) * P], ident[:, :])
                    m.then_inc(s_pt, 1)

        @block.scalar
        def _(act):
            act.wait_ge(s_const, NCONST)
            act.wait_ge(s_set, 3)
            act.sem_inc(s_z, 1)
            act.sem_inc(s_vs, 1)
            act.sem_inc(s_sg, 1)
            with act.Fori(0, GROUPS) as i:
                act.wait_ge(s_xTp, i + 1)
                act.activation(xT[:, :], px[:, :], ACT.Copy).then_inc(s_xT, 1)
                for c in range(3):
                    act.wait_ge(s_p, i * 3 + c + 1)
                    if c == 0:
                        act.wait_ge(s_cv, i * 3 + 1)
                    act.activation(z[:, c, :, PAD:PAD + S], pq[:, c, :].rearrange("p (b s) -> p b s", s=S),
                                   ACT.Identity, bias=bias[:, c:c + 1]).then_inc(s_z, 1)
                act.wait_ge(s_abr, i + 2)
                act.activation(abt[:, :, :], abr[:, :, :], ACT.Tanh, scale=0.5).then_inc(s_abt, 1)
                act.wait_ge(s_gr, i + 2)
                act.wait_ge(s_sg, i * 16 + 1)
                act.activation(g[:, :, :], gr[:, :, :], ACT.Silu).then_inc(s_g, 1)
                for c in range(3):
                    act.wait_ge(s_cv, i * 3 + c + 2)
                    act.activation(cs[:, c, :], cv[:, c, :], ACT.Silu).then_inc(s_cs, 1)
                for c in range(2):
                    act.wait_ge(s_pt, i * 3 + c + 1)
                    act.activation(sq[:, c, :, :], pt[:, c, :, :], ACT.Square).then_inc(s_sq, 1)
                act.wait_ge(s_pt, i * 3 + 3)
                act.wait_ge(s_out, i + 1)
                act.activation(vs[:, :, :], pt[:, 2, :, :], ACT.Copy).then_inc(s_vs, 1)

        @block.gpsimd
        def _(pool):
            pool.memset(neghalf[:, :], -0.5).then_inc(s_set, 1)
            pool.memset(half[:, :], 0.5).then_inc(s_set, 1)
            pool.memset(z[:, :, :, 0:PAD], 0.0).then_inc(s_set, 1)
            pool.wait_ge(s_set, 3)
            pool.sem_inc(s_out, 1)
            with pool.Fori(0, GROUPS) as i:
                pool.wait_ge(s_var, i + 1)
                pool.tensor_tensor(rs[:, :], ve[:, :], neghalf[:, :], ALU.pow).then_inc(s_rstd, 1)
                pool.wait_ge(s_ss, i + 1)
                pool.tensor_tensor(nr[:, :], ss[:, :], half[:, :], ALU.pow).then_inc(s_nr, 1)
                pool.wait_ge(s_qk, i + 2)
                pool.wait_ge(s_ab, i + 1)
                pool.tensor_tensor(out[:, :, 2 * D:3 * D].rearrange("p t (h e) -> p t h e", e=DH),
                                   out[:, :, D:2 * D].rearrange("p t (h e) -> p t h e", e=DH),
                                   apb.rearrange("p t (h o) -> p t h o", o=1).broadcast_to((P, TILES, H, DH)), ALU.mult)
                pool.wait_ge(s_vs, i + 2)
                pool.tensor_tensor(out[:, :, 3 * D:4 * D].rearrange("p t (h e) -> p t h e", e=DH),
                                   vs.rearrange("p t (h e) -> p t h e", e=DH),
                                   ab[:, :, H:2 * H].rearrange("p t (h o) -> p t h o", o=1).broadcast_to((P, TILES, H, DH)),
                                   ALU.mult).then_inc(s_out, 1)

        @block.vector
        def _(v):
            v.wait_ge(s_const, NCONST)
            v.wait_ge(s_set, 3)
            v.sem_inc(s_xfree, 1)
            v.sem_inc(s_cv, 1)
            v.sem_inc(s_abr, 1)
            v.sem_inc(s_gr, 1)
            v.sem_inc(s_qk, 1)
            v.sem_inc(s_sx, 1)
            v.sem_inc(s_rows, 1)
            with v.Fori(0, GROUPS) as i:
                n = [0]
                STEPS = 20

                def link(ins):
                    n[0] += 1
                    ins.then_inc(s_dv, 1)
                    v.wait_ge(s_dv, i * STEPS + n[0])

                v.wait_ge(s_x, i * 32 + 32)
                link(v.tensor_tensor(r[:, :, :], xa[:, :, :], xf[:, :, :], ALU.add))
                v.sem_inc(s_xfree, 1)
                for t in range(TILES):
                    m = v.bn_stats(st[:, t, :], r[:, t, :])
                link(m)
                v.sem_inc(s_turn, 1)
                for t in range(TILES):
                    m = v.bn_aggr(mv[:, t, :], st[:, t, :])
                link(m)
                v.tensor_scalar(ve[:, :], mv[:, :, 1], LN_EPS, None, ALU.add).then_inc(s_var, 1)
                v.wait_ge(s_rstd, i + 1)
                v.wait_ge(s_sx, i * 16 + 1)
                for t in range(TILES):
                    m = v.tensor_scalar(x3[:, t, :], r[:, t, :], mv[:, t, 0:1], rs[:, t:t + 1], ALU.subtract, ALU.mult)
                m.then_inc(s_x3, 1)
                v.wait_ge(s_abp, i + 1)
                v.tensor_tensor(abr[:, :, :], pab, bab.rearrange("p (o n) -> p o n", o=1).broadcast_to((P, TILES, 2 * H)),
                                ALU.add).then_inc(s_abr, 1)
                v.wait_ge(s_gp, i + 1)
                v.tensor_tensor(gr[:, :, :], pg[:, :, :], bg.rearrange("p (o n) -> p o n", o=1).broadcast_to((P, TILES, D)),
                                ALU.add).then_inc(s_gr, 1)
                for c in range(3):
                    v.wait_ge(s_z, i * 3 + c + 2)
                    acc = cv[:, c, :].rearrange("p (b s) -> p b s", s=S)
                    for k in range(CONV):
                        src = z[:, c, :, k:k + S]
                        if k == 0:
                            link(v.tensor_scalar(acc, src, cw[:, c, k:k + 1], None, ALU.mult))
                        elif k < CONV - 1:
                            link(v.scalar_tensor_tensor(acc, src, cw[:, c, k:k + 1], acc, ALU.mult, ALU.add))
                        else:
                            v.scalar_tensor_tensor(acc, src, cw[:, c, k:k + 1], acc, ALU.mult, ALU.add).then_inc(s_cv, 1)
                v.wait_ge(s_abt, i + 1)
                link(v.tensor_scalar(ab[:, :, :], abt[:, :, :], 0.5, 0.5, ALU.mult, ALU.add))
                v.wait_ge(s_out, i + 1)
                v.wait_ge(s_rows, i * 16 * TILES + 1)
                v.tensor_tensor(apb[:, :, :], ab[:, :, 0:H], ab[:, :, H:2 * H], ALU.mult)
                v.tensor_copy(out[:, :, 4 * D:TW], ab[:, :, 0:H]).then_inc(s_ab, 1)
                v.wait_ge(s_sq, i * 2 + 2)
                v.tensor_reduce(ss[:, :], sq.rearrange("p c t (h e) -> p (c t h) e", e=DH), AX.X, ALU.add).then_inc(s_ss, 1)
                v.wait_ge(s_nr, i + 1)
                link(v.tensor_scalar(ne[:, :], nr[:, :], 1e-6, None, ALU.add))
                link(v.reciprocal(rn[:, :], ne[:, :]))
                for c in range(2):
                    m = v.tensor_tensor(out[:, :, c * D:(c + 1) * D].rearrange("p t (h e) -> p t h e", e=DH),
                                        pt[:, c, :, :].rearrange("p t (h e) -> p t h e", e=DH),
                                        rn.rearrange("p (c t h o) -> p c t h o", c=2, t=TILES, o=1)[:, c].broadcast_to((P, TILES, H, DH)),
                                        ALU.mult)
                m.then_inc(s_qk, 1)
                assert n[0] <= STEPS, n
                for _ in range(STEPS - n[0]):
                    v.sem_inc(s_dv, 1)


def delta_scan(nc, d, keep):
    ident = keep["ident"]
    HH = H // 2
    CH = 8
    with ExitStack() as ctx:
        def sb(name, shape, dt=F32):
            return ctx.enter_context(nc.sbuf_tensor("D_" + name, shape, dt))

        def pb(name, shape, dt=F32):
            return ctx.enter_context(nc.psum_tensor("D_" + name, shape, dt))

        sem = stage_semaphores(nc, ctx, "D_")

        rows = sb("rows", [P, 1 + S, TW])
        Sx = [sb(f"S{f}", [P, HH, DH, DH]) for f in range(2)]
        aS = [sb(f"aS{f}", [P, HH, DH, DH]) for f in range(2)]
        T1 = [sb(f"T1{f}", [P, HH, DH, DH]) for f in range(2)]
        T2 = sb("T2", [P, H, DH, DH]); sk = [sb(f"sk{f}", [P, HH * DH]) for f in range(2)]
        U = [sb(f"U{f}", [P, HH, DH, DH]) for f in range(2)]
        de = [sb(f"de{f}", [P, HH * DH]) for f in range(2)]
        gs = sb("gs", [P, D]); gb = sb("gb", [P, D]); sums = sb("sums", [P, 2, H]); small = sb("small", [P, 6, H])
        A = sb("A", [P, D]); Bc = sb("Bc", [P, D]); nh = sb("nh", [P, H])
        po = pb("po", [P, 512])
        s_const = sem("const"); s_set = sem("set"); s_rows = sem("rows"); s_pad = sem("pad")
        s_t1 = [sem(f"t1{f}") for f in range(2)]; s_sk = [sem(f"sk{f}") for f in range(2)]
        s_as = [sem(f"as{f}") for f in range(2)]; s_de = [sem(f"de{f}") for f in range(2)]
        s_u = [sem(f"u{f}") for f in range(2)]; s_S = [sem(f"S{f}") for f in range(2)]
        s_t2 = sem("t2"); s_o = sem("o"); s_oc = sem("oc")
        s_sqr = sem("sqr"); s_n = sem("n"); s_var = sem("var"); s_rstd = sem("rstd"); s_y = sem("y"); s_sy = sem("sy")
        block = ctx.enter_context(nc.Block())
        NCONST = 32
        YC = 4

        def vec(t, c, f, how):
            x = rows[:, bass.ds(t + 1, 1), c * D + f * HH * DH:c * D + (f + 1) * HH * DH].rearrange("p o (h e) -> p (o h) e", h=HH)
            if how == "k":
                return x.rearrange("p h (o e) -> p h o e", o=1).broadcast_to((P, HH, DH, DH))
            return x.rearrange("p h (e o) -> p h e o", o=1).broadcast_to((P, HH, DH, DH))

        @block.sync
        def _(sp):
            sp.dma_start(gs[:, :], d["l1_gs"].broadcast_to((P, D))).then_inc(s_const, 16)
            sp.dma_start(gb[:, :], d["l1_gb"].broadcast_to((P, D))).then_inc(s_const, 16)
            for c in range(S // CH):
                q = slice(c * CH, (c + 1) * CH)
                sp.dma_start(rows[:, 1 + c * CH:1 + (c + 1) * CH, :], d["s_rows"][:, q, :]).then_inc(s_rows, 16)
                sp.wait_ge(s_rows, 16 * (c + 1))
            for c in range(YC):
                sp.wait_ge(s_y, c + 1)
                q = slice(c * S // YC, (c + 1) * S // YC)
                sp.dma_start(d["s_y"][:, q, :], rows[:, 1 + c * S // YC:1 + (c + 1) * S // YC, 2 * D:3 * D]).then_inc(s_sy, 16)
            sp.wait_ge(s_sy, 16 * YC)

        @block.tensor
        def _(pe):
            pe.sem_inc(s_o, 1)
            with pe.Fori(0, S) as t:
                pe.wait_ge(s_t2, t + 1)
                pe.wait_ge(s_oc, t + 1)
                for e in range(DH):
                    m = pe.matmul(po[:, 0:D], ident[:, :], T2.rearrange("p h d e -> p (h d) e")[:, :, e],
                                  start=(e == 0), stop=(e == DH - 1))
                m.then_inc(s_o, 1)

        @block.scalar
        def _(act):
            act.wait_ge(s_set, 2)
            with act.Fori(0, S) as t:
                for f in range(2):
                    act.wait_ge(s_t1[f], t + 1)
                    for h in range(HH):
                        at = 4 * D + f * HH + h
                        m = act.activation(aS[f][:, h, :, :].rearrange("p d e -> p (d e)"), Sx[f][:, h, :, :].rearrange("p d e -> p (d e)"),
                                           ACT.Copy, scale=rows[:, bass.ds(t + 1, 1), at:at + 1].rearrange("p o n -> p (o n)"))
                    m.then_inc(s_as[f], 1)
                act.wait_ge(s_o, t + 1)
                act.activation(rows[:, bass.ds(t, 1), 0:D].rearrange("p o n -> p (o n)"), po[:, 0:D], ACT.Copy).then_inc(s_oc, 1)
            act.wait_ge(s_o, S + 1)
            act.activation(rows[:, S, 0:D], po[:, 0:D], ACT.Copy).then_inc(s_oc, 1)
            act.wait_ge(s_oc, S + 1)
            act.activation(rows[:, 1:, D:2 * D], rows[:, 1:, 0:D], ACT.Square).then_inc(s_sqr, 1)

        @block.gpsimd
        def _(pool):
            pool.memset(nh[:, :], -0.5).then_inc(s_set, 1)
            pool.wait_ge(s_set, 2)
            pool.wait_ge(s_var, 1)
            pool.tensor_tensor(small[:, 3, :], small[:, 2, :], nh[:, :], ALU.pow).then_inc(s_rstd, 1)

        @block.vector
        def _(v):
            v.memset(po[:, 0:D], 0.0).then_inc(s_set, 1)
            for f in range(2):
                v.memset(Sx[f][:, :, :, :], 0.0).then_inc(s_S[f], 1)
            with v.Fori(0, S // CH) as c:
                v.wait_ge(s_rows, c * 16 + 16)
                v.sem_inc(s_pad, 1)
                with v.Fori(0, CH) as j:
                    t = c * CH + j
                    for f in range(2):
                        v.wait_ge(s_S[f], t + 1)
                        v.tensor_tensor(T1[f][:, :, :, :], Sx[f][:, :, :, :], vec(t, 2, f, "k"), ALU.mult).then_inc(s_t1[f], 1)
                    for f in range(2):
                        v.wait_ge(s_t1[f], t + 1)
                        v.tensor_reduce(sk[f][:, :], T1[f].rearrange("p h d e -> p (h d) e"), AX.X, ALU.add).then_inc(s_sk[f], 1)
                    for f in range(2):
                        v.wait_ge(s_sk[f], t + 1)
                        vb = rows[:, bass.ds(t + 1, 1), 3 * D + f * HH * DH:3 * D + (f + 1) * HH * DH].rearrange("p o n -> p (o n)")
                        v.tensor_tensor(de[f][:, :], vb, sk[f][:, :], ALU.subtract).then_inc(s_de[f], 1)
                    for f in range(2):
                        v.wait_ge(s_de[f], t + 1)
                        v.tensor_tensor(U[f][:, :, :, :], de[f].rearrange("p (h d o) -> p h d o", h=HH, o=1).broadcast_to((P, HH, DH, DH)),
                                        vec(t, 1, f, "k"), ALU.mult).then_inc(s_u[f], 1)
                    for f in range(2):
                        v.wait_ge(s_u[f], t + 1)
                        v.wait_ge(s_as[f], t + 1)
                        v.tensor_tensor(Sx[f][:, :, :, :], aS[f][:, :, :, :], U[f][:, :, :, :], ALU.add).then_inc(s_S[f], 1)
                    v.wait_ge(s_o, t + 1)
                    for f in range(2):
                        v.wait_ge(s_S[f], t + 2)
                        m = v.tensor_tensor(T2[:, f * HH:(f + 1) * HH, :, :], Sx[f][:, :, :, :], vec(t, 0, f, "k"), ALU.mult)
                    m.then_inc(s_t2, 1)
            n = [0]

            def link(ins):
                n[0] += 1
                ins.then_inc(s_n, 1)
                v.wait_ge(s_n, n[0])

            cnt = 1.0 / (S * DH)
            o4 = rows[:, 1:, 0:D].rearrange("p s (h e) -> p h s e", h=H)
            q4 = rows[:, 1:, D:2 * D].rearrange("p s (h e) -> p h s e", h=H)
            v.wait_ge(s_oc, S + 1)
            v.tensor_reduce(sums[:, 0, :], o4, AX.XY, ALU.add)
            v.wait_ge(s_sqr, 1)
            link(v.tensor_reduce(sums[:, 1, :], q4, AX.XY, ALU.add))
            mu, m2, ve, rstd, t0 = (small[:, k, :] for k in range(5))
            link(v.tensor_scalar(mu, sums[:, 0, :], cnt, None, ALU.mult))
            link(v.tensor_tensor(t0, mu, mu, ALU.mult))
            link(v.scalar_tensor_tensor(m2, sums[:, 1, :], cnt, t0, ALU.mult, ALU.subtract))
            v.tensor_scalar(ve, m2, 1e-5, None, ALU.add).then_inc(s_var, 1)
            v.wait_ge(s_rstd, 1)
            v.wait_ge(s_const, NCONST)
            hd = lambda x: x.rearrange("p (h e) -> p h e", h=H)
            bc = lambda x: x.rearrange("p (h o) -> p h o", o=1).broadcast_to((P, H, DH))
            link(v.tensor_tensor(hd(A), hd(gs), bc(rstd), ALU.mult))
            link(v.tensor_tensor(hd(Bc), hd(A), bc(mu), ALU.mult))
            link(v.tensor_tensor(Bc[:, :], gb[:, :], Bc[:, :], ALU.subtract))
            for c in range(YC):
                q = slice(1 + c * S // YC, 1 + (c + 1) * S // YC)
                n4 = S // YC
                b3 = lambda x: x.rearrange("p (o n) -> p o n", o=1).broadcast_to((P, n4, D))
                link(v.tensor_tensor(rows[:, q, D:2 * D], rows[:, q, 0:D], b3(A), ALU.mult))
                v.tensor_tensor(rows[:, q, 2 * D:3 * D], rows[:, q, D:2 * D], b3(Bc), ALU.add).then_inc(s_y, 1)


XH, XD = 8, 64
XSCALE = XD ** -0.5
KEYS = 2 * S
XP = XH // 2
MASKED = -1e30


def latent_attention(nc, d, keep):
    ident = keep["ident"]
    with ExitStack() as ctx:
        def sb(name, shape, dt=F32):
            return ctx.enter_context(nc.sbuf_tensor("F_" + name, shape, dt))

        def pb(name, shape, dt=F32):
            return ctx.enter_context(nc.psum_tensor("F_" + name, shape, dt))

        sem = stage_semaphores(nc, ctx, "F_")

        wo = sb("wo", [P, D]); bo = sb("bo", [P, D])
        wqT = sb("wqT", [XD, XH, D]); wkT = sb("wkT", [XD, XH, D]); wvT = sb("wvT", [XD, XH, D]); wout = sb("wout", [XD, XH, D])
        qk = sb("qk", [P, XH, D]); vo = sb("vo", [P, XH, D])
        par = sb("par", [P, 5])
        gg = sb("gg", [P, 2])
        neghalf = sb("neghalf", [P, TILES])
        yi = sb("yi", [P, TILES, D]); gi = sb("gi", [P, TILES, D]); xi = sb("xi", [P, TILES, D]); ci = sb("ci", [P, TILES, D])
        mi = sb("mi", [P, GB, S], mybir.dt.uint8)
        zz = sb("zz", [P, TILES, D]); zT = sb("zT", [P, GTOK]); xb = sb("xb", [P, TILES, D]); r = sb("r", [P, TILES, D])
        ln = sb("ln", [P, TILES, D]); cn = sb("cn", [P, TILES, D]); x5 = sb("x5", [P, TILES, D]); r5 = sb("r5", [P, TILES, D])
        latT = sb("latT", [P, GTOK])
        pen, x4, kvT, kvN, qh = ([sb(f"{n}{q}", shape) for q in range(2)] for n, shape in (
            ("pen", [P, GB, S]), ("x4_", [P, TILES, D]), ("kvT", [P, GB, 2, S]), ("kvN", [P, GB, D]), ("qh", [P, XP, GB, 2, S])))
        CN, X4, LN, X5 = range(4)
        st = sb("st", [P, 4, TILES, 6]); mv = sb("mv", [P, 4, TILES, 2]); ve = sb("ve", [P, 4, TILES]); rs = sb("rs", [P, 4, TILES])
        e = sb("e", [P, 2, XP, KEYS]); nm = sb("nm", [P, 2, XP]); den = sb("den", [P, 2, XP]); rd = sb("rd", [P, 2, XP])
        en = sb("en", [P, 2, XP, KEYS]); pT = sb("pT", [P, 2, XP, P]); gh = sb("gh", [P, XH, GB, S])
        pw = pb("pw", [P, 2, 512]); sc = pb("sc", [P, 2, 512]); tp = pb("tp", [P, XP, P]); pg = pb("pg", [P, 2, 512])
        yy = pb("yy", [P, TILES, D])

        s_const = sem("const"); s_set = sem("set"); s_w = sem("w_psum"); s_wc = sem("w"); s_gg = sem("gg")
        s_in = sem("loaded"); s_infree = sem("in_free"); s_pen = sem("pen")
        s_zz = sem("zz"); s_zTp = sem("zT_psum"); s_zT = sem("zT"); s_y = sem("y_psum"); s_r = sem("r"); s_dv = sem("dve_step"); s_turn = sem("turn")
        s_var = [sem(f"var{k}") for k in range(4)]; s_rstd = [sem(f"rstd{k}") for k in range(4)]
        s_x4 = sem("x4"); s_ln = sem("ln"); s_cn = sem("cn")
        s_lp = sem("lat_psum"); s_lT = sem("latT"); s_cp = sem("ctx_psum"); s_kc = sem("kvT_ctx"); s_kl = sem("kvT_lat")
        s_kp = sem("kv_psum"); s_kvN = sem("kvN")
        s_qp = sem("q_psum"); s_qa = sem("q_even"); s_qd = sem("q_odd")
        s_sc = sem("scores"); s_nm = sem("rowmax"); s_exp = sem("exp"); s_rd = sem("rden"); s_en = sem("normalised")
        s_tp = sem("pT_psum"); s_pT = sem("pT"); s_g = sem("g_psum"); s_gh = sem("gh"); s_o = sem("o_psum"); s_r5 = sem("r5"); s_x5 = sem("x5"); s_st = sem("stored")
        s_mxp = sem("masked")
        block = ctx.enter_context(nc.Block())
        y_g = d["s_y"].rearrange("(g t q) s d -> g (q s) t d", t=TILES, q=2)
        c_g = d["ctx"].rearrange("(g t q) s d -> g (q s) t d", t=TILES, q=2)
        m_g = d["mask"].rearrange("(o g b) s -> g o b s", o=1, b=GB)
        loads = [(wo[:, :], d["l1_wo"]), (bo[:, :], d["l1_bo"].broadcast_to((P, D))), (wqT[:, :, :], d["x_wqT"]),
                 (wkT[:, :, :], d["x_wkT"]), (wvT[:, :, :], d["x_wvT"]), (wout[:, :, :], d["x_wout"]),
                 (par[:, 0:4], d["x_par"]), (par[:, 4:5], d["x_gate"].broadcast_to((P, 1)))]
        NCONST = 16 * len(loads)
        NLN = 4

        PAIRS = GROUPS // 2

        def schedule(eng, unit):
            with eng.Fori(0, PAIRS - 1) as i:
                unit(i * 2, 0, True)
                unit(i * 2 + 1, 1, True)
            unit(GROUPS - 2, 0, True)
            unit(GROUPS - 1, 1, False)

        @block.sync
        def _(sp):
            for dst, src in loads:
                sp.dma_start(dst, src).then_inc(s_const, 16)

            def load(g):
                sp.wait_ge(s_infree, g + 1)
                sp.dma_start(yi[:, :, :], y_g[g]).then_inc(s_in, 16)
                sp.dma_start(gi[:, :, :], d["s_gate"][g]).then_inc(s_in, 16)
                sp.dma_start(xi[:, :, :], d["s_x3"][g]).then_inc(s_in, 16)
                sp.dma_start(ci[:, :, :], c_g[g]).then_inc(s_in, 16)
                sp.dma_start(mi[:, :, :], m_g[g].broadcast_to((P, GB, S))).then_inc(s_in, 16)

            def store(g):
                sp.wait_ge(s_x5, g + 1)
                sp.dma_start(d["s_x5"][g], x5[:, :, :]).then_inc(s_st, 16)

            load(0)
            load(1)
            with sp.Fori(0, GROUPS - 2) as g:
                store(g)
                load(g + 2)
            store(GROUPS - 2)
            store(GROUPS - 1)
            sp.wait_ge(s_st, GROUPS * 16 + 1)

        @block.tensor
        def _(pe):
            pe.wait_ge(s_const, NCONST)
            for c in range(4):
                a, b = ((wqT, wkT), (wvT, wout))[c // 2]
                if c >= 2:
                    pe.wait_ge(s_wc, c - 1)
                for h in range(4):
                    hh = 4 * (c % 2) + h
                    m = pe.matmul(pw[:, c % 2, h * D:(h + 1) * D], a[:, hh, :], b[:, hh, :], start=True, stop=True)
                m.then_inc(s_w, 1)
            pe.wait_ge(s_wc, 4)

            def flat(x):
                return x.rearrange("p a s -> p (a s)")

            def gated(g):
                pe.wait_ge(s_zz, g + 1)
                pe.wait_ge(s_qa, g * XP + 1)
                for t in range(TILES):
                    m = pe.transpose(pw[:, 0, t * P:(t + 1) * P], zz[:, t, :], ident[:, :])
                m.then_inc(s_zTp, 1)

            def project(g):
                pe.wait_ge(s_zT, g + 1)
                pe.wait_ge(s_qd, g * XP + 1)
                for t in range(TILES):
                    m = pe.matmul(pw[:, 1, t * P:(t + 1) * P], zT[:, t * P:(t + 1) * P], wo[:, :], start=True, stop=True)
                m.then_inc(s_y, 1)

            def context(g):
                pe.wait_ge(s_cn, g + 1)
                for t in range(TILES):
                    m = pe.transpose(pw[:, 0, t * P:(t + 1) * P], cn[:, t, :], ident[:, :])
                m.then_inc(s_cp, 1)

            def latents(g):
                pe.wait_ge(s_ln, g + 1)
                pe.wait_ge(s_r, g + 1)
                for t in range(TILES):
                    m = pe.transpose(pw[:, 1, t * P:(t + 1) * P], ln[:, t, :], ident[:, :])
                m.then_inc(s_lp, 1)

            def keys(g, q):
                pe.wait_ge(s_kc, g + 1)
                pe.wait_ge(s_kl, g + 1)
                for b in range(GB):
                    m = pe.transpose(pw[:, b // 4, (b % 4) * P:(b % 4 + 1) * P], flat(kvT[q][:, b, :, :]), ident[:, :])
                m.then_inc(s_kp, 1)

            def queries(g, h):
                if h == 0:
                    pe.wait_ge(s_kvN, g + 1)
                    pe.wait_ge(s_lT, g + 1)
                if h >= 2:
                    pe.wait_ge(s_qa if h % 2 == 0 else s_qd, g * XP + h // 2 + 1)
                pe.matmul(pw[:, h % 2, :], qk[:, h, :], latT[:, :], start=True, stop=True).then_inc(s_qp, 1)

            def scores(g, q, b):
                if b == 0:
                    pe.wait_ge(s_qa, g * XP + XP + 1)
                    pe.wait_ge(s_qd, g * XP + XP + 1)
                pe.wait_ge(s_exp, g * GB + b + 1)
                for j in range(XP):
                    m = pe.matmul(sc[:, b % 2, j * KEYS:(j + 1) * KEYS], flat(qh[q][:, j, b, :, :]),
                                  flat(kvT[q][:, b, :, :]), start=True, stop=True)
                m.then_inc(s_sc, 1)

            def transposes(g, b):
                pe.wait_ge(s_en, g * GB + b + 3)
                pe.wait_ge(s_pT, g * GB + b + 1)
                for j in range(XP):
                    m = pe.transpose(tp[:, j, :], en[:, b % 2, j, :], ident[:, :])
                m.then_inc(s_tp, 1)

            def weighted(g, q, b):
                pe.wait_ge(s_pT, g * GB + b + 2)
                pe.wait_ge(s_gh, g * GB + b + 1)
                pe.matmul(pg[:, b % 2, :], kvN[q][:, b, :], pT[:, b % 2, :, :], start=True, stop=True).then_inc(s_g, 1)

            def back(g):
                pe.wait_ge(s_gh, g * GB + GB + 2)
                pe.wait_ge(s_r5, g + 1)
                for t in range(TILES):
                    for h in range(XH):
                        m = pe.matmul(yy[:, t, :], flat(gh[:, h, 2 * t:2 * t + 2, :]), vo[:, h, :],
                                      start=(h == 0), stop=(h == XH - 1))
                m.then_inc(s_o, 1)

            def unit(g, q, following):
                for b in range(GB):
                    transposes(g, b)
                    if b + 2 < GB:
                        scores(g, q, b + 2)
                    weighted(g, q, b)
                    if following:
                        if b == 0:
                            gated(g + 1)
                        if b == 1:
                            project(g + 1)
                        if b == 3:
                            context(g + 1)
                        if b == 5:
                            latents(g + 1)
                        if b == 6:
                            keys(g + 1, 1 - q)
                            queries(g + 1, 0)
                            queries(g + 1, 1)
                if following:
                    for h in range(2, XH):
                        queries(g + 1, h)
                    scores(g + 1, 1 - q, 0)
                    scores(g + 1, 1 - q, 1)
                back(g)

            gated(0)
            project(0)
            context(0)
            latents(0)
            keys(0, 0)
            for h in range(XH):
                queries(0, h)
            scores(0, 0, 0)
            scores(0, 0, 1)
            schedule(pe, unit)

        @block.scalar
        def _(act):
            act.wait_ge(s_const, NCONST)
            act.wait_ge(s_set, 1)
            for c in range(4):
                dst = (qk, vo)[c // 2]
                act.wait_ge(s_w, c + 1)
                act.activation(dst[:, 4 * (c % 2):4 * (c % 2) + 4, :], pw[:, c % 2, :], ACT.Copy,
                               scale=XSCALE if c < 2 else 1.0).then_inc(s_wc, 1)
            act.sem_inc(s_pT, 1)
            act.sem_inc(s_gh, 2)
            act.sem_inc(s_exp, 2)
            act.sem_inc(s_qa, 1)

            def by_seq(x):
                return x.rearrange("p (b s) -> p b s", s=S)

            def gated(g):
                act.wait_ge(s_zTp, g + 1)
                act.activation(zT[:, :], pw[:, 0, :], ACT.Copy).then_inc(s_zT, 1)

            def context(g, q):
                act.wait_ge(s_cp, g + 1)
                act.activation(kvT[q][:, :, 0, :], by_seq(pw[:, 0, :]), ACT.Identity,
                               bias=par[:, 1:2], scale=par[:, 0:1]).then_inc(s_kc, 1)

            def latents(g, q):
                act.wait_ge(s_lp, g + 1)
                act.activation(latT[:, :], pw[:, 1, :], ACT.Identity, bias=par[:, 3:4], scale=par[:, 2:3]).then_inc(s_lT, 1)
                act.wait_ge(s_gg, 1)
                act.activation(kvT[q][:, :, 1, :], by_seq(pw[:, 1, :]), ACT.Identity,
                               bias=gg[:, 1:2], scale=gg[:, 0:1]).then_inc(s_kl, 1)

            def keys(g, q):
                act.wait_ge(s_kp, g + 1)
                act.activation(kvN[q].rearrange("p b n -> p (b n)"), pw.rearrange("p a n -> p (a n)"), ACT.Copy).then_inc(s_kvN, 1)

            def queries(g, q, j):
                act.wait_ge(s_qp, g * XH + 2 * j + 1)
                act.activation(qh[q][:, j, :, 0, :], by_seq(pw[:, 0, :]), ACT.Copy).then_inc(s_qa, 1)

            def exps(g, b):
                act.wait_ge(s_nm, g * GB + b + 1)
                act.wait_ge(s_en, g * GB + b + 1)
                for j in range(XP):
                    m = act.activation(e[:, b % 2, j, :], sc[:, b % 2, j * KEYS:(j + 1) * KEYS], ACT.Exp,
                                       bias=nm[:, b % 2, j:j + 1], accum_out=den[:, b % 2, j:j + 1])
                m.then_inc(s_exp, 1)

            def evacuate(g, b):
                act.wait_ge(s_tp, g * GB + b + 3)
                act.wait_ge(s_g, g * GB + b + 1)
                act.activation(pT[:, b % 2, :, :], tp[:, :, :], ACT.Copy).then_inc(s_pT, 1)
                act.wait_ge(s_g, g * GB + b + 3)
                if b == 0:
                    act.wait_ge(s_o, g + 1)
                act.activation(gh[:, :, b, :], pg[:, b % 2, :].rearrange("p (h s) -> p h s", s=S), ACT.Copy).then_inc(s_gh, 1)

            def unit(g, q, following):
                for b in range(GB):
                    if b + 1 < GB:
                        exps(g, b + 1)
                    evacuate(g, b)
                    if following:
                        if b == 0:
                            gated(g + 1)
                        if b == 3:
                            context(g + 1, 1 - q)
                        if b == 5:
                            latents(g + 1, 1 - q)
                        if b == 6:
                            keys(g + 1, 1 - q)
                            queries(g + 1, 1 - q, 0)
                if following:
                    for j in range(1, XP):
                        queries(g + 1, 1 - q, j)
                    exps(g + 1, 0)

            act.sem_inc(s_g, 2)
            act.sem_inc(s_o, 1)
            gated(0)
            context(0, 0)
            latents(0, 0)
            keys(0, 0)
            for j in range(XP):
                queries(0, 0, j)
            exps(0, 0)
            schedule(act, unit)

        @block.gpsimd
        def _(pool):
            pool.memset(neghalf[:, :], -0.5).then_inc(s_set, 1)
            pool.wait_ge(s_set, 1)

            def root(g, k):
                pool.wait_ge(s_var[k], g + 1)
                pool.tensor_tensor(rs[:, k, :], ve[:, k, :], neghalf[:, :], ALU.pow).then_inc(s_rstd[k], 1)

            for k in (CN, X4, LN):
                root(0, k)
            with pool.Fori(0, GROUPS - 1) as g:
                for k in (CN, X4, LN):
                    root(g + 1, k)
                root(g, X5)
            root(GROUPS - 1, X5)

        @block.vector
        def _(v):
            v.wait_ge(s_const, NCONST)
            v.tensor_scalar(gg[:, :], par[:, 2:4], par[:, 4:5], None, ALU.mult).then_inc(s_gg, 1)
            v.sem_inc(s_infree, 1)
            v.sem_inc(s_st, 1)
            v.sem_inc(s_qd, 1)
            v.sem_inc(s_r5, 1)
            v.sem_inc(s_en, 2)
            v.sem_inc(s_tp, 2)
            STEPS = 16
            n = [0, 0]

            def link(ins):
                n[1] += 1
                assert n[1] <= STEPS
                ins.then_inc(s_dv, 1)
                v.wait_ge(s_dv, (n[0] + 1) * STEPS + n[1])

            def close():
                if n[1] < STEPS:
                    v.sem_inc(s_dv, STEPS - n[1])

            def stats(src, k):
                for t in range(TILES):
                    m = v.bn_stats(st[:, k, t, :], src[:, t, :])
                link(m)
                v.sem_inc(s_turn, 1)
                for t in range(TILES):
                    m = v.bn_aggr(mv[:, k, t, :], st[:, k, t, :])
                link(m)
                v.tensor_scalar(ve[:, k, :], mv[:, k, :, 1], LN_EPS, None, ALU.add).then_inc(s_var[k], 1)

            def norm(g, dst, src, k):
                v.wait_ge(s_rstd[k], g + 1)
                for t in range(TILES):
                    m = v.tensor_scalar(dst[:, t, :], src[:, t, :], mv[:, k, t, 0:1], rs[:, k, t:t + 1], ALU.subtract, ALU.mult)
                return m

            def enter(g, q):
                v.wait_ge(s_in, g * 80 + 80)
                v.tensor_tensor(zz[:, :, :], yi[:, :, :], gi[:, :, :], ALU.mult).then_inc(s_zz, 1)
                v.tensor_scalar(pen[q][:, :, :], mi[:, :, :], MASKED, None, ALU.mult).then_inc(s_pen, 1)
                v.tensor_tensor(xb[:, :, :], xi[:, :, :], bo.rearrange("p (o n) -> p o n", o=1).broadcast_to((P, TILES, D)), ALU.add)

            def residual(g):
                v.wait_ge(s_y, g + 1)
                m = v.tensor_tensor(r[:, :, :], pw[:, 1, :].rearrange("p (t n) -> p t n", t=TILES), xb[:, :, :], ALU.add)
                m.then_inc(s_r, 1)
                v.wait_ge(s_r, g + 1)
                stats(r, X4)

            def rowmax(g, q, b):
                v.wait_ge(s_sc, g * GB + b + 1)
                if b == 0:
                    v.wait_ge(s_pen, g + 1)
                s3 = sc[:, b % 2, :].rearrange("p (j k) -> p j k", j=XP)
                v.tensor_tensor(s3[:, :, 0:S], s3[:, :, 0:S],
                                pen[q][:, b:b + 1, :].broadcast_to((P, XP, S)), ALU.add).then_inc(s_mxp, 1)
                v.wait_ge(s_mxp, g * GB + b + 1)
                v.wait_ge(s_exp, g * GB + b + 1)
                v.tensor_reduce(nm[:, b % 2, :], s3, AX.X, ALU.max, negate=True).then_inc(s_nm, 1)

            def normalise(g, b):
                v.wait_ge(s_exp, g * GB + b + 3)
                v.reciprocal(rd[:, b % 2, :], den[:, b % 2, :]).then_inc(s_rd, 1)
                v.wait_ge(s_rd, g * GB + b + 1)
                v.wait_ge(s_tp, g * GB + b + 1)
                v.tensor_tensor(en[:, b % 2, :, :], e[:, b % 2, :, :],
                                rd[:, b % 2, :].rearrange("p (j o) -> p j o", o=1).broadcast_to((P, XP, KEYS)),
                                ALU.mult).then_inc(s_en, 1)

            def queries(g, q, j):
                v.wait_ge(s_qp, g * XH + 2 * j + 2)
                v.tensor_copy(qh[q][:, j, :, 1, :], pw[:, 1, :].rearrange("p (b s) -> p b s", s=S)).then_inc(s_qd, 1)

            def back_stats(g, q):
                v.wait_ge(s_o, g + 2)
                v.tensor_tensor(r5[:, :, :], yy[:, :, :], x4[q][:, :, :], ALU.add).then_inc(s_r5, 1)
                v.wait_ge(s_r5, g + 2)
                stats(r5, X5)

            def back_norm(g):
                v.wait_ge(s_st, g * 16 + 1)
                norm(g, x5, r5, X5).then_inc(s_x5, 1)

            def front(g, q, b):
                if b == 0:
                    enter(g, q)
                if b == 1:
                    stats(ci, CN)
                if b == 2:
                    norm(g, cn, ci, CN).then_inc(s_cn, 1)
                    residual(g)
                    v.wait_ge(s_cn, g + 1)
                    v.sem_inc(s_infree, 1)
                if b == 3:
                    link(norm(g, x4[q], r, X4))
                    stats(x4[q], LN)
                if b == 4:
                    norm(g, ln, x4[q], LN).then_inc(s_ln, 1)
                if b == 6:
                    queries(g, q, 0)

            def unit(g, q, following):
                n[0], n[1] = g, 0
                for b in range(GB):
                    if b + 1 < GB:
                        rowmax(g, q, b + 1)
                    normalise(g, b)
                    if following:
                        front(g + 1, 1 - q, b)
                if following:
                    for j in range(1, XP):
                        queries(g + 1, 1 - q, j)
                    rowmax(g + 1, 1 - q, 0)
                back_stats(g, q)
                back_norm(g)
                close()

            n[0], n[1] = -1, 0
            for b in range(GB):
                front(0, 0, b)
            for j in range(1, XP):
                queries(0, 0, j)
            close()
            rowmax(0, 0, 0)
            schedule(v, unit)


E8, FF = 8, 256
EC = FF // P
NG4, NL = 4, 2
LOOPS = 2
RMS_EPS, TOP_EPS = 1e-6, 1e-9


def experts(nc, d, keep):
    ident = keep["ident"]
    with ExitStack() as ctx:
        def sb(name, shape, dt=F32):
            return ctx.enter_context(nc.sbuf_tensor("G_" + name, shape, dt))

        def pb(name, shape, dt=F32):
            return ctx.enter_context(nc.psum_tensor("G_" + name, shape, dt))

        sem = stage_semaphores(nc, ctx, "G_")

        w1 = sb("w1", [P, E8 * EC, P]); w2 = sb("w2", [P, E8 * EC, D]); wr = sb("wr", [P, NG4 + E8]); nw = sb("nw", [P, 1])
        neghalf = sb("neghalf", [P, TILES]); tri = sb("tri", [P, NG4, NG4])
        xin = [sb(f"xin{g}", [P, TILES, D]) for g in range(2)]; z = [sb(f"z{g}", [P, TILES, D]) for g in range(2)]
        zn = sb("zn", [P, TILES, D]); acc = sb("acc", [P, TILES, D]); r = sb("r", [P, TILES, D]); junk = sb("junk", [P, TILES, D])
        ss = sb("ss", [P, TILES]); ve = sb("ve", [P, TILES]); rs = sb("rs", [P, TILES]); vt = sb("vt", [P, TILES]); rt = sb("rt", [P, TILES])
        st = sb("st", [P, TILES, 6]); mv = sb("mv", [P, TILES, 2]); out = sb("out", [P, TILES, D])
        znT = [sb(f"znT{g}", [P, GTOK]) for g in range(2)]; hT = sb("hT", [P, E8 * EC, GTOK])
        lg = sb("lg", [P, TILES, 12]); ex = sb("ex", [P, TILES, 12]); pr = sb("pr", [P, TILES, 12])
        t4 = sb("t4", [P, 8, TILES, NG4]); t1 = sb("t1", [P, 4, TILES]); cmp = sb("cmp", [P, TILES, NG4, NG4])
        ceq = sb("ceq", [P, TILES, NG4, NG4]); s1 = sb("s1", [P, TILES, NG4, NL]); comb = [sb(f"comb{g}", [P, TILES, E8]) for g in range(2)]
        px = pb("px", [P, 2, 512]); ph = pb("ph", [P, 4, 512]); py = pb("py", [P, 2, TILES, D])

        s_const = sem("const"); s_set = sem("set")
        s_x = [sem(f"x{g}_loaded") for g in range(2)]; s_xfree = [sem(f"x{g}_free") for g in range(2)]
        s_z = sem("z"); s_sq = sem("sq"); s_var = sem("var"); s_rstd = sem("rstd"); s_vt = sem("tail_var"); s_rt = sem("tail_rstd")
        s_zn = sem("zn"); s_znp = sem("zn_psum"); s_znT = sem("znT")
        s_lg = sem("logits"); s_sub = sem("sub"); s_ex = sem("ex"); s_h = sem("h_psum"); s_hT = sem("hT")
        s_y = sem("y_psum"); s_acc = sem("acc")
        s_dv = sem("dve_step"); s_turn = sem("turn"); s_out = sem("out"); s_st = sem("stored")
        block = ctx.enter_context(nc.Block())
        o_g = d["out"].rearrange("(g t q) s d -> g (q s) t d", t=TILES, q=2)
        loads = [(w1[:, :, :], d["m_w1"]), (w2[:, :, :], d["m_w2"]), (wr[:, :], d["m_wr"]), (nw[:, :], d["m_nw"])]
        NCONST = 16 * len(loads)
        NC = E8 * EC
        PAIRS = GROUPS // 2
        AHEAD = 4

        def schedule(eng, one_pass):
            one_pass(0, 0, False, True, 0)
            with eng.Fori(0, PAIRS - 1) as i:
                for p in (1, 2, 3, 4):
                    one_pass(i * 4 + p, p % 4, p >= 3, True, i * 2 + (p - 3))
            i = PAIRS - 1
            for p in (1, 2, 3):
                one_pass(i * 4 + p, p, p == 3, p < 3, i * 2)

        @block.sync
        def _(sp):
            for dst, src in loads:
                sp.dma_start(dst, src).then_inc(s_const, 16)
            for g in range(2):
                sp.dma_start(xin[g][:, :, :], d["s_x5"][g]).then_inc(s_x[g], 16)
            with sp.Fori(0, PAIRS - 1) as i:
                for g in range(2):
                    sp.wait_ge(s_xfree[g], i + 1)
                    sp.dma_start(xin[g][:, :, :], d["s_x5"][i * 2 + 2 + g]).then_inc(s_x[g], 16)
                    sp.wait_ge(s_out, i * 2 + g + 1)
                    sp.dma_start(o_g[i * 2 + g], out[:, :, :]).then_inc(s_st, 16)
            for g in range(2):
                sp.wait_ge(s_out, GROUPS - 1 + g)
                sp.dma_start(o_g[GROUPS - 2 + g], out[:, :, :]).then_inc(s_st, 16)
            sp.wait_ge(s_st, GROUPS * 16 + 1)

        @block.tensor
        def _(pe):
            pe.wait_ge(s_const, NCONST)

            def transposes(k):
                pe.wait_ge(s_zn, k + 1)
                for t in range(TILES):
                    m = pe.transpose(px[:, 0, t * P:(t + 1) * P], zn[:, t, :], ident[:, :])
                m.then_inc(s_znp, 1)

            def logits(k, q):
                pe.wait_ge(s_znT, k + 1)
                for t in range(TILES):
                    m = pe.matmul(px[:, 1, 12 * t:12 * t + 12], znT[q][:, t * P:(t + 1) * P], wr[:, :], start=True, stop=True)
                m.then_inc(s_lg, 1)

            def up(k, q, c):
                pe.wait_ge(s_hT, k * NC + c + 1)
                pe.matmul(ph[:, c % 4, :], w1[:, c, :], znT[q][:, :],
                          start=True, stop=True).then_inc(s_h, 1)

            def down(k, ee):
                pe.wait_ge(s_hT, k * NC + 2 * ee + 2 + AHEAD)
                pe.wait_ge(s_acc, k * E8 + ee + 1)
                for t in range(TILES):
                    for f in range(EC):
                        m = pe.matmul(py[:, ee % 2, t, :], hT[:, 2 * ee + f, t * P:(t + 1) * P], w2[:, 2 * ee + f, :],
                                      start=(f == 0), stop=(f == EC - 1))
                m.then_inc(s_y, 1)

            def one_pass(k, p, tail, following, g):
                q = p % 2
                for c in range(AHEAD, NC + 4):
                    if c < NC:
                        up(k, q, c)
                    elif following and c - NC < AHEAD:
                        up(k + 1, 1 - q, c - NC)
                    if c >= 5 and c % 2 == 1:
                        ee = (c - 5) // 2
                        down(k, ee)
                        if following and ee == 3 + tail:
                            transposes(k + 1)
                        if following and ee == 4 + tail:
                            logits(k + 1, 1 - q)

            transposes(0)
            logits(0, 0)
            for c in range(AHEAD):
                up(0, 0, c)
            schedule(pe, one_pass)

        @block.scalar
        def _(act):
            act.wait_ge(s_const, NCONST)
            act.sem_inc(s_hT, AHEAD)
            act.sem_inc(s_y, E8)

            def squares(k, q):
                act.wait_ge(s_z, k + 1)
                for t in range(TILES):
                    m = act.activation(junk[:, t, :], z[q][:, t, :], ACT.Square, accum_out=ss[:, t:t + 1])
                m.then_inc(s_sq, 1)

            def evacuate(k, q):
                act.wait_ge(s_znp, k + 1)
                act.activation(znT[q][:, :], px[:, 0, :], ACT.Copy, scale=nw[:, :]).then_inc(s_znT, 1)

            def exponentials(k):
                act.wait_ge(s_sub, k + 1)
                act.activation(ex[:, :, :], lg[:, :, :], ACT.Exp).then_inc(s_ex, 1)

            def one_pass(k, p, tail, following, g):
                q = p % 2
                for c in range(NC):
                    act.wait_ge(s_h, k * NC + c + 1)
                    if c % 2 == 0:
                        act.wait_ge(s_y, k * E8 + c // 2 + 1)
                    act.activation(hT[:, c, :], ph[:, c % 4, :], ACT.Silu).then_inc(s_hT, 1)
                    if following and c == 6 + 2 * tail:
                        squares(k + 1, 1 - q)
                    if following and c == 12 + 2 * tail:
                        evacuate(k + 1, 1 - q)
                if following:
                    exponentials(k + 1)

            squares(0, 0)
            evacuate(0, 0)
            exponentials(0)
            schedule(act, one_pass)

        @block.gpsimd
        def _(pool):
            pool.memset(neghalf[:, :], -0.5).then_inc(s_set, 1)
            pool.memset(tri[:, :, :], 0.0).then_inc(s_set, 1)
            pool.wait_ge(s_set, 2)
            for g in range(1, NG4):
                pool.memset(tri[:, g, 0:g], 1.0).then_inc(s_set, 1)

            def head(k):
                pool.wait_ge(s_var, k + 1)
                pool.tensor_tensor(rs[:, :], ve[:, :], neghalf[:, :], ALU.pow).then_inc(s_rstd, 1)

            def tail_root(g):
                pool.wait_ge(s_vt, g + 1)
                pool.tensor_tensor(rt[:, :], vt[:, :], neghalf[:, :], ALU.pow).then_inc(s_rt, 1)

            def one_pass(k, p, tail, following, g):
                if tail:
                    tail_root(g)
                if following:
                    head(k + 1)

            head(0)
            schedule(pool, one_pass)
            tail_root(GROUPS - 1)

        @block.vector
        def _(v):
            v.wait_ge(s_const, NCONST)
            v.wait_ge(s_set, 2 + NG4 - 1)
            v.sem_inc(s_acc, 2)
            v.sem_inc(s_st, 1)
            STEPS = 20
            n = [0, 0]

            def link(ins):
                n[1] += 1
                assert n[1] <= STEPS
                ins.then_inc(s_dv, 1)
                v.wait_ge(s_dv, (n[0] + 1) * STEPS + n[1])

            def close():
                if n[1] < STEPS:
                    v.sem_inc(s_dv, STEPS - n[1])

            def b4(x):
                return x.rearrange("p (t o) -> p t o", o=1).broadcast_to((P, TILES, NG4))

            def take(k, q, loop, at):
                if loop == 0:
                    v.wait_ge(s_x[q], at)
                    v.tensor_copy(z[q][:, :, :], xin[q][:, :, :]).then_inc(s_z, 1)
                else:
                    v.sem_inc(s_z, 1)

            def variance(k):
                v.wait_ge(s_sq, k + 1)
                v.tensor_scalar(ve[:, :], ss[:, :], 1.0 / D, RMS_EPS, ALU.mult, ALU.add).then_inc(s_var, 1)

            def scaled(k, q):
                v.wait_ge(s_rstd, k + 1)
                v.wait_ge(s_z, k + 1)
                for t in range(TILES):
                    m = v.tensor_scalar(zn[:, t, :], z[q][:, t, :], rs[:, t:t + 1], None, ALU.mult)
                m.then_inc(s_zn, 1)

            def shifted(k):
                v.wait_ge(s_lg, k + 1)
                raw = px[:, 1, 0:TILES * 12].rearrange("p (t n) -> p t n", t=TILES)
                v.tensor_reduce(t1[:, 0, :], raw[:, :, 0:NG4], AX.X, ALU.max)
                link(v.tensor_reduce(t4[:, 0, :, :], raw[:, :, NG4:12].rearrange("p t (g l) -> p t g l", l=NL), AX.X, ALU.max))
                v.tensor_tensor(lg[:, :, 0:NG4], raw[:, :, 0:NG4], b4(t1[:, 0, :]), ALU.subtract)
                v.tensor_tensor(lg[:, :, NG4:12].rearrange("p t (g l) -> p t g l", l=NL),
                                raw[:, :, NG4:12].rearrange("p t (g l) -> p t g l", l=NL),
                                t4[:, 0, :, :].rearrange("p t (g o) -> p t g o", o=1).broadcast_to((P, TILES, NG4, NL)),
                                ALU.subtract).then_inc(s_sub, 1)

            def combine(k, q):
                v.wait_ge(s_ex, k + 1)
                exl = ex[:, :, NG4:12].rearrange("p t (g l) -> p t g l", l=NL)
                prl = pr[:, :, NG4:12].rearrange("p t (g l) -> p t g l", l=NL)
                v.tensor_reduce(t1[:, 1, :], ex[:, :, 0:NG4], AX.X, ALU.add)
                link(v.tensor_reduce(t4[:, 1, :, :], exl, AX.X, ALU.add))
                v.reciprocal(t1[:, 2, :], t1[:, 1, :])
                link(v.reciprocal(t4[:, 2, :, :], t4[:, 1, :, :]))
                v.tensor_tensor(pr[:, :, 0:NG4], ex[:, :, 0:NG4], b4(t1[:, 2, :]), ALU.mult)
                link(v.tensor_tensor(prl, exl, t4[:, 2, :, :].rearrange("p t (g o) -> p t g o", o=1).broadcast_to((P, TILES, NG4, NL)), ALU.mult))
                mine = pr[:, :, 0:NG4].rearrange("p t (g o) -> p t g o", o=1).broadcast_to((P, TILES, NG4, NG4))
                other = pr[:, :, 0:NG4].rearrange("p t (o g) -> p t o g", o=1).broadcast_to((P, TILES, NG4, NG4))
                v.tensor_tensor(cmp[:, :, :, :], other, mine, ALU.is_gt)
                v.tensor_tensor(s1[:, :, :, 1], prl[:, :, :, 1], prl[:, :, :, 0], ALU.is_gt)
                v.tensor_tensor(t4[:, 3, :, :], prl[:, :, :, 0], prl[:, :, :, 1], ALU.max)
                link(v.tensor_tensor(ceq[:, :, :, :], other, mine, ALU.is_equal))
                v.tensor_scalar(s1[:, :, :, 0], s1[:, :, :, 1], -1.0, 1.0, ALU.mult, ALU.add)
                v.tensor_scalar(t4[:, 4, :, :], t4[:, 3, :, :], TOP_EPS, None, ALU.add)
                link(v.tensor_tensor(ceq[:, :, :, :], ceq[:, :, :, :],
                                     tri.rearrange("p (o a) b -> p o a b", o=1).broadcast_to((P, TILES, NG4, NG4)), ALU.mult))
                v.reciprocal(t4[:, 5, :, :], t4[:, 4, :, :])
                link(v.tensor_tensor(cmp[:, :, :, :], cmp[:, :, :, :], ceq[:, :, :, :], ALU.add))
                v.tensor_tensor(t4[:, 6, :, :], t4[:, 3, :, :], t4[:, 5, :, :], ALU.mult)
                link(v.tensor_reduce(t4[:, 7, :, :], cmp[:, :, :, :], AX.X, ALU.add))
                link(v.tensor_scalar(t4[:, 7, :, :], t4[:, 7, :, :], 2.0, None, ALU.is_lt))
                link(v.tensor_tensor(t4[:, 7, :, :], t4[:, 7, :, :], pr[:, :, 0:NG4], ALU.mult))
                link(v.tensor_reduce(t1[:, 3, :], t4[:, 7, :, :], AX.X, ALU.add))
                link(v.tensor_scalar(t1[:, 3, :], t1[:, 3, :], TOP_EPS, None, ALU.add))
                link(v.reciprocal(t1[:, 0, :], t1[:, 3, :]))
                link(v.tensor_tensor(t4[:, 0, :, :], t4[:, 7, :, :], b4(t1[:, 0, :]), ALU.mult))
                link(v.tensor_tensor(t4[:, 0, :, :], t4[:, 0, :, :], t4[:, 6, :, :], ALU.mult))
                link(v.tensor_tensor(comb[q].rearrange("p t (g l) -> p t g l", l=NL), s1[:, :, :, :],
                                     t4[:, 0, :, :].rearrange("p t (g o) -> p t g o", o=1).broadcast_to((P, TILES, NG4, NL)), ALU.mult))

            def gather(k, q, ee):
                v.wait_ge(s_y, k * E8 + ee + 1 + E8)
                if ee:
                    v.wait_ge(s_acc, k * E8 + ee + 2)
                for t in range(TILES):
                    base = z[q] if ee == 0 else acc
                    dst = z[q] if ee == E8 - 1 else acc
                    m = v.scalar_tensor_tensor(dst[:, t, :], py[:, ee % 2, t, :], comb[q][:, t, ee:ee + 1], base[:, t, :],
                                               ALU.mult, ALU.add)
                m.then_inc(s_acc, 1)

            def tail_stats(q):
                link(v.tensor_tensor(r[:, :, :], z[q][:, :, :], xin[q][:, :, :], ALU.add))
                v.sem_inc(s_xfree[q], 1)
                for t in range(TILES):
                    m = v.bn_stats(st[:, t, :], r[:, t, :])
                link(m)
                v.sem_inc(s_turn, 1)
                for t in range(TILES):
                    m = v.bn_aggr(mv[:, t, :], st[:, t, :])
                link(m)
                v.tensor_scalar(vt[:, :], mv[:, :, 1], LN_EPS, None, ALU.add).then_inc(s_vt, 1)

            def tail_norm(g):
                v.wait_ge(s_rt, g + 1)
                v.wait_ge(s_st, g * 16 + 1)
                for t in range(TILES):
                    m = v.tensor_scalar(out[:, t, :], r[:, t, :], mv[:, t, 0:1], rt[:, t:t + 1], ALU.subtract, ALU.mult)
                m.then_inc(s_out, 1)

            def one_pass(k, p, tail, following, g):
                q = p % 2
                n[0], n[1] = k, 0
                nxt_loop = ((p + 1) % 4) // 2
                for ee in range(E8):
                    gather(k, q, ee)
                    if tail and ee == 0:
                        tail_stats(1 - q)
                    if tail and ee == 1:
                        tail_norm(g)
                    if following and ee == 1 + tail:
                        take(k + 1, 1 - q, nxt_loop, k * 4 + (16 if p == 0 else 20))
                    if following and ee == 2 + tail:
                        variance(k + 1)
                    if following and ee == 3 + tail:
                        scaled(k + 1, 1 - q)
                    if following and ee == 5 + tail:
                        shifted(k + 1)
                    if following and ee == 7:
                        combine(k + 1, 1 - q)
                v.wait_ge(s_acc, k * E8 + E8 + 2)
                close()

            def head(k, q, at):
                n[0], n[1] = -1, 0
                take(k, q, 0, at)
                variance(k)
                scaled(k, q)
                shifted(k)
                combine(k, q)

            head(0, 0, 16)
            close()
            schedule(v, one_pass)
            n[0], n[1] = 4 * PAIRS, 0
            tail_stats(1)
            tail_norm(GROUPS - 1)


SCRATCH = [P, TILES, D]


def decoder(nc, d):
    for name in ("s_x2", "s_f1", "s_x3", "s_gate", "s_x5"):
        d[name] = nc.dram_tensor(name, [GROUPS] + SCRATCH, F32, kind="Internal").ap()
    d["s_rows"] = nc.dram_tensor("s_rows", [B, S, TW], F32, kind="Internal").ap()
    d["s_y"] = nc.dram_tensor("s_y", [B, S, D], F32, kind="Internal").ap()
    with ExitStack() as ctx:
        ident = ctx.enter_context(nc.sbuf_tensor("ident", [P, P], F32))
        keep = {"ident": ident, "novelty": NOVELTY}
        ident_loaded = ctx.enter_context(nc.semaphore("ident_loaded"))
        with nc.Block() as block:
            @block.sync
            def _(sp):
                sp.dma_start(ident[:, :], d["ident"]).then_inc(ident_loaded, 16)
                sp.wait_ge(ident_loaded, 16)
        with ExitStack() as ffn:
            for name, shape, dt in (("pooledT", [P, B], F32), ("go", [1, 1], I32), ("mask", [P, FULL], F32),
                                    ("maskT", [P, FCH, P], F32)):
                keep[name] = ffn.enter_context(nc.sbuf_tensor(name, shape, dt))
            self_attention_and_ffn(nc, d, keep)
            route(nc, d, keep, True, False)
            route(nc, d, keep, True, True)
            route(nc, d, keep, False, True)
        delta_inputs(nc, d, keep)
        delta_scan(nc, d, keep)
        latent_attention(nc, d, keep)
        experts(nc, d, keep)


def layouts(x, ctx_1024, mask_BxS2_bk0, **w):
    p = np.arange(P)
    lag = p[None, :] - p[:, None]
    same = p[None, :] // S == p[:, None] // S
    qkv = w["L0_attn_W_qkv"].reshape(H, 3, DH, D)
    bqkv = w["L0_attn_b_qkv"].reshape(H, 3, DH)
    a = {
        "x": x, "ctx": ctx_1024, "mask": mask_BxS2_bk0,
        "ident": np.eye(P, dtype=np.float32),
        "headmask": ((p[:, None] % 64) // DH == np.arange(8)[None]).astype(np.float32),
        "decayT": np.where((lag >= 0) & same, 0.9 ** np.maximum(lag, 0), 0.0).astype(np.float32),
        "meanw": np.where(p[:, None] // S == np.arange(2)[None], 1.0 / S, 0.0).astype(np.float32),
        "a0_wqT": qkv[:, 0].reshape(D, D).T, "a0_wkT": qkv[:, 1].reshape(D, D).T, "a0_wvT": qkv[:, 2].reshape(D, D).T,
        "a0_bq": bqkv[:, 0].reshape(D, 1), "a0_bk": bqkv[:, 1].reshape(D, 1), "a0_bv": bqkv[:, 2].reshape(1, D),
        "a0_woT": w["L0_attn_W_out"].T, "a0_bo": w["L0_attn_b_out"][None],
        "f0_wmT": w["L0_ffn_Wm"].T, "f0_wpT": w["L0_ffn_Wp"].T, "f0_wc1T": w["L0_ffn_Wc1"].T, "f0_wc2T": w["L0_ffn_Wc2"].T,
        "l1_w": np.stack([w["L1_attn_W" + c] for c in "qkv"], 1), "l1_b": np.stack([w["L1_attn_b" + c] for c in "qkv"], 1),
        "l1_conv": np.stack([w[f"L1_attn_{c}_conv"] for c in "qkv"], 1),
        "l1_wab": np.concatenate([w["L1_attn_Wa"], w["L1_attn_Wb"]], 1),
        "l1_bab": np.concatenate([w["L1_attn_ba"], w["L1_attn_bb"]])[None],
        "l1_wg": w["L1_attn_Wg"], "l1_bg": w["L1_attn_bg"][None],
        "l1_gs": w["L1_attn_gn_scale"][None], "l1_gb": w["L1_attn_gn_bias"][None],
        "l1_wo": w["L1_attn_Wo"], "l1_bo": w["L1_attn_bo"][None],
        "x_wqT": w["L1_xattn_Wq"].reshape(D, XH, XD).transpose(2, 1, 0),
        "x_wkT": w["L1_xattn_Wk"].reshape(D, XH, XD).transpose(2, 1, 0),
        "x_wvT": w["L1_xattn_Wv"].reshape(D, XH, XD).transpose(2, 1, 0),
        "x_wout": w["L1_xattn_Wout"].reshape(XH, XD, D).transpose(1, 0, 2),
        "x_par": np.stack([w["L1_xattn_" + c] for c in ("gamma_media", "beta_media", "gamma_lat", "beta_lat")], 1),
        "x_gate": w["L1_xattn_kv_gate"].reshape(1, 1),
        "m_w1": w["L1_ffn_w1"].reshape(E8, EC, P, D).transpose(3, 0, 1, 2).reshape(D, E8 * EC, P),
        "m_w2": w["L1_ffn_w2"].reshape(E8, D, EC, P).transpose(3, 0, 2, 1).reshape(P, E8 * EC, D),
        "m_wr": np.concatenate([w["L1_ffn_w_macro"], w["L1_ffn_w_micro"].reshape(E8, D)]).T,
        "m_nw": w["L1_ffn_norm_w"][:, None],
    }
    return {k: np.ascontiguousarray(v) for k, v in a.items()}


def kernel(**inputs):
    import concourse.bacc as bacc
    from concourse.bass_utils import run_bass_kernel_spmd

    arrays = layouts(**{k: np.asarray(v) for k, v in inputs.items()})
    nc = bacc.Bacc("TRN2", target_bir_lowering=False, num_devices=1)
    d = {k: nc.dram_tensor("in_" + k, a.shape, mybir.dt.from_np(a.dtype), kind="ExternalInput").ap()
         for k, a in arrays.items()}
    d["out"] = nc.dram_tensor("out", [B, S, D], F32, kind="ExternalOutput").ap()
    decoder(nc, d)
    r = run_bass_kernel_spmd(nc, [{"in_" + k: a for k, a in arrays.items()}], core_ids=[0])
    return r.results[0]["out"]
```

```python
import numpy as np
import concourse.bass as bass
from concourse import mybir
from contextlib import ExitStack

F32 = mybir.dt.float32
F32R = mybir.dt.float32r
I32 = mybir.dt.int32
ACT = mybir.ActivationFunctionType
ALU = mybir.AluOpType
AX = mybir.AxisListType

P = 128
B, S, D = 128, 64, 128
TOK = B * S
TILES = 4
GTOK = TILES * P
GROUPS = TOK // GTOK
GB = GTOK // S
H, DH = 16, 8
LN_EPS = 1e-5


def stage_semaphores(nc, ctx, prefix):
    taken = []

    def release():
        nc.clear_and_free_semaphores(taken)
        nc.all_engine_barrier()

    ctx.callback(release)

    def sem(name):
        taken.append(nc.alloc_semaphore(prefix + name))
        return taken[-1]

    return sem


def self_attention_and_ffn(nc, d, keep):
    ident = keep["ident"]
    pooledT = keep["pooledT"]
    VW = DH + 1
    HH = H // 2
    SLOTS = 2 * TILES
    F1 = 4 * D
    FC = F1 // P
    SCALE = float(np.float32(1.0) / np.sqrt(np.float32(DH)))
    x_g = d["x"].rearrange("(g t q) s d -> g (q s) t d", t=TILES, q=2)
    c_g = d["ctx"].rearrange("(g t q) s d -> g (q s) t d", t=TILES, q=2)
    with ExitStack() as ctx:
        def sb(name, shape, dt=F32):
            return ctx.enter_context(nc.sbuf_tensor("A_" + name, shape, dt))

        def pb(name, shape, dt=F32):
            return ctx.enter_context(nc.psum_tensor("A_" + name, shape, dt))

        sem = stage_semaphores(nc, ctx, "A_")

        wqT = sb("wqT", [P, D]); wkT = sb("wkT", [P, D]); wvT = sb("wvT", [P, D])
        bq = sb("bq", [P, 2]); bk = sb("bk", [P, 2])
        bv = sb("bv", [P, D]); woT = sb("woT", [P, D]); bo = sb("bo", [P, D])
        headmask = sb("headmask", [P, HH])
        decayT = sb("decayT", [P, P])
        meanw = sb("meanw", [P, 2])
        wmT = sb("wmT", [P, F1]); wpT = sb("wpT", [P, FC, D])
        neghalf = sb("neghalf", [P, TILES])
        xin = sb("xin", [P, TILES, D]); xT = sb("xT", [P, GTOK])
        xb, qB, kM, va = ([sb(f"{n}{q}", shape) for q in range(2)] for n, shape in (
            ("xb", [P, TILES, D]),
            ("qB", [P, TILES, 2, 2, S]),
            ("kM", [P, 2, TILES, HH, S]),
            ("va", [P, GB, H // 2, 2, VW])))
        mx = sb("mx", [P, 2, HH]); e = sb("e", [P, 2, HH, S]); pT = sb("pT", [P, 2, HH // 2, P])
        rden = sb("rden", [P, 2, H]); att = sb("att", [P, 2, D]); attT = sb("attT", [P, 2, P])
        cin = sb("cin", [P, TILES, D]); csq = sb("csq", [P, TILES, D])
        r = sb("r", [P, TILES, D]); x1 = sb("x1", [P, TILES, D]); x2 = sb("x2", [P, TILES, D])
        st = sb("st", [P, TILES, 6]); mv = sb("mv", [P, TILES, 2]); ve = sb("ve", [P, TILES]); rs = sb("rs", [P, TILES])
        x2T = sb("x2T", [P, GTOK]); hT = sb("hT", [P, FC, GTOK]); f1 = sb("f1", [P, TILES, D])
        sc = pb("sc", [P, 2, 512])
        tp = pb("tp", [P, 2, HH // 2, P])
        oa = pb("oa", [P, 512])
        yy = pb("yy", [P, TILES, D])
        pw = pb("pw", [P, 2, 512])
        o_v = oa[:, 0:8 * 2 * 2 * VW].rearrange("p (j b r w) -> p j b r w", j=8, b=2, r=2)
        o_t = oa[:, 320:320 + P]
        o_p = pw[:, 1, 0:GB]

        s_const = sem("const"); s_ones = sem("ones"); s_x = sem("x_loaded"); s_c = sem("c_loaded"); s_csq = sem("csq")
        s_xTp = sem("xT_psum"); s_xT = sem("xT"); s_xb = sem("xb")
        s_qp = sem("q_psum"); s_q = sem("q"); s_kp = sem("k_psum"); s_k = sem("k"); s_vp = sem("v_psum"); s_va = sem("va")
        s_sc = sem("scores"); s_mx = sem("rowmax"); s_sub = sem("sub"); s_exp = sem("exp")
        s_tp = sem("pT_psum"); s_pT = sem("pT"); s_o = sem("o_psum"); s_rd = sem("rden"); s_at = sem("att")
        s_aTp = sem("attT_psum"); s_aT = sem("attT"); s_y = sem("y_psum"); s_r1 = sem("residual"); s_r2 = sem("scanned")
        s_dv = sem("dve_step"); s_turn = sem("turn")
        s_var = sem("var"); s_rstd = sem("rstd"); s_R = sem("decay_psum"); s_x2 = sem("x2")
        s_x2Tp = sem("x2T_psum"); s_x2T = sem("x2T"); s_h = sem("h_psum"); s_hT = sem("hT")
        s_f = sem("f_psum"); s_f1 = sem("f1"); s_pl = sem("pool_psum"); s_plc = sem("pooled")
        s_sx2 = sem("x2_stored"); s_sf1 = sem("f1_stored")
        block = ctx.enter_context(nc.Block())
        loads = [(wqT[:, :], d["a0_wqT"]), (wkT[:, :], d["a0_wkT"]), (wvT[:, :], d["a0_wvT"]), (bq[:, :], d["a0_bq"]),
                 (bk[:, :], d["a0_bk"]), (woT[:, :], d["a0_woT"]), (headmask[:, :], d["headmask"]),
                 (decayT[:, :], d["decayT"]), (meanw[:, :], d["meanw"]), (wmT[:, :], d["f0_wmT"][:, 0:F1]),
                 (wpT[:, :, :], d["f0_wpT"][0:F1, :].rearrange("(c p) n -> p c n", p=P)),
                 (bv[:, :], d["a0_bv"].broadcast_to((P, D))), (bo[:, :], d["a0_bo"].broadcast_to((P, D)))]
        NCONST = 16 * len(loads)

        def run(eng, unit):
            unit(0, 0, False, False, True)
            unit(1, 1, True, False, True)
            with eng.Fori(0, (GROUPS - 4) // 2) as i:
                unit(i * 2 + 2, 0, True, True, True)
                unit(i * 2 + 3, 1, True, True, True)
            unit(GROUPS - 2, 0, True, True, True)
            unit(GROUPS - 1, 1, True, True, False)

        @block.sync
        def _(sp):
            for dst, src in loads:
                sp.dma_start(dst, src).then_inc(s_const, 16)

            def load_x(g, first=False):
                if not first:
                    sp.wait_ge(s_xTp, g)
                    sp.wait_ge(s_xb, g)
                sp.dma_start(xin[:, :, :], x_g[g]).then_inc(s_x, 16)

            def load_c(g, first=False):
                if not first:
                    sp.wait_ge(s_csq, g)
                sp.dma_start(cin[:, :, :], c_g[g]).then_inc(s_c, 16)

            def store(g):
                sp.wait_ge(s_x2, g + 1)
                sp.dma_start(d["s_x2"][g], x2[:, :, :]).then_inc(s_sx2, 16)
                sp.wait_ge(s_f1, g + 2)
                sp.dma_start(d["s_f1"][g], f1[:, :, :]).then_inc(s_sf1, 16)

            load_x(0, True)
            load_c(0, True)
            load_x(1)
            load_x(2)
            with sp.Fori(1, GROUPS - 2) as g:
                load_c(g)
                load_x(g + 2)
                store(g - 1)
            load_c(GROUPS - 2)
            store(GROUPS - 3)
            load_c(GROUPS - 1)
            store(GROUPS - 2)
            store(GROUPS - 1)
            sp.wait_ge(s_sx2, GROUPS * 16 + 1)
            sp.wait_ge(s_sf1, GROUPS * 16 + 1)

        @block.tensor
        def _(pe):
            pe.wait_ge(s_const, NCONST)

            def x_transposed(g):
                pe.wait_ge(s_x, g * 16 + 16)
                pe.wait_ge(s_va, g * 2 + 1)
                for t in range(TILES):
                    m = pe.transpose(pw[:, 0, t * P:(t + 1) * P], xin[:, t, :], ident[:, :])
                m.then_inc(s_xTp, 1)

            def halves(w):
                xs = xT.rearrange("p (t b s) -> p t b s", t=TILES, b=2)
                pe.sem_inc(s_turn, 1)
                for hf in range(2):
                    for b in range(2):
                        m = pe.matmul(pw[64 * b:64 * b + 64, 0, hf * 256:(hf + 1) * 256], w[:, hf * 64:(hf + 1) * 64],
                                      xs[:, :, b, :], start=True, stop=True)
                return m

            def queries(g):
                pe.wait_ge(s_xT, g + 1)
                halves(wqT).then_inc(s_qp, 1)

            def keys(g):
                pe.wait_ge(s_q, g + 1)
                halves(wkT).then_inc(s_kp, 1)

            def values_in(g, c, behind):
                if c:
                    pe.wait_ge(s_va, g * 2 + 2)
                elif behind:
                    pe.wait_ge(s_hT, (g - 2) * FC + 4)
                else:
                    pe.wait_ge(s_k, g + 1)
                pe.sem_inc(s_turn, 1)
                for b in range(GB // 2):
                    for par in range(2):
                        m = pe.matmul(pw[64 * par:64 * par + 64, 0, b * D:(b + 1) * D],
                                      xT[:, (4 * c + b) * S:(4 * c + b + 1) * S], wvT[:, :], start=True, stop=True)
                m.then_inc(s_vp, 1)

            def scores(g, q, u):
                if u == 0:
                    pe.wait_ge(s_k, g + 1)
                pe.wait_ge(s_sub, g * SLOTS + u + 1)
                pe.matmul(sc[:, u % 2, :], qB[q][:, u // 2, u % 2, :, :].rearrange("p b s -> p (b s)"),
                          kM[q][:, u % 2, u // 2, :, :], start=True, stop=True).then_inc(s_sc, 1)

            def transposes(g, u):
                pe.wait_ge(s_exp, g * SLOTS + u + 1)
                pe.wait_ge(s_pT, g * SLOTS + u + 1)
                for j in range(HH // 2):
                    m = pe.transpose(tp[:, u % 2, j, :], e[:, u % 2, 2 * j:2 * j + 2, :], ident[:, :])
                m.then_inc(s_tp, 1)

            def values(g, q, u, behind):
                pe.wait_ge(s_pT, g * SLOTS + u + 3)
                if u == 0:
                    pe.wait_ge(s_va, g * 2 + 3)
                if u % 2 == 0:
                    pe.wait_ge(s_at, g * TILES + u // 2 + 1)
                    if u or behind:
                        pe.wait_ge(s_aT, g * TILES + u // 2)
                t, hf = u // 2, u % 2
                for j in range(HH // 2):
                    m = pe.matmul(o_v[:, 4 * hf + j, :, :, :], pT[:, u % 2, j, :], va[q][:, 2 * t:2 * t + 2, 4 * hf + j, :, :],
                                  start=True, stop=True)
                m.then_inc(s_o, 1)

            def att_transposed(g, t):
                pe.wait_ge(s_at, g * TILES + t + 2)
                pe.transpose(o_t, att[:, t % 2, :], ident[:, :]).then_inc(s_aTp, 1)

            def project(g, t):
                pe.wait_ge(s_aT, g * TILES + t + 1)
                if t == 0:
                    pe.wait_ge(s_r1, g + 1)
                m = pe.matmul(yy[:, t, :], attT[:, t % 2, :], woT[:, :], start=True, stop=True)
                if t == TILES - 1:
                    m.then_inc(s_y, 1)

            def decayed(g):
                pe.wait_ge(s_csq, g + 1)
                pe.wait_ge(s_f1, g + 1)
                pe.matmul(pw[:, 1, :], decayT[:, :], csq[:, :, :], start=True, stop=True).then_inc(s_R, 1)

            def x2_transposed(g):
                pe.wait_ge(s_x2, g + 1)
                pe.wait_ge(s_plc, g + 1)
                for t in range(TILES):
                    m = pe.transpose(pw[:, 1, t * P:(t + 1) * P], x2[:, t, :], ident[:, :])
                m.then_inc(s_x2Tp, 1)

            def up(g, c, ahead):
                if c == 1 and ahead:
                    pe.wait_ge(s_k, g + 3)
                if c < 2:
                    pe.wait_ge(s_x2T, g + 1)
                else:
                    pe.wait_ge(s_hT, g * FC + c - 1)
                pe.matmul(pw[:, (c + 1) % 2, :], wmT[:, c * P:(c + 1) * P], x2T[:, :], start=True, stop=True).then_inc(s_h, 1)

            def down(g):
                pe.wait_ge(s_hT, g * FC + FC)
                for t in range(TILES):
                    for c in range(FC):
                        m = pe.matmul(pw[:, 1, t * P:(t + 1) * P], hT[:, c, t * P:(t + 1) * P], wpT[:, c, :],
                                      start=(c == 0), stop=(c == FC - 1))
                m.then_inc(s_f, 1)

            def means(g, at):
                pe.wait_ge(s_f1, g + 2)
                pe.wait_ge(s_r2, at + 1)
                for t in range(TILES):
                    m = pe.matmul(o_p[:, 2 * t:2 * t + 2], f1[:, t, :], meanw[:, :], start=True, stop=True)
                m.then_inc(s_pl, 1)

            def unit(g, q, behind, behind2, ahead):
                for u in range(SLOTS):
                    transposes(g, u)
                    if u + 2 < SLOTS:
                        scores(g, q, u + 2)
                    elif ahead:
                        scores(g + 1, 1 - q, u + 2 - SLOTS)
                    if u % 2 == 0 and (u or behind):
                        att_transposed(*((g, u // 2 - 1) if u else (g - 1, TILES - 1)))
                    if u % 2 and (u > 1 or behind):
                        project(*((g, u // 2 - 1) if u > 1 else (g - 1, TILES - 1)))
                    if u == 0 and ahead:
                        x_transposed(g + 1)
                    if u == 1:
                        if behind:
                            decayed(g - 1)
                        if ahead:
                            queries(g + 1)
                    if u == 2 and ahead:
                        keys(g + 1)
                    if u == 3 and behind2:
                        means(g - 2, g - 1)
                    if u == 4 and behind:
                        x2_transposed(g - 1)
                    if u in (5, 6) and behind:
                        up(g - 1, 2 * (u - 5), ahead)
                        up(g - 1, 2 * (u - 5) + 1, ahead)
                    if u == 7 and behind:
                        down(g - 1)
                    values(g, q, u, behind)
                    if u == 6 and ahead:
                        values_in(g + 1, 0, behind)
                    if u == 7 and ahead:
                        values_in(g + 1, 1, behind)

            x_transposed(0)
            queries(0)
            keys(0)
            values_in(0, 0, False)
            values_in(0, 1, False)
            scores(0, 0, 0)
            scores(0, 0, 1)
            run(pe, unit)
            att_transposed(GROUPS - 1, TILES - 1)
            project(GROUPS - 1, TILES - 1)
            decayed(GROUPS - 1)
            means(GROUPS - 2, GROUPS - 1)
            x2_transposed(GROUPS - 1)
            for c in range(FC):
                up(GROUPS - 1, c, False)
            down(GROUPS - 1)
            means(GROUPS - 1, GROUPS - 1)

        @block.scalar
        def _(act):
            act.wait_ge(s_const, NCONST)
            act.wait_ge(s_ones, 7)
            act.sem_inc(s_pT, 2)

            def x_transposed(g):
                act.wait_ge(s_xTp, g + 1)
                act.activation(xT[:, :], pw[:, 0, :], ACT.Copy).then_inc(s_xT, 1)

            def queries(g, q):
                act.wait_ge(s_qp, g + 1)
                ps = pw[:, 0, :].rearrange("p (h t s) -> p h t s", h=2, t=TILES)
                for b in range(2):
                    rows = slice(64 * b, 64 * b + 64)
                    for hf in range(2):
                        m = act.activation(qB[q][rows, :, hf, b, :], ps[rows, hf, :, :], ACT.Identity, bias=bq[rows, hf:hf + 1])
                m.then_inc(s_q, 1)

            def exps(g, u):
                act.wait_ge(s_sub, g * SLOTS + u + 3)
                act.activation(e[:, u % 2, :, :], e[:, u % 2, :, :], ACT.Exp, scale=SCALE).then_inc(s_exp, 1)

            def evacuate(g, u):
                act.wait_ge(s_tp, g * SLOTS + u + 3)
                act.wait_ge(s_o, g * SLOTS + u + 1)
                act.activation(pT[:, u % 2, :, :], tp[:, u % 2, :, :], ACT.Copy).then_inc(s_pT, 1)

            def att_transposed(g, t):
                act.wait_ge(s_aTp, g * TILES + t + 1)
                act.activation(attT[:, t % 2, :], o_t, ACT.Copy).then_inc(s_aT, 1)

            def squares(g):
                act.wait_ge(s_c, g * 16 + 16)
                act.wait_ge(s_R, g + 1)
                act.activation(csq[:, :, :], cin[:, :, :], ACT.Square).then_inc(s_csq, 1)

            def x2_transposed(g):
                act.wait_ge(s_x2Tp, g + 1)
                act.activation(x2T[:, :], pw[:, 1, :], ACT.Copy).then_inc(s_x2T, 1)

            def relu(g, c):
                act.wait_ge(s_h, g * FC + c + 1)
                if c == 0:
                    act.wait_ge(s_f, g + 1)
                act.activation(hT[:, c, :], pw[:, (c + 1) % 2, :], ACT.Relu).then_inc(s_hT, 1)

            def unit(g, q, behind, behind2, ahead):
                for u in range(SLOTS):
                    evacuate(g, u)
                    if u % 2 == 0 and (u or behind):
                        att_transposed(*((g, u // 2 - 1) if u else (g - 1, TILES - 1)))
                    if u + 2 < SLOTS:
                        exps(g, u + 2)
                    elif ahead:
                        exps(g + 1, u + 2 - SLOTS)
                    if u == 0 and behind:
                        squares(g - 1)
                    if u == 0 and ahead:
                        x_transposed(g + 1)
                    if u == 1 and ahead:
                        queries(g + 1, 1 - q)
                    if u == 4 and behind:
                        x2_transposed(g - 1)
                    if u in (5, 6) and behind:
                        relu(g - 1, 2 * (u - 5))
                        relu(g - 1, 2 * (u - 5) + 1)

            act.sem_inc(s_o, 2)
            act.sem_inc(s_R, 1)
            act.sem_inc(s_f, 1)
            x_transposed(0)
            queries(0, 0)
            exps(0, 0)
            exps(0, 1)
            run(act, unit)
            att_transposed(GROUPS - 1, TILES - 1)
            squares(GROUPS - 1)
            x2_transposed(GROUPS - 1)
            for c in range(FC):
                relu(GROUPS - 1, c)

        @block.gpsimd
        def _(pool):
            pool.memset(neghalf[:, :], -0.5).then_inc(s_ones, 1)
            for q in range(2):
                pool.memset(qB[q][:, :, :, :, :], 0.0).then_inc(s_ones, 1)
                pool.memset(va[q][:, :, :, :, :], 0.0).then_inc(s_ones, 1)
            pool.wait_ge(s_ones, 5)
            for q in range(2):
                pool.memset(va[q][0:64, :, :, 0, DH:VW], 1.0)
                pool.memset(va[q][64:128, :, :, 1, DH:VW], 1.0).then_inc(s_ones, 1)
            with pool.Fori(0, 2 * GROUPS) as n:
                pool.wait_ge(s_var, n + 1)
                pool.tensor_tensor(rs[:, :], ve[:, :], neghalf[:, :], ALU.pow).then_inc(s_rstd, 1)

        @block.vector
        def _(v):
            v.wait_ge(s_const, NCONST)
            v.wait_ge(s_ones, 7)
            v.sem_inc(s_va, 1)
            v.sem_inc(s_sub, 2)
            v.sem_inc(s_tp, 2)
            v.sem_inc(s_at, 1)
            v.sem_inc(s_r1, 1)
            v.sem_inc(s_f1, 1)
            v.sem_inc(s_plc, 1)
            v.sem_inc(s_sx2, 1)
            v.sem_inc(s_sf1, 1)
            STEPS = 8
            n = [0, 0]

            def link(ins):
                n[1] += 1
                assert n[1] <= STEPS
                ins.then_inc(s_dv, 1)
                v.wait_ge(s_dv, n[0] * STEPS + n[1])

            def close():
                if n[1] < STEPS:
                    v.sem_inc(s_dv, STEPS - n[1])

            def biased(g, q):
                v.wait_ge(s_x, g * 16 + 16)
                v.tensor_tensor(xb[q][:, :, :], xin[:, :, :],
                                bo.rearrange("p (o n) -> p o n", o=1).broadcast_to((P, TILES, D)), ALU.add).then_inc(s_xb, 1)

            def keys(g, q, pieces):
                v.wait_ge(s_kp, g + 1)
                for c in pieces:
                    hf, t = c // TILES, c % TILES
                    m = v.scalar_tensor_tensor(
                        kM[q][:, hf, t, :, :],
                        pw[:, 0, c * S:(c + 1) * S].rearrange("p (o s) -> p o s", o=1).broadcast_to((P, HH, S)),
                        bk[:, hf:hf + 1], headmask.rearrange("p (h i) -> p h i", i=1).broadcast_to((P, HH, S)), ALU.add, ALU.mult)
                if 2 * TILES - 1 in pieces:
                    m.then_inc(s_k, 1)

            def values_in(g, q, c):
                v.wait_ge(s_vp, g * 2 + c + 1)
                v5 = pw[:, 0, :].rearrange("p (b j r d) -> p b j r d", b=4, j=8, r=2)
                b4 = bv.rearrange("p (o j r d) -> p o j r d", o=1, j=8, r=2)
                for par in range(2):
                    rows = slice(64 * par, 64 * par + 64)
                    m = v.tensor_tensor(va[q][rows, 4 * c:4 * c + 4, :, par, 0:DH], v5[rows, :, :, par, :],
                                        b4[rows, :, :, par, :].broadcast_to((64, 4, 8, DH)), ALU.add)
                m.then_inc(s_va, 1)

            def softmax(g, u):
                v.wait_ge(s_sc, g * SLOTS + u + 1)
                s3 = sc[:, u % 2, :].rearrange("p (h k) -> p h k", k=S)
                v.tensor_reduce(mx[:, u % 2, :], s3, AX.X, ALU.max).then_inc(s_mx, 1)
                v.wait_ge(s_mx, g * SLOTS + u + 1)
                v.wait_ge(s_tp, g * SLOTS + u + 1)
                v.tensor_tensor(e[:, u % 2, :, :], s3,
                                mx[:, u % 2, :].rearrange("p (h o) -> p h o", o=1).broadcast_to((P, HH, S)),
                                ALU.subtract).then_inc(s_sub, 1)

            def normalise(g, t):
                v.wait_ge(s_o, g * SLOTS + 2 * t + 4)
                for b in range(2):
                    rows = slice(64 * b, 64 * b + 64)
                    m = v.reciprocal(rden[rows, t % 2, :].rearrange("p (j r) -> p j r", j=8), o_v[rows, :, b, :, DH])
                m.then_inc(s_rd, 1)
                v.wait_ge(s_rd, g * TILES + t + 1)
                for b in range(2):
                    rows = slice(64 * b, 64 * b + 64)
                    m = v.tensor_tensor(att[rows, t % 2, :].rearrange("p (j r d) -> p j r d", j=8, r=2),
                                        o_v[rows, :, b, :, 0:DH],
                                        rden[rows, t % 2, :].rearrange("p (j r o) -> p j r o", j=8, r=2)
                                        .broadcast_to((64, 8, 2, DH)), ALU.mult)
                m.then_inc(s_at, 1)

            def statistics():
                for t in range(TILES):
                    m = v.bn_stats(st[:, t, :], r[:, t, :])
                link(m)
                v.sem_inc(s_turn, 1)
                for t in range(TILES):
                    m = v.bn_aggr(mv[:, t, :], st[:, t, :])
                link(m)
                v.tensor_scalar(ve[:, :], mv[:, :, 1], LN_EPS, None, ALU.add).then_inc(s_var, 1)

            def norm(dst, count):
                v.wait_ge(s_rstd, count)
                for t in range(TILES):
                    m = v.tensor_scalar(dst[:, t, :], r[:, t, :], mv[:, t, 0:1], rs[:, t:t + 1], ALU.subtract, ALU.mult)
                return m

            def residual(g, q):
                v.wait_ge(s_y, g + 1)
                v.tensor_tensor(r[:, :, :], yy[:, :, :], xb[q][:, :, :], ALU.add).then_inc(s_r1, 1)
                v.wait_ge(s_r1, g + 2)
                statistics()

            def scan(g):
                link(norm(x1, g * 2 + 1))
                v.wait_ge(s_R, g + 2)
                v.scalar_tensor_tensor(r[:, :, :].rearrange("p t d -> p (t d)"), pw[:, 1, :], 1.0,
                                       x1[:, :, :].rearrange("p t d -> p (t d)"), ALU.add, ALU.mult).then_inc(s_r2, 1)
                v.wait_ge(s_r2, g + 1)
                statistics()

            def second_norm(g):
                v.wait_ge(s_sx2, g * 16 + 1)
                norm(x2, g * 2 + 2).then_inc(s_x2, 1)

            def ffn_out(g):
                v.wait_ge(s_f, g + 2)
                v.wait_ge(s_sf1, g * 16 + 1)
                v.tensor_copy(f1[:, :, :], pw[:, 1, :].rearrange("p (t n) -> p t n", t=TILES)).then_inc(s_f1, 1)

            def means(g):
                v.wait_ge(s_pl, g + 1)
                v.tensor_copy(pooledT[:, bass.ds(g * GB, GB)], o_p).then_inc(s_plc, 1)

            def unit(g, q, behind, behind2, ahead):
                n[0], n[1] = g, 0
                for u in range(SLOTS):
                    if u + 2 < SLOTS:
                        softmax(g, u + 2)
                    elif ahead:
                        softmax(g + 1, u + 2 - SLOTS)
                    if u % 2 and u < 7:
                        normalise(g, u // 2)
                    if u == 1 and behind:
                        residual(g - 1, 1 - q)
                    if u == 2:
                        if behind:
                            scan(g - 1)
                    if u == 5 and ahead:
                        biased(g + 1, 1 - q)
                    if u == 3 and behind:
                        second_norm(g - 1)
                    if u == 3 and behind2:
                        means(g - 2)
                    if u in (3, 4) and ahead:
                        keys(g + 1, 1 - q, range(TILES * (u - 3), TILES * (u - 2)))
                    if u == 7 and behind:
                        ffn_out(g - 1)
                    if u == 7:
                        normalise(g, u // 2)
                    if u == 6 and ahead:
                        values_in(g + 1, 1 - q, 0)
                    if u == 7 and ahead:
                        values_in(g + 1, 1 - q, 1)
                close()

            biased(0, 0)
            keys(0, 0, range(2 * TILES))
            values_in(0, 0, 0)
            values_in(0, 0, 1)
            softmax(0, 0)
            softmax(0, 1)
            run(v, unit)
            n[0], n[1] = GROUPS, 0
            residual(GROUPS - 1, 1)
            scan(GROUPS - 1)
            means(GROUPS - 2)
            second_norm(GROUPS - 1)
            ffn_out(GROUPS - 1)
            means(GROUPS - 1)


FULL = 12 * D
KEEP = 4 * D
FCH = FULL // P
BISECT = 48
UNROLL = 8
SIGNED = FULL // 2
NOVELTY = float(np.float32(0.7)) * B * KEEP


def route(nc, d, keep, first, run):
    ident, pooledT, go, mask, maskT = (keep[k] for k in ("ident", "pooledT", "go", "mask", "maskT"))
    name = ("R" if not run else "S" if first else "T") + "_"
    choose = first or not run
    with ExitStack() as ctx:
        def sb(n, shape, dt=F32):
            return ctx.enter_context(nc.sbuf_tensor(name + n, shape, dt))

        def pb(n, shape, dt=F32):
            return ctx.enter_context(nc.psum_tensor(name + n, shape, dt))

        sem = stage_semaphores(nc, ctx, name)

        s_const = sem("const")
        if run:
            wmT = sb("wmT", [P, FULL]); wpT = sb("wpT", [P, FCH, D]); meanw = sb("meanw", [P, 2])
            xc = sb("xc", [P, TILES, D]); xT = sb("xT", [P, GTOK])
            hr = sb("hr", [P, FCH, GTOK]); hm = sb("hm", [P, FCH, GTOK]); fo = sb("fo", [P, TILES, D])
            ph = pb("ph", [P, 3, GTOK]); pt = pb("pt", [P, GTOK]); pf = pb("pf", [P, TILES, D])
            s_x = sem("x"); s_xfree = sem("xfree"); s_xTp = sem("xTp"); s_xT = sem("xT")
            s_h = sem("h"); s_hr = sem("hr"); s_hm = sem("hm"); s_f = sem("f"); s_fo = sem("fo"); s_fst = sem("fst")
            s_pl = sem("pl"); s_plc = sem("plc")
        if choose:
            wc1T = sb("wc1T", [P, D // 4]); wc2T = sb("wc2T", [D // 4, FULL])
            hid = sb("hid", [D // 4, B]); ck = sb("ck", [P, FULL]); junk = sb("junk", [P, FULL]); signs = sb("signs", [P, SIGNED])
            gt = sb("gt", [P, FULL]); eq = sb("eq", [P, FULL]); cum = sb("cum", [P, FULL]); old = sb("old", [P, FULL])
            one = sb("one", [P, FULL]); ones = sb("ones", [P, 1])
            sm = sb("sm", [P, 16])
            pc = pb("pc", [P, 3, 512]) if not run else None
            s_hid = sem("hid"); s_hidr = sem("hidr"); s_ck = sem("ck"); s_d = sem("d"); s_msk = sem("msk"); s_pm = sem("pm")
            s_mt = sem("mt"); s_tot = sem("tot"); s_go = sem("go"); s_loop = sem("loop"); s_mid = sem("mid"); s_sign = sem("signs")
            if run:
                pc = ph
        pm = pb("pm", [P, 512])
        block = ctx.enter_context(nc.Block())
        loads = []
        if run:
            loads += [(wmT[:, :], d["f0_wmT"]), (wpT[:, :, :], d["f0_wpT"].rearrange("(c p) n -> p c n", p=P)),
                      (meanw[:, :], d["meanw"])]
        if choose:
            loads += [(wc1T[:, :], d["f0_wc1T"]), (wc2T[:, :], d["f0_wc2T"])]
        NCONST = 16 * len(loads)

        def conditional(eng, body):
            if not run:
                body()
                return
            due = eng.value_load(go[0:1, 0:1], min_val=0, max_val=1)
            with eng.If(due > 0):
                body()
                eng.nop()
            with eng.Else():
                eng.nop()

        @block.sync
        def _(sp):
            def body():
                for dst, src in loads:
                    sp.dma_start(dst, src).then_inc(s_const, 16)
                if run:
                    with sp.Fori(0, GROUPS) as i:
                        sp.wait_ge(s_xfree, i + 1)
                        sp.dma_start(xc[:, :, :], d["s_f1"][i]).then_inc(s_x, 16)
                        sp.wait_ge(s_fo, i + 1)
                        sp.dma_start(d["s_f1"][i], fo[:, :, :]).then_inc(s_fst, 16)
                    sp.wait_ge(s_fst, GROUPS * 16)
                else:
                    sp.wait_ge(s_const, NCONST)
            conditional(sp, body)

        @block.tensor
        def _(pe):
            def body():
                pe.wait_ge(s_const, NCONST)
                if run:
                    with pe.Fori(0, GROUPS) as i:
                        pe.wait_ge(s_x, i * 16 + 16)
                        for t in range(TILES):
                            m = pe.transpose(pt[:, t * P:(t + 1) * P], xc[:, t, :], ident[:, :])
                        m.then_inc(s_xTp, 1)
                        pe.wait_ge(s_xT, i + 1)
                        for c in range(FCH):
                            if c >= 3:
                                pe.wait_ge(s_hr, i * FCH + c - 2)
                            pe.matmul(ph[:, c % 3, :], wmT[:, c * P:(c + 1) * P], xT[:, :],
                                      start=True, stop=True).then_inc(s_h, 1)
                        pe.wait_ge(s_hm, i * FCH + FCH + 1)
                        for t in range(TILES):
                            for c in range(FCH):
                                m = pe.matmul(pf[:, t, :], hm[:, c, t * P:(t + 1) * P], wpT[:, c, :],
                                              start=(c == 0), stop=(c == FCH - 1))
                        m.then_inc(s_f, 1)
                        pe.wait_ge(s_fo, i + 1)
                        if choose:
                            pe.wait_ge(s_plc, i + 1)
                            for t in range(TILES):
                                m = pe.matmul(pm[:, 2 * t:2 * t + 2], fo[:, t, :], meanw[:, :], start=True, stop=True)
                            m.then_inc(s_pl, 1)
                if choose:
                    if run:
                        pe.wait_ge(s_plc, GROUPS + 1)
                    pe.matmul(pm[0:D // 4, 128:128 + B], wc1T[:, :], pooledT[:, :], start=True, stop=True).then_inc(s_hid, 1)
                    pe.wait_ge(s_hidr, 1)
                    for c in range(3):
                        m = pe.matmul(pc[:, c, :], hid[:, :], wc2T[:, c * 512:(c + 1) * 512], start=True, stop=True)
                    m.then_inc(s_ck, 1)
                    pe.wait_ge(s_msk, 1)
                    for c in range(3):
                        for j in range(4):
                            m = pe.transpose(pc[:, c, j * P:(j + 1) * P], mask[:, (4 * c + j) * P:(4 * c + j + 1) * P], ident[:, :])
                    m.then_inc(s_pm, 1)
                    pe.matmul(pm[0:1, 0:1], sm[:, 8:9], ones[:, :], start=True, stop=True).then_inc(s_tot, 1)
            conditional(pe, body)

        @block.scalar
        def _(act):
            def body():
                act.wait_ge(s_const, NCONST)
                if run:
                    act.sem_inc(s_xfree, 1)
                    with act.Fori(0, GROUPS) as i:
                        act.wait_ge(s_xTp, i + 1)
                        act.activation(xT[:, :], pt[:, :], ACT.Copy).then_inc(s_xT, 1)
                        act.wait_ge(s_xT, i + 1)
                        act.sem_inc(s_xfree, 1)
                        for c in range(FCH):
                            act.wait_ge(s_h, i * FCH + c + 1)
                            if c == 0:
                                act.wait_ge(s_hm, i * FCH + 1)
                            act.activation(hr[:, c, :], ph[:, c % 3, :], ACT.Relu).then_inc(s_hr, 1)
                if choose:
                    act.wait_ge(s_hid, 1)
                    act.activation(hid[:, :], pm[0:D // 4, 128:128 + B], ACT.Relu).then_inc(s_hidr, 1)
                    with act.Fori(0, BISECT // UNROLL) as j:
                        for u in range(UNROLL):
                            act.wait_ge(s_mid, j * UNROLL + u + 2)
                            act.activation(signs[:, :], ck[:, FULL - SIGNED:FULL], ACT.Sign, bias=sm[:, 2:3], scale=-1.0,
                                           accum_out=sm[:, 9:10]).then_inc(s_sign, 1)
                    act.wait_ge(s_pm, 1)
                    for c in range(3):
                        m = act.activation(maskT[:, 4 * c:4 * c + 4, :], pc[:, c, :], ACT.Copy)
                    m.then_inc(s_mt, 1)
                    act.wait_ge(s_mt, 1)
            conditional(act, body)

        @block.gpsimd
        def _(pool):
            pool.nop()

        @block.vector
        def _(v):
            n = [0]

            def link(ins):
                n[0] += 1
                ins.then_inc(s_d, 1)
                v.wait_ge(s_d, n[0])

            def body():
                v.wait_ge(s_const, NCONST)
                if run:
                    v.sem_inc(s_hm, 1)
                    if choose:
                        v.sem_inc(s_plc, 1)
                    with v.Fori(0, GROUPS) as i:
                        for c in range(FCH):
                            v.wait_ge(s_hr, i * FCH + c + 1)
                            m4 = maskT[:, c, bass.ds(i * GB, GB)].rearrange("p (b o) -> p b o", o=1).broadcast_to((P, GB, S))
                            v.tensor_tensor(hm[:, c, :].rearrange("p (b s) -> p b s", s=S),
                                            hr[:, c, :].rearrange("p (b s) -> p b s", s=S), m4, ALU.mult).then_inc(s_hm, 1)
                        v.wait_ge(s_f, i + 1)
                        v.wait_ge(s_x, i * 16 + 16)
                        v.tensor_copy(fo[:, :, :], pf[:, :, :]).then_inc(s_fo, 1)
                        if choose:
                            v.wait_ge(s_pl, i + 1)
                            v.tensor_copy(pooledT[:, bass.ds(i * GB, GB)], pm[:, 0:8]).then_inc(s_plc, 1)
                if not choose:
                    return
                lo, w, mid, cnt, t0, hi, need, cg = (sm[:, k:k + 1] for k in range(8))
                new, below = sm[:, 8:9], sm[:, 9:10]
                v.wait_ge(s_ck, 1)
                v.memset(one[:, :], 1.0)
                v.memset(ones[:, :], 1.0)
                if run:
                    link(v.tensor_copy(old[:, :], mask[:, :]))
                    link(v.memset(old[:, 0:KEEP], 1.0))
                else:
                    v.memset(old[:, KEEP:FULL], 0.0)
                    link(v.memset(old[:, 0:KEEP], 1.0))
                link(v.tensor_copy(ck[:, :], pc[:, :, :].rearrange("p c n -> p (c n)")))
                v.tensor_reduce(lo, ck[:, :], AX.X, ALU.min)
                link(v.tensor_reduce(hi, ck[:, :], AX.X, ALU.max))
                link(v.tensor_tensor(w, hi, lo, ALU.subtract))
                v.sem_inc(s_mid, 1)
                with v.Fori(0, BISECT // UNROLL) as j:
                    k = [0]

                    def chain(ins):
                        k[0] += 1
                        ins.then_inc(s_loop, 1)
                        v.wait_ge(s_loop, j * (4 * UNROLL) + k[0])

                    for u in range(UNROLL):
                        v.tensor_tensor(mid, lo, w, ALU.add).then_inc(s_mid, 1)
                        v.wait_ge(s_mid, j * UNROLL + u + 2)
                        chain(v.tensor_scalar(junk[:, 0:FULL - SIGNED], ck[:, 0:FULL - SIGNED], mid, 0.0, ALU.is_ge, ALU.add, accum_out=cnt))
                        v.wait_ge(s_sign, j * UNROLL + u + 1)
                        chain(v.scalar_tensor_tensor(t0, cnt, 2.0, below, ALU.mult, ALU.subtract))
                        chain(v.scalar_tensor_tensor(t0, t0, float(2 * KEEP - SIGNED), w, ALU.is_ge, ALU.mult))
                        v.tensor_scalar(w, w, 0.5, None, ALU.mult)
                        chain(v.tensor_tensor(lo, lo, t0, ALU.add))
                link(v.tensor_scalar(junk[:, :], ck[:, :], lo, 3.0e38, ALU.is_lt, ALU.mult))
                link(v.tensor_tensor(junk[:, :], junk[:, :], ck[:, :], ALU.add))
                link(v.tensor_reduce(hi, junk[:, :], AX.X, ALU.min))
                v.tensor_scalar(gt[:, :], ck[:, :], hi, 0.0, ALU.is_gt, ALU.add, accum_out=cg)
                link(v.tensor_scalar(eq[:, :], ck[:, :], hi, None, ALU.is_equal))
                link(v.tensor_tensor_scan(cum[:, :], one[:, :], gt[:, :], 0.0, ALU.mult, ALU.add))
                link(v.scalar_tensor_tensor(gt[:, :], cum[:, :], float(KEEP), gt[:, :], ALU.is_le, ALU.mult))
                link(v.tensor_scalar(need, cg, -1.0, float(KEEP), ALU.mult, ALU.add))
                link(v.tensor_tensor_scan(cum[:, :], one[:, :], eq[:, :], 0.0, ALU.mult, ALU.add))
                link(v.scalar_tensor_tensor(eq[:, :], cum[:, :], need, eq[:, :], ALU.is_le, ALU.mult))
                link(v.tensor_tensor(mask[:, :], gt[:, :], eq[:, :], ALU.add))
                link(v.tensor_tensor(junk[:, :], mask[:, :], old[:, :], ALU.mult))
                link(v.tensor_tensor(junk[:, :], mask[:, :], junk[:, :], ALU.subtract))
                v.tensor_reduce(new, junk[:, :], AX.X, ALU.add).then_inc(s_msk, 1)
                v.wait_ge(s_tot, 1)
                v.tensor_scalar(go[0:1, :], pm[0:1, 0:1], keep["novelty"], None, ALU.is_ge).then_inc(s_go, 1)
                v.wait_ge(s_go, 1)
            conditional(v, body)


CONV = 4
PAD = CONV - 1
TW = 4 * D + H


def delta_inputs(nc, d, keep):
    ident = keep["ident"]
    rows_g = d["s_rows"].rearrange("(g t q) s n -> g (q s) t n", t=TILES, q=2)
    D3 = 3 * D
    GW = D + 2 * H
    QK = 2 * TILES * H
    with ExitStack() as ctx:
        def sb(name, shape, dt=F32):
            return ctx.enter_context(nc.sbuf_tensor("C_" + name, shape, dt))

        def pb(name, shape, dt=F32):
            return ctx.enter_context(nc.psum_tensor("C_" + name, shape, dt))

        sem = stage_semaphores(nc, ctx, "C_")

        w = sb("w", [P, D3]); taps = sb("taps", [P, CONV, D3]); wt = sb("wt", [P, CONV, D3])
        valid = sb("valid", [P, CONV]); bias = sb("bias", [P, D3]); bt = sb("bt", [P, D3])
        wg = sb("wg", [P, GW]); bg = sb("bg", [P, GW]); neghalf = sb("neghalf", [P, TILES])
        xa = sb("xa", [P, TILES, D]); xf = sb("xf", [P, TILES, D]); r = sb("r", [P, TILES, D]); x3 = sb("x3", [P, TILES, D])
        st = sb("st", [P, TILES, 6]); mv = sb("mv", [P, TILES, 2]); ve = sb("ve", [P, TILES]); rs = sb("rs", [P, TILES])
        xT = [sb(f"xT{q}", [P, GB, PAD + S]) for q in range(2)]
        act_in = [sb(f"qkv{q}", [P, TILES, D3]) for q in range(2)]
        gates = [sb(f"gates{q}", [P, TILES, GW]) for q in range(2)]
        g_out = sb("g_out", [P, TILES, D])
        sq = sb("sq", [P, TILES, 2 * D]); ss = sb("ss", [P, QK]); nr = sb("nr", [P, QK]); ne = sb("ne", [P, QK]); rn = sb("rn", [P, QK])
        ab = sb("ab", [P, TILES, 2 * H]); apb = sb("apb", [P, TILES, H]); out = sb("out", [P, TILES, TW])
        px = pb("px", [P, GTOK]); pc = pb("pc", [P, TILES, 512]); pg = pb("pg", [P, 2, 512])

        s_const = sem("const"); s_set = sem("set"); s_wt = sem("weights"); s_x = sem("x"); s_xfree = sem("xfree"); s_dv = sem("dve_step")
        s_turn = sem("turn"); s_var = sem("var"); s_rstd = sem("rstd"); s_x3 = sem("x3"); s_xTp = sem("xT_psum"); s_xT = sem("xT")
        s_conv = sem("conv_psum"); s_pre = sem("conv"); s_gp = sem("gates_psum"); s_gr = sem("gates_biased")
        s_silu = sem("silu"); s_g = sem("gate"); s_abt = sem("tanh"); s_sq = sem("squares"); s_ss = sem("sums"); s_nr = sem("norms")
        s_out = sem("out"); s_sx = sem("x3_stored"); s_sg = sem("gate_stored"); s_rows = sem("rows_stored")
        block = ctx.enter_context(nc.Block())
        loads = [(w[:, :], d["l1_w"]), (bias[:, :], d["l1_b"].broadcast_to((P, D3))), (valid[:, :], d["l1_valid"]),
                 (taps.rearrange("p k n -> p (k n)"), d["l1_conv"].broadcast_to((P, CONV * D3))),
                 (wg[:, :], d["l1_wg"]), (bg[:, :], d["l1_bg"].broadcast_to((P, GW)))]
        NCONST = 16 * len(loads)

        def run(eng, unit):
            unit(0, 0, False, True)
            with eng.Fori(0, (GROUPS - 2) // 2) as i:
                unit(i * 2 + 1, 1, True, True)
                unit(i * 2 + 2, 0, True, True)
            unit(GROUPS - 1, 1, True, False)

        @block.sync
        def _(sp):
            for dst, src in loads:
                sp.dma_start(dst, src).then_inc(s_const, 16)

            def load(g):
                sp.wait_ge(s_xfree, g + 1)
                sp.dma_start(xa[:, :, :], d["s_x2"][g]).then_inc(s_x, 16)
                sp.dma_start(xf[:, :, :], d["s_f1"][g]).then_inc(s_x, 16)

            def store_x3(g):
                sp.wait_ge(s_x3, g + 1)
                sp.dma_start(d["s_x3"][g], x3[:, :, :]).then_inc(s_sx, 16)

            def store_gate(g):
                sp.wait_ge(s_g, g + 1)
                sp.dma_start(d["s_gate"][g], g_out[:, :, :]).then_inc(s_sg, 16)

            def store_rows(g):
                sp.wait_ge(s_out, g + 1)
                for t in range(TILES):
                    sp.dma_start(rows_g[g][:, t, :], out[:, t, :]).then_inc(s_rows, 16)

            load(0)
            store_x3(0)
            load(1)
            store_x3(1)
            load(2)
            store_gate(0)
            with sp.Fori(1, GROUPS - 2) as g:
                store_x3(g + 1)
                load(g + 2)
                store_gate(g)
                store_rows(g - 1)
            store_x3(GROUPS - 1)
            store_gate(GROUPS - 2)
            store_rows(GROUPS - 3)
            store_gate(GROUPS - 1)
            store_rows(GROUPS - 2)
            store_rows(GROUPS - 1)
            sp.wait_ge(s_sx, GROUPS * 16 + 1)
            sp.wait_ge(s_sg, GROUPS * 16 + 1)
            sp.wait_ge(s_rows, GROUPS * 16 * TILES + 1)

        @block.tensor
        def _(pe):
            pe.wait_ge(s_wt, 2)

            def transposes(g):
                pe.wait_ge(s_x3, g + 1)
                for t in range(TILES):
                    m = pe.transpose(px[:, t * P:(t + 1) * P], x3[:, t, :], ident[:, :])
                m.then_inc(s_xTp, 1)

            def conv(g, q, t):
                if t == 0:
                    pe.wait_ge(s_xT, g + 1)
                pe.wait_ge(s_pre, g * TILES + t + 1)
                pe.sem_inc(s_turn, 1)
                for k in range(CONV):
                    for b in range(2):
                        m = pe.matmul(pc[64 * b:64 * b + 64, t, 0:D3], xT[q][:, 2 * t + b, k:k + S], wt[:, k, :],
                                      start=(k == 0), stop=(k == CONV - 1))
                m.then_inc(s_conv, 1)

            def gating(g, q, p):
                pe.wait_ge(s_gr, g * 2 + p + 1)
                pe.sem_inc(s_turn, 1)
                for t in range(2):
                    for b in range(2):
                        m = pe.matmul(pg[64 * b:64 * b + 64, p, t * GW:(t + 1) * GW], xT[q][:, 2 * (2 * p + t) + b, PAD:PAD + S],
                                      wg[:, :], start=True, stop=True)
                m.then_inc(s_gp, 1)

            def unit(g, q, prev, following):
                conv(g, q, 0)
                conv(g, q, 1)
                gating(g, q, 0)
                conv(g, q, 2)
                if following:
                    transposes(g + 1)
                conv(g, q, 3)
                gating(g, q, 1)

            transposes(0)
            run(pe, unit)

        @block.scalar
        def _(act):
            act.wait_ge(s_const, NCONST)
            act.wait_ge(s_set, 3)
            act.sem_inc(s_sg, 1)

            def transposed(g, q):
                act.wait_ge(s_xTp, g + 1 + 1)
                act.activation(xT[q][:, :, PAD:PAD + S], px.rearrange("p (b s) -> p b s", s=S), ACT.Copy).then_inc(s_xT, 1)

            def silu(g, q, t):
                act.wait_ge(s_pre, (g + 1) * TILES + t + 1)
                act.activation(act_in[q][:, t, :], act_in[q][:, t, :], ACT.Silu).then_inc(s_silu, 1)

            def gating(g, q):
                act.wait_ge(s_gr, (g + 1) * 2 + 2)
                act.wait_ge(s_sg, g * 16 + 1)
                act.activation(g_out[:, :, :], gates[q][:, :, 0:D], ACT.Silu).then_inc(s_g, 1)
                act.activation(gates[q][:, :, D:GW], gates[q][:, :, D:GW], ACT.Tanh, scale=0.5).then_inc(s_abt, 1)

            def squares(g, q):
                act.wait_ge(s_silu, g * TILES + TILES)
                act.wait_ge(s_ss, g + 1)
                act.activation(sq[:, :, :], act_in[q][:, :, 0:2 * D], ACT.Square).then_inc(s_sq, 1)

            def norms(g):
                act.wait_ge(s_ss, g + 2)
                act.activation(nr[:, :], ss[:, :], ACT.Sqrt).then_inc(s_nr, 1)

            def unit(g, q, prev, following):
                if prev:
                    norms(g - 1)
                silu(g, q, 0)
                silu(g, q, 1)
                silu(g, q, 2)
                if following:
                    transposed(g + 1, 1 - q)
                silu(g, q, 3)
                squares(g, q)
                gating(g, q)

            transposed(0, 0)
            run(act, unit)
            norms(GROUPS - 1)

        @block.gpsimd
        def _(pool):
            pool.memset(neghalf[:, :], -0.5).then_inc(s_set, 1)
            for q in range(2):
                pool.memset(xT[q][:, :, 0:PAD], 0.0).then_inc(s_set, 1)
            pool.wait_ge(s_set, 3)
            with pool.Fori(0, GROUPS) as g:
                pool.wait_ge(s_var, g + 1)
                pool.tensor_tensor(rs[:, :], ve[:, :], neghalf[:, :], ALU.pow).then_inc(s_rstd, 1)

        @block.vector
        def _(v):
            v.wait_ge(s_const, NCONST)
            v.wait_ge(s_set, 3)
            v.sem_inc(s_xfree, 1)
            v.sem_inc(s_pre, TILES)
            v.sem_inc(s_gr, 2)
            v.sem_inc(s_xTp, 1)
            v.sem_inc(s_ss, 1)
            v.sem_inc(s_sx, 1)
            v.sem_inc(s_rows, 1)
            STEPS = 12
            n = [0, 0]

            def link(ins):
                n[1] += 1
                assert n[1] <= STEPS
                ins.then_inc(s_dv, 1)
                v.wait_ge(s_dv, (n[0] + 1) * STEPS + n[1])

            def close():
                if n[1] < STEPS:
                    v.sem_inc(s_dv, STEPS - n[1])

            def statistics(g):
                v.wait_ge(s_x, g * 32 + 32)
                link(v.tensor_tensor(r[:, :, :], xa[:, :, :], xf[:, :, :], ALU.add))
                v.sem_inc(s_xfree, 1)
                for t in range(TILES):
                    m = v.bn_stats(st[:, t, :], r[:, t, :])
                link(m)
                v.sem_inc(s_turn, 1)
                for t in range(TILES):
                    m = v.bn_aggr(mv[:, t, :], st[:, t, :])
                link(m)
                v.tensor_scalar(ve[:, :], mv[:, :, 1], LN_EPS, None, ALU.add).then_inc(s_var, 1)

            def norm(g):
                v.wait_ge(s_rstd, g + 1)
                v.wait_ge(s_sx, g * 16 + 1)
                v.wait_ge(s_xTp, g + 1)
                for t in range(TILES):
                    m = v.tensor_scalar(x3[:, t, :], r[:, t, :], mv[:, t, 0:1], rs[:, t:t + 1], ALU.subtract, ALU.mult)
                m.then_inc(s_x3, 1)

            def add_bias(g, q, t):
                v.wait_ge(s_conv, g * TILES + t + 1)
                v.tensor_tensor(act_in[q][:, t, :], pc[:, t, 0:D3], bt[:, :], ALU.add).then_inc(s_pre, 1)

            def add_gate_bias(g, q, p):
                v.wait_ge(s_gp, g * 2 + p + 1)
                v.tensor_tensor(gates[q][:, 2 * p:2 * p + 2, :], pg[:, p, 0:2 * GW].rearrange("p (t n) -> p t n", t=2),
                                bg.rearrange("p (o n) -> p o n", o=1).broadcast_to((P, 2, GW)), ALU.add).then_inc(s_gr, 1)

            def sums(g):
                v.wait_ge(s_sq, g + 1)
                v.tensor_reduce(ss[:, :], sq.rearrange("p t (h e) -> p (t h) e", e=DH), AX.X, ALU.add).then_inc(s_ss, 1)

            def heads(x):
                return x.rearrange("p t (h e) -> p t h e", e=DH)

            def over(x):
                return x.rearrange("p t (h o) -> p t h o", o=1)

            def products(g, q):
                v.wait_ge(s_abt, g + 1)
                v.wait_ge(s_rows, g * 16 * TILES + 1)
                v.tensor_scalar(ab[:, :, :], gates[q][:, :, D:GW], 0.5, 0.5, ALU.mult, ALU.add)
                v.wait_ge(s_nr, g + 1)
                link(v.tensor_scalar(ne[:, :], nr[:, :], 1e-6, None, ALU.add))
                v.tensor_tensor(apb[:, :, :], ab[:, :, 0:H], ab[:, :, H:2 * H], ALU.mult)
                v.tensor_copy(out[:, :, 4 * D:TW], ab[:, :, 0:H])
                link(v.reciprocal(rn[:, :], ne[:, :]))
                link(v.tensor_tensor(heads(out[:, :, 0:2 * D]), heads(act_in[q][:, :, 0:2 * D]),
                                     over(rn.rearrange("p (t h) -> p t h", t=TILES)).broadcast_to((P, TILES, 2 * H, DH)), ALU.mult))
                v.tensor_tensor(heads(out[:, :, 3 * D:4 * D]), heads(act_in[q][:, :, 2 * D:3 * D]),
                                over(ab[:, :, H:2 * H]).broadcast_to((P, TILES, H, DH)), ALU.mult)
                v.tensor_tensor(heads(out[:, :, 2 * D:3 * D]), heads(out[:, :, D:2 * D]),
                                over(apb[:, :, :]).broadcast_to((P, TILES, H, DH)), ALU.mult).then_inc(s_out, 1)

            def unit(g, q, prev, following):
                n[0], n[1] = g, 0
                if following:
                    statistics(g + 1)
                if prev:
                    sums(g - 1)
                add_bias(g, q, 0)
                if following:
                    norm(g + 1)
                add_bias(g, q, 1)
                add_gate_bias(g, q, 0)
                if prev:
                    products(g - 1, 1 - q)
                add_bias(g, q, 2)
                add_bias(g, q, 3)
                add_gate_bias(g, q, 1)
                close()

            n[0], n[1] = -1, 0
            for k in range(CONV):
                m = v.tensor_tensor(wt[:, k, :], w[:, :], taps[:, k, :], ALU.mult)
            m.then_inc(s_wt, 1)
            link(v.tensor_scalar(bt[:, :], taps[:, 0, :], valid[:, 0:1], None, ALU.mult))
            for k in range(1, CONV):
                link(v.scalar_tensor_tensor(bt[:, :], taps[:, k, :], valid[:, k:k + 1], bt[:, :], ALU.mult, ALU.add))
            link(v.tensor_tensor(bt[:, :], bt[:, :], bias[:, :], ALU.mult))
            v.sem_inc(s_wt, 1)
            statistics(0)
            norm(0)
            close()
            run(v, unit)
            n[0], n[1] = GROUPS, 0
            sums(GROUPS - 1)
            products(GROUPS - 1, 1)


def delta_scan(nc, d, keep):
    ident = keep["ident"]
    HH = H // 2
    CH = 8
    with ExitStack() as ctx:
        def sb(name, shape, dt=F32):
            return ctx.enter_context(nc.sbuf_tensor("D_" + name, shape, dt))

        def pb(name, shape, dt=F32):
            return ctx.enter_context(nc.psum_tensor("D_" + name, shape, dt))

        sem = stage_semaphores(nc, ctx, "D_")

        rows = sb("rows", [P, 1 + S, TW])
        Sx = [sb(f"S{f}", [P, HH, DH, DH]) for f in range(2)]
        aS = [sb(f"aS{f}", [P, HH, DH, DH]) for f in range(2)]
        T1 = [sb(f"T1{f}", [P, HH, DH, DH]) for f in range(2)]
        T2 = sb("T2", [P, H, DH, DH]); sk = sb("sk", [P, HH * DH])
        U = [sb(f"U{f}", [P, HH, DH, DH]) for f in range(2)]
        de = [sb(f"de{f}", [P, HH * DH]) for f in range(2)]
        gs = sb("gs", [P, D]); gb = sb("gb", [P, D]); sums = sb("sums", [P, 2, H]); small = sb("small", [P, 6, H])
        A = sb("A", [P, D]); Bc = sb("Bc", [P, D]); nh = sb("nh", [P, H])
        po = pb("po", [P, 512]); ps = pb("ps", [P, 512])
        s_const = sem("const"); s_set = sem("set"); s_rows = sem("rows"); s_pad = sem("pad")
        s_t1 = [sem(f"t1{f}") for f in range(2)]; s_sk = [sem(f"sk{f}") for f in range(2)]
        s_as = [sem(f"as{f}") for f in range(2)]; s_de = [sem(f"de{f}") for f in range(2)]
        s_u = [sem(f"u{f}") for f in range(2)]; s_S = [sem(f"S{f}") for f in range(2)]
        s_t2 = sem("t2"); s_o = sem("o"); s_oc = sem("oc")
        s_sqr = sem("sqr"); s_n = sem("n"); s_var = sem("var"); s_rstd = sem("rstd"); s_y = sem("y"); s_sy = sem("sy")
        block = ctx.enter_context(nc.Block())
        NCONST = 32
        YC = 4

        def vec(t, c, f):
            x = rows[:, bass.ds(t + 1, 1), c * D + f * HH * DH:c * D + (f + 1) * HH * DH].rearrange("p o (h e) -> p (o h) e", h=HH)
            return x.rearrange("p h (o e) -> p h o e", o=1).broadcast_to((P, HH, DH, DH))

        @block.sync
        def _(sp):
            sp.dma_start(gs[:, :], d["l1_gs"].broadcast_to((P, D))).then_inc(s_const, 16)
            sp.dma_start(gb[:, :], d["l1_gb"].broadcast_to((P, D))).then_inc(s_const, 16)
            for c in range(S // CH):
                q = slice(c * CH, (c + 1) * CH)
                sp.dma_start(rows[:, 1 + c * CH:1 + (c + 1) * CH, :], d["s_rows"][:, q, :]).then_inc(s_rows, 16)
                sp.wait_ge(s_rows, 16 * (c + 1))
            for c in range(YC):
                sp.wait_ge(s_y, c + 1)
                q = slice(c * S // YC, (c + 1) * S // YC)
                sp.dma_start(d["s_y"][:, q, :], rows[:, 1 + c * S // YC:1 + (c + 1) * S // YC, 2 * D:3 * D]).then_inc(s_sy, 16)
            sp.wait_ge(s_sy, 16 * YC)

        @block.tensor
        def _(pe):
            pe.sem_inc(s_o, 1)

            def key_sum(dst, src):
                for e in range(DH):
                    m = pe.matmul(dst, ident[:, :], src.rearrange("p h d e -> p (h d) e")[:, :, e],
                                  start=(e == 0), stop=(e == DH - 1))
                return m

            def outputs(t):
                pe.wait_ge(s_t2, t + 1)
                pe.wait_ge(s_oc, t + 1)
                key_sum(po[:, 0:D], T2).then_inc(s_o, 1)

            with pe.Fori(0, S) as t:
                pe.wait_ge(s_t1[0], t + 1)
                key_sum(ps[:, 0:HH * DH], T1[0]).then_inc(s_sk[0], 1)
                outputs(t)
            outputs(S)

        @block.scalar
        def _(act):
            act.wait_ge(s_set, 2)
            act.sem_inc(s_oc, 1)
            with act.Fori(0, S) as t:
                for f in range(2):
                    act.wait_ge(s_t1[f], t + 1)
                    for h in range(HH):
                        at = 4 * D + f * HH + h
                        m = act.activation(aS[f][:, h, :, :].rearrange("p d e -> p (d e)"), Sx[f][:, h, :, :].rearrange("p d e -> p (d e)"),
                                           ACT.Copy, scale=rows[:, bass.ds(t + 1, 1), at:at + 1].rearrange("p o n -> p (o n)"))
                    m.then_inc(s_as[f], 1)
                act.wait_ge(s_o, t + 2)
                act.activation(rows[:, bass.ds(t, 1), 0:D].rearrange("p o n -> p (o n)"), po[:, 0:D], ACT.Copy).then_inc(s_oc, 1)
            act.wait_ge(s_o, S + 2)
            act.activation(rows[:, S, 0:D], po[:, 0:D], ACT.Copy).then_inc(s_oc, 1)
            act.wait_ge(s_oc, S + 2)
            for h in range(H):
                m = act.activation(rows[:, 1:, D + h * DH:D + (h + 1) * DH], rows[:, 1:, h * DH:(h + 1) * DH], ACT.Square,
                                   accum_out=sums[:, 1, h:h + 1])
            m.then_inc(s_sqr, 1)

        @block.gpsimd
        def _(pool):
            pool.memset(nh[:, :], -0.5).then_inc(s_set, 1)
            pool.wait_ge(s_set, 2)
            pool.wait_ge(s_var, 1)
            pool.tensor_tensor(small[:, 3, :], small[:, 2, :], nh[:, :], ALU.pow).then_inc(s_rstd, 1)

        @block.vector
        def _(v):
            v.memset(rows[:, 0, 0:D], 0.0).then_inc(s_set, 1)
            for f in range(2):
                v.memset(Sx[f][:, :, :, :], 0.0).then_inc(s_S[f], 1)
            v.wait_ge(s_set, 2)

            def query(t):
                v.wait_ge(s_o, t + 1)
                for f in range(2):
                    m = v.tensor_tensor(T2[:, f * HH:(f + 1) * HH, :, :], Sx[f][:, :, :, :], vec(t - 1, 0, f), ALU.mult)
                m.then_inc(s_t2, 1)

            with v.Fori(0, S // CH) as c:
                v.wait_ge(s_rows, c * 16 + 16)
                v.sem_inc(s_pad, 1)
                with v.Fori(0, CH) as j:
                    t = c * CH + j
                    for f in range(2):
                        v.wait_ge(s_S[f], t + 1)
                        v.tensor_tensor(T1[f][:, :, :, :], Sx[f][:, :, :, :], vec(t, 2, f), ALU.mult).then_inc(s_t1[f], 1)
                    query(t)
                    v.wait_ge(s_t1[1], t + 1)
                    v.tensor_reduce(sk[:, :], T1[1].rearrange("p h d e -> p (h d) e"), AX.X, ALU.add).then_inc(s_sk[1], 1)
                    for f in range(2):
                        v.wait_ge(s_sk[f], t + 1)
                        vb = rows[:, bass.ds(t + 1, 1), 3 * D + f * HH * DH:3 * D + (f + 1) * HH * DH].rearrange("p o n -> p (o n)")
                        v.tensor_tensor(de[f][:, :], vb, (ps[:, 0:HH * DH], sk[:, :])[f], ALU.subtract).then_inc(s_de[f], 1)
                    for f in range(2):
                        v.wait_ge(s_de[f], t + 1)
                        v.tensor_tensor(U[f][:, :, :, :], de[f].rearrange("p (h d o) -> p h d o", h=HH, o=1).broadcast_to((P, HH, DH, DH)),
                                        vec(t, 1, f), ALU.mult).then_inc(s_u[f], 1)
                    for f in range(2):
                        v.wait_ge(s_u[f], t + 1)
                        v.wait_ge(s_as[f], t + 1)
                        v.tensor_tensor(Sx[f][:, :, :, :], aS[f][:, :, :, :], U[f][:, :, :, :], ALU.add).then_inc(s_S[f], 1)
            for f in range(2):
                v.wait_ge(s_S[f], S + 1)
            query(S)
            n = [0]

            def link(ins):
                n[0] += 1
                ins.then_inc(s_n, 1)
                v.wait_ge(s_n, n[0])

            cnt = 1.0 / (S * DH)
            o4 = rows[:, 1:, 0:D].rearrange("p s (h e) -> p h s e", h=H)
            v.wait_ge(s_oc, S + 2)
            link(v.tensor_reduce(sums[:, 0, :], o4, AX.XY, ALU.add))
            mu, m2, ve, rstd, t0 = (small[:, k, :] for k in range(5))
            link(v.tensor_scalar(mu, sums[:, 0, :], cnt, None, ALU.mult))
            link(v.tensor_tensor(t0, mu, mu, ALU.mult))
            v.wait_ge(s_sqr, 1)
            link(v.scalar_tensor_tensor(m2, sums[:, 1, :], cnt, t0, ALU.mult, ALU.subtract))
            v.tensor_scalar(ve, m2, 1e-5, None, ALU.add).then_inc(s_var, 1)
            v.wait_ge(s_rstd, 1)
            v.wait_ge(s_const, NCONST)
            hd = lambda x: x.rearrange("p (h e) -> p h e", h=H)
            bc = lambda x: x.rearrange("p (h o) -> p h o", o=1).broadcast_to((P, H, DH))
            link(v.tensor_tensor(hd(A), hd(gs), bc(rstd), ALU.mult))
            link(v.tensor_tensor(hd(Bc), hd(A), bc(mu), ALU.mult))
            link(v.tensor_tensor(Bc[:, :], gb[:, :], Bc[:, :], ALU.subtract))
            for c in range(YC):
                q = slice(1 + c * S // YC, 1 + (c + 1) * S // YC)
                n4 = S // YC
                b3 = lambda x: x.rearrange("p (o n) -> p o n", o=1).broadcast_to((P, n4, D))
                link(v.tensor_tensor(rows[:, q, D:2 * D], rows[:, q, 0:D], b3(A), ALU.mult))
                v.tensor_tensor(rows[:, q, 2 * D:3 * D], rows[:, q, D:2 * D], b3(Bc), ALU.add).then_inc(s_y, 1)


XH, XD = 8, 64
XSCALE = XD ** -0.5
KEYS = 2 * S
XP = XH // 2
MASKED = -1e30


def latent_attention(nc, d, keep):
    ident = keep["ident"]
    with ExitStack() as ctx:
        def sb(name, shape, dt=F32):
            return ctx.enter_context(nc.sbuf_tensor("F_" + name, shape, dt))

        def pb(name, shape, dt=F32):
            return ctx.enter_context(nc.psum_tensor("F_" + name, shape, dt))

        sem = stage_semaphores(nc, ctx, "F_")

        wo = sb("wo", [P, D]); bo = sb("bo", [P, D])
        wqT = sb("wqT", [XD, XH, D]); wkT = sb("wkT", [XD, XH, D]); wvT = sb("wvT", [XD, XH, D]); wout = sb("wout", [XD, XH, D])
        qk = sb("qk", [P, XH, D]); vo = sb("vo", [P, XH, D])
        par = sb("par", [P, 5])
        gg = sb("gg", [P, 2])
        neghalf = sb("neghalf", [P, TILES])
        yi = sb("yi", [P, TILES, D]); gi = sb("gi", [P, TILES, D]); xi = sb("xi", [P, TILES, D]); ci = sb("ci", [P, TILES, D])
        mi = sb("mi", [P, GB, S], mybir.dt.uint8)
        zz = sb("zz", [P, TILES, D]); zT = sb("zT", [P, GTOK]); xb = sb("xb", [P, TILES, D]); r = sb("r", [P, TILES, D])
        ln = sb("ln", [P, TILES, D]); cn = sb("cn", [P, TILES, D]); x5 = sb("x5", [P, TILES, D]); r5 = sb("r5", [P, TILES, D])
        latT = sb("latT", [P, GTOK])
        pen, x4, kvT, kvN, qh = ([sb(f"{n}{q}", shape) for q in range(2)] for n, shape in (
            ("pen", [P, GB, S]), ("x4_", [P, TILES, D]), ("kvT", [P, GB, 2, S]), ("kvN", [P, GB, D]), ("qh", [P, XP, GB, 2, S])))
        CN, X4, LN, X5 = range(4)
        st = sb("st", [P, 4, TILES, 6]); mv = sb("mv", [P, 4, TILES, 2]); ve = sb("ve", [P, 4, TILES]); rs = sb("rs", [P, 4, TILES])
        e = sb("e", [P, 2, XP, KEYS]); nm = sb("nm", [P, 2, XP]); den = sb("den", [P, 2, XP]); rd = sb("rd", [P, 2, XP])
        en = sb("en", [P, 2, XP, KEYS]); pT = sb("pT", [P, 2, XP, P]);
        qkh = sb("qkh", [P, XH, D], F32R); qkl = sb("qkl", [P, XH, D], F32R)
        latTh = sb("latTh", [P, GTOK], F32R); latTl = sb("latTl", [P, GTOK], F32R)
        gh = sb("gh", [P, XH, GB, S])
        pw = pb("pw", [P, 2, 512]); sc = pb("sc", [P, 2, 512]); tp = pb("tp", [P, XP, P]); pg = pb("pg", [P, 2, 512])
        yy = pb("yy", [P, TILES, D])

        s_const = sem("const"); s_set = sem("set"); s_w = sem("w_psum"); s_wc = sem("w"); s_gg = sem("gg")
        s_in = sem("loaded"); s_infree = sem("in_free"); s_pen = sem("pen")
        s_zz = sem("zz"); s_zTp = sem("zT_psum"); s_zT = sem("zT"); s_y = sem("y_psum"); s_r = sem("r"); s_dv = sem("dve_step"); s_turn = sem("turn")
        s_var = [sem(f"var{k}") for k in range(4)]; s_rstd = [sem(f"rstd{k}") for k in range(4)]
        s_ln = sem("ln"); s_cn = sem("cn")
        s_lp = sem("lat_psum"); s_lT = sem("latT"); s_cp = sem("ctx_psum"); s_kc = sem("kvT_ctx"); s_kl = sem("kvT_lat")
        s_kp = sem("kv_psum"); s_kvN = sem("kvN")
        s_qp = sem("q_psum"); s_qa = sem("q_even"); s_qd = sem("q_odd")
        s_sc = sem("scores"); s_nm = sem("rowmax"); s_exp = sem("exp"); s_rd = sem("rden"); s_en = sem("normalised")
        s_tp = sem("pT_psum"); s_pT = sem("pT"); s_g = sem("g_psum"); s_gh = sem("gh"); s_o = sem("o_psum"); s_r5 = sem("r5"); s_x5 = sem("x5"); s_st = sem("stored")
        s_mxp = sem("masked"); s_parts = sem("weights_split"); s_ls = sem("latT_split")
        block = ctx.enter_context(nc.Block())
        y_g = d["s_y"].rearrange("(g t q) s d -> g (q s) t d", t=TILES, q=2)
        c_g = d["ctx"].rearrange("(g t q) s d -> g (q s) t d", t=TILES, q=2)
        m_g = d["mask"].rearrange("(o g b) s -> g o b s", o=1, b=GB)
        loads = [(wo[:, :], d["l1_wo"]), (bo[:, :], d["l1_bo"].broadcast_to((P, D))), (wqT[:, :, :], d["x_wqT"]),
                 (wkT[:, :, :], d["x_wkT"]), (wvT[:, :, :], d["x_wvT"]), (wout[:, :, :], d["x_wout"]),
                 (par[:, 0:4], d["x_par"]), (par[:, 4:5], d["x_gate"].broadcast_to((P, 1)))]
        NCONST = 16 * len(loads)
        NLN = 4

        def schedule(eng, unit):
            unit(0, 0, False, True)
            with eng.Fori(0, (GROUPS - 2) // 2) as i:
                unit(i * 2 + 1, 1, True, True)
                unit(i * 2 + 2, 0, True, True)
            unit(GROUPS - 1, 1, True, False)

        @block.sync
        def _(sp):
            for dst, src in loads:
                sp.dma_start(dst, src).then_inc(s_const, 16)

            def load(g):
                sp.wait_ge(s_infree, g + 1)
                sp.dma_start(yi[:, :, :], y_g[g]).then_inc(s_in, 16)
                sp.dma_start(gi[:, :, :], d["s_gate"][g]).then_inc(s_in, 16)
                sp.dma_start(xi[:, :, :], d["s_x3"][g]).then_inc(s_in, 16)
                sp.dma_start(ci[:, :, :], c_g[g]).then_inc(s_in, 16)
                sp.dma_start(mi[:, :, :], m_g[g].broadcast_to((P, GB, S))).then_inc(s_in, 16)

            def store(g):
                sp.wait_ge(s_x5, g + 1)
                sp.dma_start(d["s_x5"][g], x5[:, :, :]).then_inc(s_st, 16)

            load(0)
            load(1)
            load(2)
            with sp.Fori(0, GROUPS - 3) as g:
                load(g + 3)
                store(g)
            store(GROUPS - 3)
            store(GROUPS - 2)
            store(GROUPS - 1)
            sp.wait_ge(s_st, GROUPS * 16 + 1)

        @block.tensor
        def _(pe):
            pe.wait_ge(s_const, NCONST)
            for c in range(4):
                a, b = ((wqT, wkT), (wvT, wout))[c // 2]
                if c >= 2:
                    pe.wait_ge(s_wc, c - 1)
                for h in range(4):
                    hh = 4 * (c % 2) + h
                    m = pe.matmul(pw[:, c % 2, h * D:(h + 1) * D], a[:, hh, :], b[:, hh, :], start=True, stop=True)
                m.then_inc(s_w, 1)
            pe.wait_ge(s_wc, 4)
            pe.wait_ge(s_parts, 2)

            def flat(x):
                return x.rearrange("p a s -> p (a s)")

            def gated(g):
                pe.wait_ge(s_zz, g + 1)
                pe.wait_ge(s_kvN, g + 1)
                for t in range(TILES):
                    m = pe.transpose(pw[:, 0, t * P:(t + 1) * P], zz[:, t, :], ident[:, :])
                m.then_inc(s_zTp, 1)

            def project(g):
                pe.wait_ge(s_zT, g + 1)
                for t in range(TILES):
                    m = pe.matmul(pw[:, 1, t * P:(t + 1) * P], zT[:, t * P:(t + 1) * P], wo[:, :], start=True, stop=True)
                m.then_inc(s_y, 1)

            def context(g):
                pe.wait_ge(s_cn, g + 1)
                for t in range(TILES):
                    m = pe.transpose(pw[:, 0, t * P:(t + 1) * P], cn[:, t, :], ident[:, :])
                m.then_inc(s_cp, 1)

            def latents(g):
                pe.wait_ge(s_ln, g + 1)
                pe.wait_ge(s_r, g + 1)
                for t in range(TILES):
                    m = pe.transpose(pw[:, 1, t * P:(t + 1) * P], ln[:, t, :], ident[:, :])
                m.then_inc(s_lp, 1)

            def keys(g, q):
                pe.wait_ge(s_qa, g * XP + XP)
                pe.wait_ge(s_qd, g * XP + XP)
                for b in range(GB):
                    m = pe.transpose(pw[:, b // 4, (b % 4) * P:(b % 4 + 1) * P], flat(kvT[q][:, b, :, :]), ident[:, :])
                m.then_inc(s_kp, 1)

            def queries(g, h):
                if h == 0:
                    pe.wait_ge(s_kc, g + 1)
                    pe.wait_ge(s_kl, g + 1)
                    pe.wait_ge(s_ls, g + 1)
                if h >= 2:
                    pe.wait_ge(s_qa if h % 2 == 0 else s_qd, g * XP + h // 2)
                for n, (w, x) in enumerate(((qkh, latTh), (qkl, latTh), (qkh, latTl))):
                    m = pe.matmul(pw[:, h % 2, :], w[:, h, :], x[:, :], start=(n == 0), stop=(n == 2))
                m.then_inc(s_qp, 1)

            def scores(g, q, b):
                if b == 0:
                    pe.wait_ge(s_qa, g * XP + XP)
                    pe.wait_ge(s_qd, g * XP + XP)
                pe.wait_ge(s_exp, g * GB + b + 1)
                for j in range(XP):
                    m = pe.matmul(sc[:, b % 2, j * KEYS:(j + 1) * KEYS], flat(qh[q][:, j, b, :, :]),
                                  flat(kvT[q][:, b, :, :]), start=True, stop=True)
                m.then_inc(s_sc, 1)

            def transposes(g, b):
                pe.wait_ge(s_en, g * GB + b + 3)
                pe.wait_ge(s_pT, g * GB + b + 1)
                for j in range(XP):
                    m = pe.transpose(tp[:, j, :], en[:, b % 2, j, :], ident[:, :])
                m.then_inc(s_tp, 1)

            def weighted(g, q, b):
                pe.wait_ge(s_pT, g * GB + b + 2)
                pe.wait_ge(s_gh, g * GB + b + 1)
                if b == 0:
                    pe.wait_ge(s_kvN, g + 2)
                pe.matmul(pg[:, b % 2, :], kvN[q][:, b, :], pT[:, b % 2, :, :], start=True, stop=True).then_inc(s_g, 1)

            def back(g, tiles):
                if 0 in tiles:
                    pe.wait_ge(s_gh, g * GB + GB + 2)
                    pe.wait_ge(s_r5, g + 1)
                for t in tiles:
                    for h in range(XH):
                        m = pe.matmul(yy[:, t, :], flat(gh[:, h, 2 * t:2 * t + 2, :]), vo[:, h, :],
                                      start=(h == 0), stop=(h == XH - 1))
                m.then_inc(s_o, 1)

            def unit(g, q, behind, ahead):
                for b in range(GB):
                    transposes(g, b)
                    if b + 2 < GB:
                        scores(g, q, b + 2)
                    elif ahead and b == GB - 1:
                        scores(g + 1, 1 - q, 1)
                    if ahead and b in (5, 6):
                        queries(g + 1, 4 * (b - 5))
                        queries(g + 1, 4 * (b - 5) + 1)
                    if behind and b < 2:
                        back(g - 1, (2 * b, 2 * b + 1))
                    weighted(g, q, b)
                    if ahead and b in (5, 6):
                        queries(g + 1, 4 * (b - 5) + 2)
                        queries(g + 1, 4 * (b - 5) + 3)
                    if ahead and b == 6:
                        scores(g + 1, 1 - q, 0)
                    if ahead:
                        if b == 0:
                            gated(g + 1)
                        if b == 1:
                            project(g + 1)
                        if b == 3:
                            context(g + 1)
                        if b == 4:
                            latents(g + 1)
                        if b == 7:
                            keys(g + 1, 1 - q)

            gated(0)
            project(0)
            context(0)
            latents(0)
            for h in range(XH):
                queries(0, h)
            keys(0, 0)
            scores(0, 0, 0)
            scores(0, 0, 1)
            schedule(pe, unit)
            back(GROUPS - 1, (0, 1))
            back(GROUPS - 1, (2, 3))

        @block.scalar
        def _(act):
            act.wait_ge(s_const, NCONST)
            act.wait_ge(s_set, 1)
            for c in range(4):
                dst = (qk, vo)[c // 2]
                act.wait_ge(s_w, c + 1)
                act.activation(dst[:, 4 * (c % 2):4 * (c % 2) + 4, :], pw[:, c % 2, :], ACT.Copy,
                               scale=XSCALE if c < 2 else 1.0).then_inc(s_wc, 1)
            act.sem_inc(s_pT, 1)
            act.sem_inc(s_gh, 2)
            act.sem_inc(s_exp, 2)
            act.sem_inc(s_kvN, 1)

            def by_seq(x):
                return x.rearrange("p (b s) -> p b s", s=S)

            def gated(g):
                act.wait_ge(s_zTp, g + 1)
                act.activation(zT[:, :], pw[:, 0, :], ACT.Copy).then_inc(s_zT, 1)

            def context(g, q):
                act.wait_ge(s_cp, g + 1)
                act.activation(kvT[q][:, :, 0, :], by_seq(pw[:, 0, :]), ACT.Identity,
                               bias=par[:, 1:2], scale=par[:, 0:1]).then_inc(s_kc, 1)

            def latents(g, q):
                act.wait_ge(s_lp, g + 1)
                act.activation(latTh[:, :], pw[:, 1, :], ACT.Identity, bias=par[:, 3:4], scale=par[:, 2:3])
                act.activation(latT[:, :], pw[:, 1, :], ACT.Identity, bias=par[:, 3:4], scale=par[:, 2:3]).then_inc(s_lT, 1)
                act.wait_ge(s_gg, 1)
                act.activation(kvT[q][:, :, 1, :], by_seq(pw[:, 1, :]), ACT.Identity,
                               bias=gg[:, 1:2], scale=gg[:, 0:1]).then_inc(s_kl, 1)

            def keys(g, q):
                act.wait_ge(s_kp, g + 1)
                act.activation(kvN[q].rearrange("p b n -> p (b n)"), pw.rearrange("p a n -> p (a n)"), ACT.Copy).then_inc(s_kvN, 1)

            def queries(g, q, j):
                act.wait_ge(s_qp, g * XH + 2 * j + 1)
                act.activation(qh[q][:, j, :, 0, :], by_seq(pw[:, 0, :]), ACT.Copy).then_inc(s_qa, 1)

            def exps(g, b):
                act.wait_ge(s_nm, g * GB + b + 1)
                act.wait_ge(s_en, g * GB + b + 1)
                for j in range(XP):
                    m = act.activation(e[:, b % 2, j, :], sc[:, b % 2, j * KEYS:(j + 1) * KEYS], ACT.Exp,
                                       bias=nm[:, b % 2, j:j + 1], accum_out=den[:, b % 2, j:j + 1])
                m.then_inc(s_exp, 1)

            def evacuate(g, b):
                act.wait_ge(s_tp, g * GB + b + 3)
                act.wait_ge(s_g, g * GB + b + 1)
                act.activation(pT[:, b % 2, :, :], tp[:, :, :], ACT.Copy).then_inc(s_pT, 1)

            def outputs(g, b):
                act.wait_ge(s_g, g * GB + b + 3)
                if b in (0, 4):
                    act.wait_ge(s_o, g * 2 + b // 4 + 1)
                act.activation(gh[:, :, b, :], pg[:, b % 2, :].rearrange("p (h s) -> p h s", s=S), ACT.Copy).then_inc(s_gh, 1)

            def unit(g, q, behind, ahead):
                for b in range(GB):
                    evacuate(g, b)
                    if ahead and b in (5, 6):
                        queries(g + 1, 1 - q, 2 * (b - 5))
                    if b + 2 < GB:
                        exps(g, b + 2)
                    elif ahead and b == GB - 1:
                        exps(g + 1, 1)
                    outputs(g, b)
                    if ahead and b in (5, 6):
                        queries(g + 1, 1 - q, 2 * (b - 5) + 1)
                    if ahead and b == 6:
                        exps(g + 1, 0)
                    if ahead:
                        if b == 0:
                            gated(g + 1)
                        if b == 3:
                            context(g + 1, 1 - q)
                        if b == 4:
                            latents(g + 1, 1 - q)
                        if b == 7:
                            keys(g + 1, 1 - q)

            act.sem_inc(s_g, 2)
            act.sem_inc(s_o, 2)
            gated(0)
            context(0, 0)
            latents(0, 0)
            for j in range(XP):
                queries(0, 0, j)
            keys(0, 0)
            exps(0, 0)
            exps(0, 1)
            schedule(act, unit)

        @block.gpsimd
        def _(pool):
            pool.memset(neghalf[:, :], -0.5).then_inc(s_set, 1)
            pool.wait_ge(s_set, 1)

            def root(g, k):
                pool.wait_ge(s_var[k], g + 1)
                pool.tensor_tensor(rs[:, k, :], ve[:, k, :], neghalf[:, :], ALU.pow).then_inc(s_rstd[k], 1)

            for g in range(2):
                for k in (CN, X4, LN):
                    root(g, k)
            with pool.Fori(1, GROUPS - 1) as g:
                root(g + 1, CN)
                root(g + 1, X4)
                root(g - 1, X5)
                root(g + 1, LN)
            root(GROUPS - 2, X5)
            root(GROUPS - 1, X5)

        @block.vector
        def _(v):
            v.wait_ge(s_const, NCONST)
            v.tensor_scalar(gg[:, :], par[:, 2:4], par[:, 4:5], None, ALU.mult).then_inc(s_gg, 1)
            v.sem_inc(s_infree, 1)
            v.sem_inc(s_st, 1)
            v.sem_inc(s_r5, 1)
            v.sem_inc(s_en, 2)
            v.sem_inc(s_tp, 2)
            STEPS = 16
            n = [0, 0]

            def link(ins):
                n[1] += 1
                assert n[1] <= STEPS
                ins.then_inc(s_dv, 1)
                v.wait_ge(s_dv, (n[0] + 1) * STEPS + n[1])

            def close():
                if n[1] < STEPS:
                    v.sem_inc(s_dv, STEPS - n[1])

            def stats(src, k):
                for t in range(TILES):
                    m = v.bn_stats(st[:, k, t, :], src[:, t, :])
                link(m)
                v.sem_inc(s_turn, 1)
                for t in range(TILES):
                    m = v.bn_aggr(mv[:, k, t, :], st[:, k, t, :])
                link(m)
                v.tensor_scalar(ve[:, k, :], mv[:, k, :, 1], LN_EPS, None, ALU.add).then_inc(s_var[k], 1)

            def norm(g, dst, src, k):
                v.wait_ge(s_rstd[k], g + 1)
                for t in range(TILES):
                    m = v.tensor_scalar(dst[:, t, :], src[:, t, :], mv[:, k, t, 0:1], rs[:, k, t:t + 1], ALU.subtract, ALU.mult)
                return m

            def enter(g, q):
                v.wait_ge(s_in, g * 80 + 80)
                v.tensor_tensor(zz[:, :, :], yi[:, :, :], gi[:, :, :], ALU.mult).then_inc(s_zz, 1)
                v.tensor_scalar(pen[q][:, :, :], mi[:, :, :], MASKED, None, ALU.mult).then_inc(s_pen, 1)
                v.tensor_tensor(xb[:, :, :], xi[:, :, :], bo.rearrange("p (o n) -> p o n", o=1).broadcast_to((P, TILES, D)), ALU.add)

            def residual(g):
                v.wait_ge(s_y, g + 1)
                m = v.tensor_tensor(r[:, :, :], pw[:, 1, :].rearrange("p (t n) -> p t n", t=TILES), xb[:, :, :], ALU.add)
                m.then_inc(s_r, 1)
                v.wait_ge(s_r, g + 1)
                stats(r, X4)

            def rowmax(g, q, b):
                v.wait_ge(s_sc, g * GB + b + 1)
                if b == 0:
                    v.wait_ge(s_pen, g + 1)
                s3 = sc[:, b % 2, :].rearrange("p (j k) -> p j k", j=XP)
                v.tensor_tensor(s3[:, :, 0:S], s3[:, :, 0:S],
                                pen[q][:, b:b + 1, :].broadcast_to((P, XP, S)), ALU.add).then_inc(s_mxp, 1)
                v.wait_ge(s_mxp, g * GB + b + 1)
                v.wait_ge(s_exp, g * GB + b + 1)
                v.tensor_reduce(nm[:, b % 2, :], s3, AX.X, ALU.max, negate=True).then_inc(s_nm, 1)

            def normalise(g, b):
                v.wait_ge(s_exp, g * GB + b + 3)
                v.reciprocal(rd[:, b % 2, :], den[:, b % 2, :]).then_inc(s_rd, 1)
                v.wait_ge(s_rd, g * GB + b + 1)
                v.wait_ge(s_tp, g * GB + b + 1)
                v.tensor_tensor(en[:, b % 2, :, :], e[:, b % 2, :, :],
                                rd[:, b % 2, :].rearrange("p (j o) -> p j o", o=1).broadcast_to((P, XP, KEYS)),
                                ALU.mult).then_inc(s_en, 1)

            def queries(g, q, j):
                v.wait_ge(s_qp, g * XH + 2 * j + 2)
                v.tensor_copy(qh[q][:, j, :, 1, :], pw[:, 1, :].rearrange("p (b s) -> p b s", s=S)).then_inc(s_qd, 1)

            def latents(g):
                v.wait_ge(s_lT, g + 1)
                v.tensor_tensor(latTl[:, :], latT[:, :], latTh[:, :], ALU.subtract).then_inc(s_ls, 1)

            def back_stats(g, q):
                v.wait_ge(s_o, g * 2 + 4)
                v.tensor_tensor(r5[:, :, :], yy[:, :, :], x4[q][:, :, :], ALU.add).then_inc(s_r5, 1)
                v.wait_ge(s_r5, g + 2)
                stats(r5, X5)

            def back_norm(g):
                v.wait_ge(s_st, g * 16 + 1)
                norm(g, x5, r5, X5).then_inc(s_x5, 1)

            def front(g, q, b):
                if b == 0:
                    enter(g, q)
                    stats(ci, CN)
                if b == 1:
                    norm(g, cn, ci, CN).then_inc(s_cn, 1)
                    v.wait_ge(s_cn, g + 1)
                    v.sem_inc(s_infree, 1)
                    residual(g)
                if b == 2:
                    link(norm(g, x4[q], r, X4))
                    stats(x4[q], LN)
                if b == 3:
                    norm(g, ln, x4[q], LN).then_inc(s_ln, 1)

            def unit(g, q, behind, ahead):
                n[0], n[1] = g, 0
                for b in range(GB):
                    if b + 1 < GB:
                        normalise(g, b + 1)
                    elif ahead:
                        normalise(g + 1, 0)
                    if b + 2 < GB:
                        rowmax(g, q, b + 2)
                    elif ahead and b == GB - 1:
                        rowmax(g + 1, 1 - q, 1)
                    if ahead and b in (5, 6):
                        queries(g + 1, 1 - q, 2 * (b - 5))
                        queries(g + 1, 1 - q, 2 * (b - 5) + 1)
                    if ahead and b == 6:
                        rowmax(g + 1, 1 - q, 0)
                    if behind and b == 2:
                        back_stats(g - 1, 1 - q)
                    if ahead:
                        front(g + 1, 1 - q, b)
                    if behind and b == 3:
                        back_norm(g - 1)
                    if ahead and b == 4:
                        latents(g + 1)
                close()

            v.wait_ge(s_wc, 2)
            v.tensor_copy(qkh[:, :, :], qk[:, :, :]).then_inc(s_parts, 1)
            v.wait_ge(s_parts, 1)
            v.tensor_tensor(qkl[:, :, :], qk[:, :, :], qkh[:, :, :], ALU.subtract).then_inc(s_parts, 1)
            n[0], n[1] = -1, 0
            for b in range(GB):
                front(0, 0, b)
            latents(0)
            for j in range(XP):
                queries(0, 0, j)
            close()
            rowmax(0, 0, 0)
            rowmax(0, 0, 1)
            normalise(0, 0)
            schedule(v, unit)
            n[0], n[1] = GROUPS, 0
            back_stats(GROUPS - 1, 1)
            back_norm(GROUPS - 1)


E8, FF = 8, 256
EC = FF // P
NG4, NL = 4, 2
LOOPS = 2
RMS_EPS, TOP_EPS = 1e-6, 1e-9


def experts(nc, d, keep):
    ident = keep["ident"]
    with ExitStack() as ctx:
        def sb(name, shape, dt=F32):
            return ctx.enter_context(nc.sbuf_tensor("G_" + name, shape, dt))

        def pb(name, shape, dt=F32):
            return ctx.enter_context(nc.psum_tensor("G_" + name, shape, dt))

        sem = stage_semaphores(nc, ctx, "G_")

        w1 = sb("w1", [P, E8 * EC, P]); w2 = sb("w2", [P, E8 * EC, D]); wr = sb("wr", [P, NG4 + E8]); nw = sb("nw", [P, 1])
        neghalf = sb("neghalf", [P, TILES]); tri = sb("tri", [P, NG4, NG4])
        xin = [sb(f"xin{g}", [P, TILES, D]) for g in range(2)]; z = [sb(f"z{g}", [P, TILES, D]) for g in range(2)]
        zn = sb("zn", [P, TILES, D]); acc = sb("acc", [P, TILES, D]); r = sb("r", [P, TILES, D]); junk = sb("junk", [P, TILES, D])
        ss = sb("ss", [P, TILES]); ve = sb("ve", [P, TILES]); rs = sb("rs", [P, TILES]); vt = sb("vt", [P, TILES]); rt = sb("rt", [P, TILES])
        st = sb("st", [P, TILES, 6]); mv = sb("mv", [P, TILES, 2]); out = sb("out", [P, TILES, D])
        w1h = sb("w1h", [P, E8 * EC, P], F32R); w1l = sb("w1l", [P, E8 * EC, P], F32R)
        znTh, znTl = ([sb(f"znT{part}{g}", [P, GTOK], F32R) for g in range(2)] for part in "hl")
        znT = [sb(f"znT{g}", [P, GTOK]) for g in range(2)]; hT = sb("hT", [P, E8 * EC, GTOK])
        lg = sb("lg", [P, TILES, 12]); ex = sb("ex", [P, TILES, 12]); pr = sb("pr", [P, TILES, 12])
        t4 = sb("t4", [P, 8, TILES, NG4]); t1 = sb("t1", [P, 4, TILES]); cmp = sb("cmp", [P, TILES, NG4, NG4])
        ceq = sb("ceq", [P, TILES, NG4, NG4]); s1 = sb("s1", [P, TILES, NG4, NL]); comb = [sb(f"comb{g}", [P, TILES, E8]) for g in range(2)]
        px = pb("px", [P, 2, 512]); ph = pb("ph", [P, 4, 512]); py = pb("py", [P, 2, TILES, D])

        s_const = sem("const"); s_set = sem("set")
        s_x = [sem(f"x{g}_loaded") for g in range(2)]; s_xfree = [sem(f"x{g}_free") for g in range(2)]
        s_z = sem("z"); s_sq = sem("sq"); s_var = sem("var"); s_rstd = sem("rstd"); s_vt = sem("tail_var"); s_rt = sem("tail_rstd")
        s_zn = sem("zn"); s_znp = sem("zn_psum"); s_znT = sem("znT"); s_split = sem("split"); s_w1 = sem("w1_split")
        s_lg = sem("logits"); s_sub = sem("sub"); s_ex = sem("ex"); s_h = sem("h_psum"); s_hT = sem("hT")
        s_y = sem("y_psum"); s_acc = sem("acc")
        s_dv = sem("dve_step"); s_turn = sem("turn"); s_out = sem("out"); s_st = sem("stored")
        block = ctx.enter_context(nc.Block())
        o_g = d["out"].rearrange("(g t q) s d -> g (q s) t d", t=TILES, q=2)
        loads = [(w1[:, :, :], d["m_w1"]), (w2[:, :, :], d["m_w2"]), (wr[:, :], d["m_wr"]), (nw[:, :], d["m_nw"])]
        NCONST = 16 * len(loads)
        NC = E8 * EC
        PAIRS = GROUPS // 2
        AHEAD = 4

        def schedule(eng, one_pass):
            one_pass(0, 0, False, True, 0)
            with eng.Fori(0, PAIRS - 1) as i:
                for p in (1, 2, 3, 4):
                    one_pass(i * 4 + p, p % 4, p >= 3, True, i * 2 + (p - 3))
            i = PAIRS - 1
            for p in (1, 2, 3):
                one_pass(i * 4 + p, p, p == 3, p < 3, i * 2)

        @block.sync
        def _(sp):
            for dst, src in loads:
                sp.dma_start(dst, src).then_inc(s_const, 16)
            for g in range(2):
                sp.dma_start(xin[g][:, :, :], d["s_x5"][g]).then_inc(s_x[g], 16)
            with sp.Fori(0, PAIRS - 1) as i:
                for g in range(2):
                    sp.wait_ge(s_xfree[g], i + 1)
                    sp.dma_start(xin[g][:, :, :], d["s_x5"][i * 2 + 2 + g]).then_inc(s_x[g], 16)
                    sp.wait_ge(s_out, i * 2 + g + 1)
                    sp.dma_start(o_g[i * 2 + g], out[:, :, :]).then_inc(s_st, 16)
            for g in range(2):
                sp.wait_ge(s_out, GROUPS - 1 + g)
                sp.dma_start(o_g[GROUPS - 2 + g], out[:, :, :]).then_inc(s_st, 16)
            sp.wait_ge(s_st, GROUPS * 16 + 1)

        @block.tensor
        def _(pe):
            pe.wait_ge(s_const, NCONST)
            pe.wait_ge(s_w1, 2)

            def transposes(k):
                pe.wait_ge(s_zn, k + 1)
                for t in range(TILES):
                    m = pe.transpose(px[:, 0, t * P:(t + 1) * P], zn[:, t, :], ident[:, :])
                m.then_inc(s_znp, 1)

            def logits(k, q):
                pe.wait_ge(s_znT, k + 1)
                for t in range(TILES):
                    m = pe.matmul(px[:, 1, 12 * t:12 * t + 12], znT[q][:, t * P:(t + 1) * P], wr[:, :], start=True, stop=True)
                m.then_inc(s_lg, 1)

            def up(k, q, c):
                if c == 0:
                    pe.wait_ge(s_split, k + 1)
                pe.wait_ge(s_hT, k * NC + c + 1)
                for n, (a, b) in enumerate(((w1h, znTh), (w1l, znTh), (w1h, znTl))):
                    m = pe.matmul(ph[:, c % 4, :], a[:, c, :], b[q][:, :], start=(n == 0), stop=(n == 2))
                m.then_inc(s_h, 1)

            def down(k, ee):
                pe.wait_ge(s_hT, k * NC + 2 * ee + 2 + AHEAD)
                pe.wait_ge(s_acc, k * E8 + ee + 1)
                for t in range(TILES):
                    for f in range(EC):
                        m = pe.matmul(py[:, ee % 2, t, :], hT[:, 2 * ee + f, t * P:(t + 1) * P], w2[:, 2 * ee + f, :],
                                      start=(f == 0), stop=(f == EC - 1))
                m.then_inc(s_y, 1)

            def one_pass(k, p, tail, following, g):
                q = p % 2
                for c in range(AHEAD, NC + 4):
                    if c < NC:
                        up(k, q, c)
                    elif following and c - NC < AHEAD:
                        up(k + 1, 1 - q, c - NC)
                    if c >= 5 and c % 2 == 1:
                        ee = (c - 5) // 2
                        down(k, ee)
                        if following and ee == 4:
                            transposes(k + 1)
                        if following and ee == 5:
                            logits(k + 1, 1 - q)

            transposes(0)
            logits(0, 0)
            for c in range(AHEAD):
                up(0, 0, c)
            schedule(pe, one_pass)

        @block.scalar
        def _(act):
            act.wait_ge(s_const, NCONST)
            act.sem_inc(s_hT, AHEAD)
            act.sem_inc(s_y, E8)

            def squares(k, q):
                act.wait_ge(s_z, k + 1)
                for t in range(TILES):
                    m = act.activation(junk[:, t, :], z[q][:, t, :], ACT.Square, accum_out=ss[:, t:t + 1])
                m.then_inc(s_sq, 1)

            def evacuate(k, q):
                act.wait_ge(s_znp, k + 1)
                act.activation(znT[q][:, :], px[:, 0, :], ACT.Copy, scale=nw[:, :]).then_inc(s_znT, 1)

            def exponentials(k):
                act.wait_ge(s_sub, k + 1)
                act.activation(ex[:, :, :], lg[:, :, :], ACT.Exp).then_inc(s_ex, 1)

            def one_pass(k, p, tail, following, g):
                q = p % 2
                for c in range(NC):
                    act.wait_ge(s_h, k * NC + c + 1)
                    if c % 2 == 0:
                        act.wait_ge(s_y, k * E8 + c // 2 + 1)
                    act.activation(hT[:, c, :], ph[:, c % 4, :], ACT.Silu).then_inc(s_hT, 1)
                    if following and c == 6 + 2 * tail:
                        squares(k + 1, 1 - q)
                    if following and c == 12 + 2 * tail:
                        evacuate(k + 1, 1 - q)
                if following:
                    exponentials(k + 1)

            squares(0, 0)
            evacuate(0, 0)
            exponentials(0)
            schedule(act, one_pass)

        @block.gpsimd
        def _(pool):
            pool.memset(neghalf[:, :], -0.5).then_inc(s_set, 1)
            pool.memset(tri[:, :, :], 0.0).then_inc(s_set, 1)
            pool.wait_ge(s_set, 2)
            for g in range(1, NG4):
                pool.memset(tri[:, g, 0:g], 1.0).then_inc(s_set, 1)

            def head(k):
                pool.wait_ge(s_var, k + 1)
                pool.tensor_tensor(rs[:, :], ve[:, :], neghalf[:, :], ALU.pow).then_inc(s_rstd, 1)

            def tail_root(g):
                pool.wait_ge(s_vt, g + 1)
                pool.tensor_tensor(rt[:, :], vt[:, :], neghalf[:, :], ALU.pow).then_inc(s_rt, 1)

            def one_pass(k, p, tail, following, g):
                if tail:
                    tail_root(g)
                if following:
                    head(k + 1)

            head(0)
            schedule(pool, one_pass)
            tail_root(GROUPS - 1)

        @block.vector
        def _(v):
            v.wait_ge(s_const, NCONST)
            v.wait_ge(s_set, 2 + NG4 - 1)
            v.tensor_copy(w1h[:, :, :], w1[:, :, :]).then_inc(s_w1, 1)
            v.wait_ge(s_w1, 1)
            v.tensor_tensor(w1l[:, :, :], w1[:, :, :], w1h[:, :, :], ALU.subtract).then_inc(s_w1, 1)
            v.sem_inc(s_acc, 2)
            v.sem_inc(s_st, 1)
            STEPS = 20
            n = [0, 0]

            def link(ins):
                n[1] += 1
                assert n[1] <= STEPS
                ins.then_inc(s_dv, 1)
                v.wait_ge(s_dv, (n[0] + 1) * STEPS + n[1])

            def close():
                if n[1] < STEPS:
                    v.sem_inc(s_dv, STEPS - n[1])

            def b4(x):
                return x.rearrange("p (t o) -> p t o", o=1).broadcast_to((P, TILES, NG4))

            def take(k, q, loop, at):
                if loop == 0:
                    v.wait_ge(s_x[q], at)
                    v.tensor_copy(z[q][:, :, :], xin[q][:, :, :]).then_inc(s_z, 1)
                else:
                    v.sem_inc(s_z, 1)

            def variance(k):
                v.wait_ge(s_sq, k + 1)
                v.tensor_scalar(ve[:, :], ss[:, :], 1.0 / D, RMS_EPS, ALU.mult, ALU.add).then_inc(s_var, 1)

            def scaled(k, q):
                v.wait_ge(s_rstd, k + 1)
                v.wait_ge(s_z, k + 1)
                for t in range(TILES):
                    m = v.tensor_scalar(zn[:, t, :], z[q][:, t, :], rs[:, t:t + 1], None, ALU.mult)
                m.then_inc(s_zn, 1)

            def split(k, q):
                v.wait_ge(s_znT, k + 1)
                link(v.tensor_copy(znTh[q][:, :], znT[q][:, :]))
                v.tensor_tensor(znTl[q][:, :], znT[q][:, :], znTh[q][:, :], ALU.subtract).then_inc(s_split, 1)

            def shifted(k):
                v.wait_ge(s_lg, k + 1)
                raw = px[:, 1, 0:TILES * 12].rearrange("p (t n) -> p t n", t=TILES)
                v.tensor_reduce(t1[:, 0, :], raw[:, :, 0:NG4], AX.X, ALU.max)
                link(v.tensor_reduce(t4[:, 0, :, :], raw[:, :, NG4:12].rearrange("p t (g l) -> p t g l", l=NL), AX.X, ALU.max))
                v.tensor_tensor(lg[:, :, 0:NG4], raw[:, :, 0:NG4], b4(t1[:, 0, :]), ALU.subtract)
                v.tensor_tensor(lg[:, :, NG4:12].rearrange("p t (g l) -> p t g l", l=NL),
                                raw[:, :, NG4:12].rearrange("p t (g l) -> p t g l", l=NL),
                                t4[:, 0, :, :].rearrange("p t (g o) -> p t g o", o=1).broadcast_to((P, TILES, NG4, NL)),
                                ALU.subtract).then_inc(s_sub, 1)

            def combine(k, q):
                v.wait_ge(s_ex, k + 1)
                exl = ex[:, :, NG4:12].rearrange("p t (g l) -> p t g l", l=NL)
                prl = pr[:, :, NG4:12].rearrange("p t (g l) -> p t g l", l=NL)
                v.tensor_reduce(t1[:, 1, :], ex[:, :, 0:NG4], AX.X, ALU.add)
                link(v.tensor_reduce(t4[:, 1, :, :], exl, AX.X, ALU.add))
                v.reciprocal(t1[:, 2, :], t1[:, 1, :])
                link(v.reciprocal(t4[:, 2, :, :], t4[:, 1, :, :]))
                v.tensor_tensor(pr[:, :, 0:NG4], ex[:, :, 0:NG4], b4(t1[:, 2, :]), ALU.mult)
                link(v.tensor_tensor(prl, exl, t4[:, 2, :, :].rearrange("p t (g o) -> p t g o", o=1).broadcast_to((P, TILES, NG4, NL)), ALU.mult))
                mine = pr[:, :, 0:NG4].rearrange("p t (g o) -> p t g o", o=1).broadcast_to((P, TILES, NG4, NG4))
                other = pr[:, :, 0:NG4].rearrange("p t (o g) -> p t o g", o=1).broadcast_to((P, TILES, NG4, NG4))
                v.tensor_tensor(cmp[:, :, :, :], other, mine, ALU.is_gt)
                v.tensor_tensor(s1[:, :, :, 1], prl[:, :, :, 1], prl[:, :, :, 0], ALU.is_gt)
                v.tensor_tensor(t4[:, 3, :, :], prl[:, :, :, 0], prl[:, :, :, 1], ALU.max)
                link(v.tensor_tensor(ceq[:, :, :, :], other, mine, ALU.is_equal))
                v.tensor_scalar(s1[:, :, :, 0], s1[:, :, :, 1], -1.0, 1.0, ALU.mult, ALU.add)
                v.tensor_scalar(t4[:, 4, :, :], t4[:, 3, :, :], TOP_EPS, None, ALU.add)
                link(v.tensor_tensor(ceq[:, :, :, :], ceq[:, :, :, :],
                                     tri.rearrange("p (o a) b -> p o a b", o=1).broadcast_to((P, TILES, NG4, NG4)), ALU.mult))
                v.reciprocal(t4[:, 5, :, :], t4[:, 4, :, :])
                link(v.tensor_tensor(cmp[:, :, :, :], cmp[:, :, :, :], ceq[:, :, :, :], ALU.add))
                v.tensor_tensor(t4[:, 6, :, :], t4[:, 3, :, :], t4[:, 5, :, :], ALU.mult)
                link(v.tensor_reduce(t4[:, 7, :, :], cmp[:, :, :, :], AX.X, ALU.add))
                link(v.tensor_scalar(t4[:, 7, :, :], t4[:, 7, :, :], 2.0, None, ALU.is_lt))
                link(v.tensor_tensor(t4[:, 7, :, :], t4[:, 7, :, :], pr[:, :, 0:NG4], ALU.mult))
                link(v.tensor_reduce(t1[:, 3, :], t4[:, 7, :, :], AX.X, ALU.add))
                link(v.tensor_scalar(t1[:, 3, :], t1[:, 3, :], TOP_EPS, None, ALU.add))
                link(v.reciprocal(t1[:, 0, :], t1[:, 3, :]))
                link(v.tensor_tensor(t4[:, 0, :, :], t4[:, 7, :, :], b4(t1[:, 0, :]), ALU.mult))
                link(v.tensor_tensor(t4[:, 0, :, :], t4[:, 0, :, :], t4[:, 6, :, :], ALU.mult))
                link(v.tensor_tensor(comb[q].rearrange("p t (g l) -> p t g l", l=NL), s1[:, :, :, :],
                                     t4[:, 0, :, :].rearrange("p t (g o) -> p t g o", o=1).broadcast_to((P, TILES, NG4, NL)), ALU.mult))

            def gather(k, q, ee):
                v.wait_ge(s_y, k * E8 + ee + 1 + E8)
                if ee:
                    v.wait_ge(s_acc, k * E8 + ee + 2)
                for t in range(TILES):
                    base = z[q] if ee == 0 else acc
                    dst = z[q] if ee == E8 - 1 else acc
                    m = v.scalar_tensor_tensor(dst[:, t, :], py[:, ee % 2, t, :], comb[q][:, t, ee:ee + 1], base[:, t, :],
                                               ALU.mult, ALU.add)
                m.then_inc(s_acc, 1)

            def tail_stats(q):
                link(v.tensor_tensor(r[:, :, :], z[q][:, :, :], xin[q][:, :, :], ALU.add))
                v.sem_inc(s_xfree[q], 1)
                for t in range(TILES):
                    m = v.bn_stats(st[:, t, :], r[:, t, :])
                link(m)
                v.sem_inc(s_turn, 1)
                for t in range(TILES):
                    m = v.bn_aggr(mv[:, t, :], st[:, t, :])
                link(m)
                v.tensor_scalar(vt[:, :], mv[:, :, 1], LN_EPS, None, ALU.add).then_inc(s_vt, 1)

            def tail_norm(g):
                v.wait_ge(s_rt, g + 1)
                v.wait_ge(s_st, g * 16 + 1)
                for t in range(TILES):
                    m = v.tensor_scalar(out[:, t, :], r[:, t, :], mv[:, t, 0:1], rt[:, t:t + 1], ALU.subtract, ALU.mult)
                m.then_inc(s_out, 1)

            def one_pass(k, p, tail, following, g):
                q = p % 2
                n[0], n[1] = k, 0
                nxt_loop = ((p + 1) % 4) // 2
                for ee in range(E8):
                    if following and ee == 3 + tail:
                        scaled(k + 1, 1 - q)
                    if following and ee == 5:
                        split(k + 1, 1 - q)
                    gather(k, q, ee)
                    if tail and ee == 0:
                        tail_stats(1 - q)
                    if tail and ee == 1:
                        tail_norm(g)
                    if following and ee == 1 + tail:
                        take(k + 1, 1 - q, nxt_loop, k * 4 + (16 if p == 0 else 20))
                    if following and ee == 2 + tail:
                        variance(k + 1)
                    if following and ee == 5 + tail:
                        shifted(k + 1)
                    if following and ee == 7:
                        combine(k + 1, 1 - q)
                v.wait_ge(s_acc, k * E8 + E8 + 2)
                close()

            def head(k, q, at):
                n[0], n[1] = -1, 0
                take(k, q, 0, at)
                variance(k)
                scaled(k, q)
                split(k, q)
                shifted(k)
                combine(k, q)

            head(0, 0, 16)
            close()
            schedule(v, one_pass)
            n[0], n[1] = 4 * PAIRS, 0
            tail_stats(1)
            tail_norm(GROUPS - 1)


SCRATCH = [P, TILES, D]


def decoder(nc, d):
    for name in ("s_x2", "s_f1", "s_x3", "s_gate", "s_x5"):
        d[name] = nc.dram_tensor(name, [GROUPS] + SCRATCH, F32, kind="Internal").ap()
    d["s_rows"] = nc.dram_tensor("s_rows", [B, S, TW], F32, kind="Internal").ap()
    d["s_y"] = nc.dram_tensor("s_y", [B, S, D], F32, kind="Internal").ap()
    with ExitStack() as ctx:
        ident = ctx.enter_context(nc.sbuf_tensor("ident", [P, P], F32))
        keep = {"ident": ident, "novelty": NOVELTY}
        ident_loaded = ctx.enter_context(nc.semaphore("ident_loaded"))
        with nc.Block() as block:
            @block.sync
            def _(sp):
                sp.dma_start(ident[:, :], d["ident"]).then_inc(ident_loaded, 16)
                sp.wait_ge(ident_loaded, 16)
        with ExitStack() as ffn:
            for name, shape, dt in (("pooledT", [P, B], F32), ("go", [1, 1], I32), ("mask", [P, FULL], F32),
                                    ("maskT", [P, FCH, P], F32)):
                keep[name] = ffn.enter_context(nc.sbuf_tensor(name, shape, dt))
            self_attention_and_ffn(nc, d, keep)
            route(nc, d, keep, True, False)
            route(nc, d, keep, True, True)
            route(nc, d, keep, False, True)
        delta_inputs(nc, d, keep)
        delta_scan(nc, d, keep)
        latent_attention(nc, d, keep)
        experts(nc, d, keep)


def layouts(x, ctx_1024, mask_BxS2_bk0, **w):
    p = np.arange(P)
    lag = p[None, :] - p[:, None]
    same = p[None, :] // S == p[:, None] // S
    qkv = w["L0_attn_W_qkv"].reshape(H, 3, DH, D)
    bqkv = w["L0_attn_b_qkv"].reshape(H, 3, DH)
    a = {
        "x": x, "ctx": ctx_1024, "mask": mask_BxS2_bk0,
        "ident": np.eye(P, dtype=np.float32),
        "headmask": ((p[:, None] % 64) // DH == np.arange(8)[None]).astype(np.float32),
        "decayT": np.where((lag >= 0) & same, 0.9 ** np.maximum(lag, 0), 0.0).astype(np.float32),
        "meanw": np.where(p[:, None] // S == np.arange(2)[None], 1.0 / S, 0.0).astype(np.float32),
        "a0_wqT": qkv[:, 0].reshape(D, D).T, "a0_wkT": qkv[:, 1].reshape(D, D).T, "a0_wvT": qkv[:, 2].reshape(D, D).T,
        "a0_bq": np.tile(bqkv[:, 0].reshape(2, D // 2).T, (2, 1)), "a0_bk": np.tile(bqkv[:, 1].reshape(2, D // 2).T, (2, 1)),
        "a0_bv": bqkv[:, 2].reshape(1, D),
        "a0_woT": w["L0_attn_W_out"].T, "a0_bo": w["L0_attn_b_out"][None],
        "f0_wmT": w["L0_ffn_Wm"].T, "f0_wpT": w["L0_ffn_Wp"].T, "f0_wc1T": w["L0_ffn_Wc1"].T, "f0_wc2T": w["L0_ffn_Wc2"].T,
        "l1_w": np.concatenate([w["L1_attn_W" + c] for c in "qkv"], 1),
        "l1_b": np.concatenate([w["L1_attn_b" + c] for c in "qkv"])[None],
        "l1_conv": np.concatenate([w[f"L1_attn_{c}_conv"] for c in "qkv"], 0).T.reshape(1, -1),
        "l1_valid": (p[:, None] % S + np.arange(CONV)[None] >= PAD).astype(np.float32),
        "l1_wg": np.concatenate([w["L1_attn_W" + c] for c in "gab"], 1),
        "l1_bg": np.concatenate([w["L1_attn_b" + c] for c in "gab"])[None],
        "l1_gs": w["L1_attn_gn_scale"][None], "l1_gb": w["L1_attn_gn_bias"][None],
        "l1_wo": w["L1_attn_Wo"], "l1_bo": w["L1_attn_bo"][None],
        "x_wqT": w["L1_xattn_Wq"].reshape(D, XH, XD).transpose(2, 1, 0),
        "x_wkT": w["L1_xattn_Wk"].reshape(D, XH, XD).transpose(2, 1, 0),
        "x_wvT": w["L1_xattn_Wv"].reshape(D, XH, XD).transpose(2, 1, 0),
        "x_wout": w["L1_xattn_Wout"].reshape(XH, XD, D).transpose(1, 0, 2),
        "x_par": np.stack([w["L1_xattn_" + c] for c in ("gamma_media", "beta_media", "gamma_lat", "beta_lat")], 1),
        "x_gate": w["L1_xattn_kv_gate"].reshape(1, 1),
        "m_w1": w["L1_ffn_w1"].reshape(E8, EC, P, D).transpose(3, 0, 1, 2).reshape(D, E8 * EC, P),
        "m_w2": w["L1_ffn_w2"].reshape(E8, D, EC, P).transpose(3, 0, 2, 1).reshape(P, E8 * EC, D),
        "m_wr": np.concatenate([w["L1_ffn_w_macro"], w["L1_ffn_w_micro"].reshape(E8, D)]).T,
        "m_nw": w["L1_ffn_norm_w"][:, None],
    }
    return {k: np.ascontiguousarray(v) for k, v in a.items()}


def kernel(**inputs):
    import concourse.bacc as bacc
    from concourse.bass_utils import run_bass_kernel_spmd

    arrays = layouts(**{k: np.asarray(v) for k, v in inputs.items()})
    nc = bacc.Bacc("TRN2", target_bir_lowering=False, num_devices=1)
    d = {k: nc.dram_tensor("in_" + k, a.shape, mybir.dt.from_np(a.dtype), kind="ExternalInput").ap()
         for k, a in arrays.items()}
    d["out"] = nc.dram_tensor("out", [B, S, D], F32, kind="ExternalOutput").ap()
    decoder(nc, d)
    r = run_bass_kernel_spmd(nc, [{"in_" + k: a for k, a in arrays.items()}], core_ids=[0])
    return r.results[0]["out"]
```
